# Optimizing a Trainium2 kernel written in Bass

```python
import numpy as np
import jax
import jax.numpy as jnp

def _softmax(x, axis=-1):
    return jax.nn.softmax(x, axis=axis)

def _gelu(x):
    return jax.nn.gelu(x, approximate=True)

def _silu(x):
    return jax.nn.silu(x)

def _sigmoid(x):
    return jax.nn.sigmoid(x)

def _layernorm(x, axis=-1, eps=1e-05):
    m = jnp.mean(x, axis=axis, keepdims=True)
    v = jnp.var(x, axis=axis, keepdims=True)
    return (x - m) / jnp.sqrt(v + eps)

def _scatter_add(tgt, idx, src, axis=0):
    return tgt.at[idx].add(src)

def _segment_sum(src, seg, n):
    return jax.ops.segment_sum(src, seg, n)
kernel_name = 'mk_gnn_ffn_d4_gnn_r16_95bd05'

def setup_inputs(seed: int=0):
    np.random.seed(seed)
    _w = jnp.asarray

    def _rec_inputs():
        import jax
        import jax.numpy as jnp
        _gk = jax.random.key(seed)
        x = -0.0003713 + 1 * jax.random.normal(jax.random.fold_in(_gk, 1), (3125, 256), jnp.float32)
        src = jax.random.randint(jax.random.fold_in(_gk, 2), (50000,), 0, 3125, jnp.int32)
        dst = jnp.minimum((3125 * jax.random.uniform(jax.random.fold_in(_gk, 3), (50000,)) ** 2.0).astype(jnp.int32), 49999)
        _o = jnp.argsort(dst, stable=True)
        src = src[_o]
        dst = dst[_o]
        edge_attr_256 = -0.000111208 + 0.99999 * jax.random.normal(jax.random.fold_in(_gk, 12), (50000, 256), jnp.float32)
        return (x, src, dst, edge_attr_256)
    x, src, dst, edge_attr_256 = _rec_inputs()

    def _L0_gnn_setup():
        import jax, jax.numpy as jnp
        import numpy as np
        N_NODES = 3125
        N_EDGES = 50000
        IN_DIM = 256
        OUT_DIM = 32
        NUM_HEADS = 8
        key = jax.random.key(seed)
        ks = jax.random.split(key, 9)
        h = jax.random.normal(ks[0], (N_NODES, IN_DIM), dtype=jnp.float32)
        src = jax.random.randint(ks[1], (N_EDGES,), 0, N_NODES, dtype=jnp.int32)
        dst = jax.random.randint(ks[2], (N_EDGES,), 0, N_NODES, dtype=jnp.int32)
        s = 1.0 / np.sqrt(IN_DIM)
        W_lin = jax.random.uniform(ks[3], (IN_DIM, IN_DIM), jnp.float32, -s, s)
        b_lin = jax.random.uniform(ks[4], (IN_DIM,), jnp.float32, -s, s)
        W_gat = jax.random.normal(ks[5], (IN_DIM, NUM_HEADS * OUT_DIM), dtype=jnp.float32) * s
        attn_l = jax.random.normal(ks[6], (NUM_HEADS, OUT_DIM), dtype=jnp.float32) * 0.1
        attn_r = jax.random.normal(ks[7], (NUM_HEADS, OUT_DIM), dtype=jnp.float32) * 0.1
        gat_bias = jnp.zeros((NUM_HEADS * OUT_DIM,), dtype=jnp.float32)
        return {'h': h, 'src': src, 'dst': dst, 'W_lin': W_lin, 'b_lin': b_lin, 'W_gat': W_gat, 'attn_l': attn_l, 'attn_r': attn_r, 'gat_bias': gat_bias}
    _L0_gnn_all = _L0_gnn_setup()
    _L0_gnn_in = {k: v for k, v in _L0_gnn_all.items() if k in ('W_lin', 'b_lin', 'W_gat', 'attn_l', 'attn_r', 'gat_bias')}
    del _L0_gnn_all

    def _L0_ffn_setup():
        import jax, jax.numpy as jnp
        import numpy as np
        B, K, D = (512, 16, 256)
        E = 32
        H = int(D * 0.25)
        key = jax.random.key(seed)
        ks = jax.random.split(key, 7)
        d_rs = D ** (-0.5)
        h_rs = H ** (-0.5)
        x = jax.random.normal(ks[0], (B, K, D), dtype=jnp.float32)
        router_w = jax.random.uniform(ks[1], (E, D), jnp.float32, -d_rs, d_rs)
        router_b = jax.random.uniform(ks[2], (E,), jnp.float32, -d_rs, d_rs)
        W1 = jax.random.uniform(ks[3], (E, D, H), jnp.float32, -h_rs, h_rs)
        b1 = jax.random.uniform(ks[4], (E, H), jnp.float32, -h_rs, h_rs)
        W2 = jax.random.uniform(ks[5], (E, H, D), jnp.float32, -d_rs, d_rs)
        b2 = jax.random.uniform(ks[6], (E, D), jnp.float32, -d_rs, d_rs)
        return {'x': x, 'router_w': router_w, 'router_b': router_b, 'W1': W1, 'b1': b1, 'W2': W2, 'b2': b2}
    _L0_ffn_all = _L0_ffn_setup()
    _L0_ffn_in = {k: v for k, v in _L0_ffn_all.items() if k in ('router_w', 'router_b', 'W1', 'b1', 'W2', 'b2')}
    del _L0_ffn_all

    def _L1_gnn_setup():
        import jax, jax.numpy as jnp
        import numpy as np
        N, E, D, H, NH = (625, 20000, 256, 256, 8)
        SLOPE = 11.0 / 48.0

        def _linear_params(key, fan_in, fan_out):
            kw, kb = jax.random.split(key)
            bound = 1.0 / np.sqrt(fan_in)
            W = jax.random.uniform(kw, (fan_out, fan_in), jnp.float32, -bound, bound)
            b = jax.random.uniform(kb, (fan_out,), jnp.float32, -bound, bound)
            return (W, b)
        key = jax.random.key(seed)
        ks = jax.random.split(key, 9)
        W1, b1 = _linear_params(ks[0], D, H)
        W2, b2 = _linear_params(ks[1], D, H)
        W3, b3 = _linear_params(ks[2], D, H)
        W4, b4 = _linear_params(ks[3], H, NH)
        W5, b5 = _linear_params(ks[4], D, NH)
        return dict(node_feats=jax.random.normal(ks[5], (N, D), jnp.float32), edge_feats=jax.random.normal(ks[6], (E, D), jnp.float32), W1=W1, b1=b1, W2=W2, b2=b2, W3=W3, b3=b3, W4=W4, b4=b4, W5=W5, b5=b5, src=jax.random.randint(ks[7], (E,), 0, N, jnp.int32), dst=jax.random.randint(ks[8], (E,), 0, N, jnp.int32))
    _L1_gnn_all = _L1_gnn_setup()
    _L1_gnn_in = {k: v for k, v in _L1_gnn_all.items() if k in ('W1', 'b1', 'W2', 'b2', 'W3', 'b3', 'W4', 'b4', 'W5', 'b5')}
    del _L1_gnn_all

    def _L1_ffn_setup():
        import math
        import jax, jax.numpy as jnp
        import numpy as np
        CAPACITY_FACTOR = 1.25
        TOP_K = 2
        LN_EPS = 1e-05

        def _layer_norm(x, gamma, beta):
            mu = jnp.mean(x, axis=-1, keepdims=True)
            var = jnp.var(x, axis=-1, keepdims=True)
            return (x - mu) * jax.lax.rsqrt(var + LN_EPS) * gamma + beta
        key = jax.random.key(seed)
        ks = jax.random.split(key, 4)
        B, S, D, F, E = (8, 256, 256, 512, 8)
        x = jax.random.normal(ks[0], (B, S, D), dtype=jnp.float32)
        Wr = jax.random.normal(ks[1], (D, E), dtype=jnp.float32) / np.sqrt(D)
        br = jnp.zeros((E,), jnp.float32)
        W1 = jax.random.normal(ks[2], (E, D, F), dtype=jnp.float32) / np.sqrt(D)
        b1 = jnp.zeros((E, F), jnp.float32)
        W2 = jax.random.normal(ks[3], (E, F, D), dtype=jnp.float32) / np.sqrt(F)
        b2 = jnp.zeros((E, D), jnp.float32)
        gamma = jnp.ones((D,), jnp.float32)
        beta = jnp.zeros((D,), jnp.float32)
        return {'x': x, 'Wr': Wr, 'br': br, 'W1': W1, 'b1': b1, 'W2': W2, 'b2': b2, 'gamma': gamma, 'beta': beta}
    _L1_ffn_all = _L1_ffn_setup()
    _L1_ffn_in = {k: v for k, v in _L1_ffn_all.items() if k in ('Wr', 'br', 'W1', 'b1', 'W2', 'b2', 'gamma', 'beta')}
    del _L1_ffn_all

    def _L2_gnn_setup():
        import jax, jax.numpy as jnp
        import numpy as np
        N, E, D, H, L = (3125, 50000, 256, 256, 4)
        EMB = 2 * H
        BN_EPS = 1e-05

        def _bn(h, gamma, beta):
            m = jnp.mean(h, axis=0)
            v = jnp.mean((h - m) ** 2, axis=0)
            return gamma * (h - m) / jnp.sqrt(v + BN_EPS) + beta
        key = jax.random.key(seed)
        ks = jax.random.split(key, 12)
        x = jax.random.normal(ks[0], (N, D), dtype=jnp.float32)
        edge_index = jax.random.randint(ks[1], (2, E), 0, N, dtype=jnp.int64)
        s1 = 1.0 / np.sqrt(D)
        s2 = 1.0 / np.sqrt(EMB)
        return {'x': x, 'edge_index': edge_index, 'W1': jax.random.uniform(ks[2], (L, D, EMB), jnp.float32, -s1, s1), 'b1': jax.random.uniform(ks[3], (L, EMB), jnp.float32, -s1, s1), 'bn1_gamma': jnp.ones((L, EMB), jnp.float32), 'bn1_beta': jnp.zeros((L, EMB), jnp.float32), 'W2': jax.random.uniform(ks[4], (L, EMB, H), jnp.float32, -s2, s2), 'b2': jax.random.uniform(ks[5], (L, H), jnp.float32, -s2, s2), 'bn2_gamma': jnp.ones((L, H), jnp.float32), 'bn2_beta': jnp.zeros((L, H), jnp.float32)}
    _L2_gnn_all = _L2_gnn_setup()
    _L2_gnn_in = {k: v for k, v in _L2_gnn_all.items() if k in ('W1', 'b1', 'bn1_gamma', 'bn1_beta', 'W2', 'b2', 'bn2_gamma', 'bn2_beta')}
    del _L2_gnn_all

    def _L2_ffn_setup():
        import jax, jax.numpy as jnp
        import numpy as np
        D_MODEL = 256
        EXPERT_DIM = 512
        NUM_EXPERTS = 8
        TOP_K = 2
        SEQ_LEN = 128
        BATCH = 2
        key = jax.random.key(seed)
        ks = jax.random.split(key, 8)
        s = 0.02
        x = jax.random.normal(ks[0], (SEQ_LEN, BATCH, D_MODEL), dtype=jnp.float32)
        Wg = jax.random.normal(ks[1], (D_MODEL, NUM_EXPERTS), dtype=jnp.float32) * s
        bg = jax.random.normal(ks[2], (NUM_EXPERTS,), dtype=jnp.float32) * s
        bias = jnp.zeros((NUM_EXPERTS,), dtype=jnp.float32)
        W1 = jax.random.normal(ks[3], (NUM_EXPERTS, D_MODEL, EXPERT_DIM), dtype=jnp.float32) * s
        b1 = jax.random.normal(ks[4], (NUM_EXPERTS, EXPERT_DIM), dtype=jnp.float32) * s
        W2 = jax.random.normal(ks[5], (NUM_EXPERTS, EXPERT_DIM, D_MODEL), dtype=jnp.float32) * s
        b2 = jax.random.normal(ks[6], (NUM_EXPERTS, D_MODEL), dtype=jnp.float32) * s
        return {'x': x, 'Wg': Wg, 'bg': bg, 'bias': bias, 'W1': W1, 'b1': b1, 'W2': W2, 'b2': b2}
    _L2_ffn_all = _L2_ffn_setup()
    _L2_ffn_in = {k: v for k, v in _L2_ffn_all.items() if k in ('Wg', 'bg', 'bias', 'W1', 'b1', 'W2', 'b2')}
    del _L2_ffn_all

    def _L3_gnn_setup():
        import jax, jax.numpy as jnp
        import numpy as np
        N, E = (3125, 50000)
        IN_DIM, HEADS, OUT_DIM = (256, 8, 32)
        NEG_SLOPE = 0.2
        LN_EPS = 1e-05
        key = jax.random.key(seed)
        ks = jax.random.split(key, 8)
        HC = HEADS * OUT_DIM
        x = jax.random.normal(ks[0], (N, IN_DIM), dtype=jnp.float32)
        edge_index = jax.random.randint(ks[1], (2, E), 0, N, dtype=jnp.int32)
        W = jax.random.normal(ks[2], (IN_DIM, HC), dtype=jnp.float32) / np.sqrt(IN_DIM)
        att_src = jax.random.normal(ks[3], (HEADS, OUT_DIM), dtype=jnp.float32) / np.sqrt(OUT_DIM)
        att_dst = jax.random.normal(ks[4], (HEADS, OUT_DIM), dtype=jnp.float32) / np.sqrt(OUT_DIM)
        bias = jnp.zeros((HC,), dtype=jnp.float32)
        ln_gamma = jnp.ones((HC,), dtype=jnp.float32)
        ln_beta = jnp.zeros((HC,), dtype=jnp.float32)
        return {'x': x, 'edge_index': edge_index, 'W': W, 'att_src': att_src, 'att_dst': att_dst, 'bias': bias, 'ln_gamma': ln_gamma, 'ln_beta': ln_beta}
    _L3_gnn_all = _L3_gnn_setup()
    _L3_gnn_in = {k: v for k, v in _L3_gnn_all.items() if k in ('W', 'att_src', 'att_dst', 'bias', 'ln_gamma', 'ln_beta')}
    del _L3_gnn_all

    def _L3_ffn_setup():
        import jax, jax.numpy as jnp
        import numpy as np
        B, S, D = (8, 256, 256)
        H = 4 * D
        CAPACITY = 0.5
        key = jax.random.key(seed)
        ks = jax.random.split(key, 6)
        x = jax.random.normal(ks[0], (B, S, D), dtype=jnp.float32)
        attention_mask = jnp.zeros((B, 1, 1, S), dtype=jnp.float32)
        wr = jax.random.normal(ks[1], (D, 1), dtype=jnp.float32) * 0.02
        br = jnp.zeros((1,), dtype=jnp.float32)
        w1 = jax.random.normal(ks[2], (D, H), dtype=jnp.float32) * 0.02
        b1 = jnp.zeros((H,), dtype=jnp.float32)
        w2 = jax.random.normal(ks[3], (H, D), dtype=jnp.float32) * 0.02
        b2 = jnp.zeros((D,), dtype=jnp.float32)
        return {'x': x, 'attention_mask': attention_mask, 'wr': wr, 'br': br, 'w1': w1, 'b1': b1, 'w2': w2, 'b2': b2}
    _L3_ffn_all = _L3_ffn_setup()
    _L3_ffn_in = {k: v for k, v in _L3_ffn_all.items() if k in ('attention_mask', 'wr', 'br', 'w1', 'b1', 'w2', 'b2')}
    del _L3_ffn_all
    return {'x': x, 'src': src, 'dst': dst, 'edge_attr_256': edge_attr_256, 'L0_gnn_W_lin': _L0_gnn_in['W_lin'], 'L0_gnn_b_lin': _L0_gnn_in['b_lin'], 'L0_gnn_W_gat': _L0_gnn_in['W_gat'], 'L0_gnn_attn_l': _L0_gnn_in['attn_l'], 'L0_gnn_attn_r': _L0_gnn_in['attn_r'], 'L0_gnn_gat_bias': _L0_gnn_in['gat_bias'], 'L0_ffn_router_w': _L0_ffn_in['router_w'], 'L0_ffn_router_b': _L0_ffn_in['router_b'], 'L0_ffn_W1': _L0_ffn_in['W1'], 'L0_ffn_b1': _L0_ffn_in['b1'], 'L0_ffn_W2': _L0_ffn_in['W2'], 'L0_ffn_b2': _L0_ffn_in['b2'], 'L1_gnn_W1': _L1_gnn_in['W1'], 'L1_gnn_b1': _L1_gnn_in['b1'], 'L1_gnn_W2': _L1_gnn_in['W2'], 'L1_gnn_b2': _L1_gnn_in['b2'], 'L1_gnn_W3': _L1_gnn_in['W3'], 'L1_gnn_b3': _L1_gnn_in['b3'], 'L1_gnn_W4': _L1_gnn_in['W4'], 'L1_gnn_b4': _L1_gnn_in['b4'], 'L1_gnn_W5': _L1_gnn_in['W5'], 'L1_gnn_b5': _L1_gnn_in['b5'], 'L1_ffn_Wr': _L1_ffn_in['Wr'], 'L1_ffn_br': _L1_ffn_in['br'], 'L1_ffn_W1': _L1_ffn_in['W1'], 'L1_ffn_b1': _L1_ffn_in['b1'], 'L1_ffn_W2': _L1_ffn_in['W2'], 'L1_ffn_b2': _L1_ffn_in['b2'], 'L1_ffn_gamma': _L1_ffn_in['gamma'], 'L1_ffn_beta': _L1_ffn_in['beta'], 'L2_gnn_W1': _L2_gnn_in['W1'], 'L2_gnn_b1': _L2_gnn_in['b1'], 'L2_gnn_bn1_gamma': _L2_gnn_in['bn1_gamma'], 'L2_gnn_bn1_beta': _L2_gnn_in['bn1_beta'], 'L2_gnn_W2': _L2_gnn_in['W2'], 'L2_gnn_b2': _L2_gnn_in['b2'], 'L2_gnn_bn2_gamma': _L2_gnn_in['bn2_gamma'], 'L2_gnn_bn2_beta': _L2_gnn_in['bn2_beta'], 'L2_ffn_Wg': _L2_ffn_in['Wg'], 'L2_ffn_bg': _L2_ffn_in['bg'], 'L2_ffn_bias': _L2_ffn_in['bias'], 'L2_ffn_W1': _L2_ffn_in['W1'], 'L2_ffn_b1': _L2_ffn_in['b1'], 'L2_ffn_W2': _L2_ffn_in['W2'], 'L2_ffn_b2': _L2_ffn_in['b2'], 'L3_gnn_W': _L3_gnn_in['W'], 'L3_gnn_att_src': _L3_gnn_in['att_src'], 'L3_gnn_att_dst': _L3_gnn_in['att_dst'], 'L3_gnn_bias': _L3_gnn_in['bias'], 'L3_gnn_ln_gamma': _L3_gnn_in['ln_gamma'], 'L3_gnn_ln_beta': _L3_gnn_in['ln_beta'], 'L3_ffn_attention_mask': _L3_ffn_in['attention_mask'], 'L3_ffn_wr': _L3_ffn_in['wr'], 'L3_ffn_br': _L3_ffn_in['br'], 'L3_ffn_w1': _L3_ffn_in['w1'], 'L3_ffn_b1': _L3_ffn_in['b1'], 'L3_ffn_w2': _L3_ffn_in['w2'], 'L3_ffn_b2': _L3_ffn_in['b2']}

def reference(x, src, dst, edge_attr_256, L0_gnn_W_lin, L0_gnn_b_lin, L0_gnn_W_gat, L0_gnn_attn_l, L0_gnn_attn_r, L0_gnn_gat_bias, L0_ffn_router_w, L0_ffn_router_b, L0_ffn_W1, L0_ffn_b1, L0_ffn_W2, L0_ffn_b2, L1_gnn_W1, L1_gnn_b1, L1_gnn_W2, L1_gnn_b2, L1_gnn_W3, L1_gnn_b3, L1_gnn_W4, L1_gnn_b4, L1_gnn_W5, L1_gnn_b5, L1_ffn_Wr, L1_ffn_br, L1_ffn_W1, L1_ffn_b1, L1_ffn_W2, L1_ffn_b2, L1_ffn_gamma, L1_ffn_beta, L2_gnn_W1, L2_gnn_b1, L2_gnn_bn1_gamma, L2_gnn_bn1_beta, L2_gnn_W2, L2_gnn_b2, L2_gnn_bn2_gamma, L2_gnn_bn2_beta, L2_ffn_Wg, L2_ffn_bg, L2_ffn_bias, L2_ffn_W1, L2_ffn_b1, L2_ffn_W2, L2_ffn_b2, L3_gnn_W, L3_gnn_att_src, L3_gnn_att_dst, L3_gnn_bias, L3_gnn_ln_gamma, L3_gnn_ln_beta, L3_ffn_attention_mask, L3_ffn_wr, L3_ffn_br, L3_ffn_w1, L3_ffn_b1, L3_ffn_w2, L3_ffn_b2):
    import jax
    import jax.numpy as jnp

    def _L0_gnn_ref(h, src, dst, W_lin, b_lin, W_gat, attn_l, attn_r, gat_bias):
        import jax, jax.numpy as jnp
        import numpy as np
        N_NODES = 3125
        N_EDGES = 50000
        IN_DIM = 256
        OUT_DIM = 32
        NUM_HEADS = 8
        N = h.shape[0]
        h = h @ W_lin + b_lin
        h_in = h
        feat = (h @ W_gat).reshape(N, NUM_HEADS, OUT_DIM)
        el = jnp.sum(feat * attn_l, axis=-1)
        er = jnp.sum(feat * attn_r, axis=-1)
        e = jax.nn.leaky_relu(el[src] + er[dst], 0.2)
        m = jax.ops.segment_max(e, dst, num_segments=N)
        m = jnp.where(jnp.isfinite(m), m, 0.0)
        e = jnp.exp(e - m[dst])
        s = jax.ops.segment_sum(e, dst, num_segments=N)
        a = e / s[dst]
        msg = feat[src] * a[:, :, None]
        out = jax.ops.segment_sum(msg, dst, num_segments=N)
        out = out.reshape(N, NUM_HEADS * OUT_DIM) + gat_bias
        out = jax.nn.leaky_relu(out, 0.01)
        return h_in + out

    def _L0_ffn_ref(x, router_w, router_b, W1, b1, W2, b2):
        import jax, jax.numpy as jnp
        import numpy as np
        B, K, D = (512, 16, 256)
        E = 32
        H = int(D * 0.25)
        xf = x.reshape(-1, D)
        logits = xf @ router_w.T + router_b
        idx = jnp.argmax(logits, axis=-1)
        w1t = jnp.take(W1, idx, axis=0)
        h = jnp.einsum('nd,ndh->nh', xf, w1t) + jnp.take(b1, idx, axis=0)
        h = jax.nn.relu(h)
        w2t = jnp.take(W2, idx, axis=0)
        out = jnp.einsum('nh,nhd->nd', h, w2t) + jnp.take(b2, idx, axis=0)
        out = jax.nn.relu(out)
        return out.reshape(x.shape)

    def _L1_gnn_ref(node_feats, edge_feats, W1, b1, W2, b2, W3, b3, W4, b4, W5, b5, src, dst):
        import jax, jax.numpy as jnp
        import numpy as np
        N, E, D, H, NH = (625, 20000, 256, 256, 8)
        SLOPE = 11.0 / 48.0

        def _linear_params(key, fan_in, fan_out):
            kw, kb = jax.random.split(key)
            bound = 1.0 / np.sqrt(fan_in)
            W = jax.random.uniform(kw, (fan_out, fan_in), jnp.float32, -bound, bound)
            b = jax.random.uniform(kb, (fan_out,), jnp.float32, -bound, bound)
            return (W, b)
        n = node_feats.shape[0]
        msg = (node_feats[src] + edge_feats) @ W1.T + b1
        s = msg @ W4.T + b4 + (node_feats @ W5.T + b5)[dst]
        smax = jax.ops.segment_max(s, dst, num_segments=n)
        smax = jnp.where(jnp.isfinite(smax), smax, 0.0)
        ex = jnp.exp(s - smax[dst])
        denom = jax.ops.segment_sum(ex, dst, num_segments=n)
        w = ex / denom[dst]
        wbar = jnp.mean(w, axis=-1)
        agg = jax.ops.segment_sum(wbar[:, None] * msg, dst, num_segments=n)
        deg = jax.ops.segment_sum(jnp.ones((src.shape[0],), jnp.int32), dst, num_segments=n)
        iso = (deg == 0)[:, None]
        self_msg = jnp.where(iso, node_feats @ W3.T + b3, node_feats @ W2.T + b2)
        z = self_msg + agg
        return jnp.where(z >= 0, z, SLOPE * z)

    def _L1_ffn_ref(x, Wr, br, W1, b1, W2, b2, gamma, beta):
        import math
        import jax, jax.numpy as jnp
        import numpy as np
        CAPACITY_FACTOR = 1.25
        TOP_K = 2
        LN_EPS = 1e-05

        def _layer_norm(x, gamma, beta):
            mu = jnp.mean(x, axis=-1, keepdims=True)
            var = jnp.var(x, axis=-1, keepdims=True)
            return (x - mu) * jax.lax.rsqrt(var + LN_EPS) * gamma + beta
        B, S, D = x.shape
        E = Wr.shape[1]
        N = B * S
        K = TOP_K
        logits = jnp.mean(x, axis=1) @ Wr + br
        routing_weights = jax.nn.softmax(logits, axis=-1)
        capacity = float(math.ceil(N * CAPACITY_FACTOR / E))
        expected_loads = routing_weights.sum(axis=0) * (N / B)
        scale = jnp.where(expected_loads > capacity, capacity / expected_loads, 1.0)
        routing_weights = jax.nn.softmax(routing_weights * scale, axis=-1)
        rw_tok = jnp.broadcast_to(routing_weights[:, None, :], (B, S, E)).reshape(N, E)
        top_w, top_i = jax.lax.top_k(rw_tok, K)
        top_w = jax.nn.softmax(top_w, axis=-1)
        xf = x.reshape(N, D)
        h = jax.nn.gelu(jnp.einsum('nd,edf->enf', xf, W1) + b1[:, None, :], approximate=False)
        y = jnp.einsum('enf,efd->end', h, W2) + b2[:, None, :]
        w_dense = jnp.zeros((N, E), x.dtype).at[jnp.arange(N)[:, None], top_i].add(top_w)
        out = jnp.einsum('ne,end->nd', w_dense, y).reshape(B, S, D)
        out = _layer_norm(out + x, gamma, beta)
        return out

    def _L2_gnn_ref(x, edge_index, W1, b1, bn1_gamma, bn1_beta, W2, b2, bn2_gamma, bn2_beta):
        import jax, jax.numpy as jnp
        import numpy as np
        N, E, D, H, L = (3125, 50000, 256, 256, 4)
        EMB = 2 * H
        BN_EPS = 1e-05

        def _bn(h, gamma, beta):
            m = jnp.mean(h, axis=0)
            v = jnp.mean((h - m) ** 2, axis=0)
            return gamma * (h - m) / jnp.sqrt(v + BN_EPS) + beta
        src, dst = (edge_index[0], edge_index[1])
        n = x.shape[0]
        h = x
        for l in range(L):
            agg = h + jax.ops.segment_sum(h[src], dst, num_segments=n)
            z = jax.nn.relu(_bn(agg @ W1[l] + b1[l], bn1_gamma[l], bn1_beta[l]))
            z = z @ W2[l] + b2[l]
            z = _bn(z, bn2_gamma[l], bn2_beta[l])
            h = z if l == L - 1 else jax.nn.relu(z)
        return h

    def _L2_ffn_ref(x, Wg, bg, bias, W1, b1, W2, b2):
        import jax, jax.numpy as jnp
        import numpy as np
        D_MODEL = 256
        EXPERT_DIM = 512
        NUM_EXPERTS = 8
        TOP_K = 2
        SEQ_LEN = 128
        BATCH = 2
        x_flat = x.reshape(-1, D_MODEL)
        gate_logits = x_flat @ Wg + bg + bias
        topk_vals, topk_idx = jax.lax.top_k(gate_logits, TOP_K)
        topk_w = jax.nn.softmax(topk_vals, axis=-1)
        combine = (jax.nn.one_hot(topk_idx, NUM_EXPERTS, dtype=x.dtype) * topk_w[..., None]).sum(axis=1)
        h = jax.nn.relu(jnp.einsum('td,edh->teh', x_flat, W1) + b1)
        y = jnp.einsum('teh,ehd->ted', h, W2) + b2
        out = jnp.einsum('ted,te->td', y, combine)
        return out.reshape(x.shape)

    def _L3_gnn_ref(x, edge_index, W, att_src, att_dst, bias, ln_gamma, ln_beta):
        import jax, jax.numpy as jnp
        import numpy as np
        N, E = (3125, 50000)
        IN_DIM, HEADS, OUT_DIM = (256, 8, 32)
        NEG_SLOPE = 0.2
        LN_EPS = 1e-05
        n = x.shape[0]
        loop = jnp.arange(n, dtype=edge_index.dtype)
        src = jnp.concatenate([edge_index[0], loop])
        dst = jnp.concatenate([edge_index[1], loop])
        h = (x @ W).reshape(n, HEADS, OUT_DIM)
        a_src = jnp.einsum('nhc,hc->nh', h, att_src)
        a_dst = jnp.einsum('nhc,hc->nh', h, att_dst)
        e = jax.nn.leaky_relu(a_src[src] + a_dst[dst], NEG_SLOPE)
        m = jax.ops.segment_max(e, dst, num_segments=n)
        e = jnp.exp(e - m[dst])
        denom = jax.ops.segment_sum(e, dst, num_segments=n)
        alpha = e / (denom[dst] + 1e-16)
        out = jax.ops.segment_sum(h[src] * alpha[:, :, None], dst, num_segments=n)
        out = out.reshape(n, HEADS * OUT_DIM) + bias
        mu = jnp.mean(out, axis=-1, keepdims=True)
        var = jnp.mean(jnp.square(out - mu), axis=-1, keepdims=True)
        return ln_gamma * (out - mu) * jax.lax.rsqrt(var + LN_EPS) + ln_beta

    def _L3_ffn_ref(x, attention_mask, wr, br, w1, b1, w2, b2):
        import jax, jax.numpy as jnp
        import numpy as np
        B, S, D = (8, 256, 256)
        H = 4 * D
        CAPACITY = 0.5
        b, s, d = x.shape
        weights = (jnp.einsum('bsd,do->bso', x, wr) + br)[..., 0]
        k = max(1, int(CAPACITY * s))
        kk = k - 1 if k > 1 else 1
        _, idx = jax.lax.top_k(weights, k)
        sel_idx = idx[:, :kk]
        sel = jnp.take_along_axis(x, sel_idx[:, :, None], axis=1)
        h = jax.nn.gelu(jnp.einsum('bkd,dh->bkh', sel, w1) + b1)
        y = jnp.einsum('bkh,hd->bkd', h, w2) + b2
        w_sel = jnp.take_along_axis(weights, sel_idx, axis=1)
        y = y * w_sel[..., None]
        batch_idx = jnp.arange(b)[:, None]
        processed = jnp.zeros_like(x).at[batch_idx, sel_idx].set(y)
        return processed + x
    edge_index = jnp.stack([src, dst])
    x = x + _L0_gnn_ref(_layernorm(x, axis=-1), src, dst, L0_gnn_W_lin, L0_gnn_b_lin, L0_gnn_W_gat, L0_gnn_attn_l, L0_gnn_attn_r, L0_gnn_gat_bias)
    x = x + _L0_ffn_ref(_layernorm(x, axis=-1)[None], L0_ffn_router_w, L0_ffn_router_b, L0_ffn_W1, L0_ffn_b1, L0_ffn_W2, L0_ffn_b2)[0]
    x = x + _L1_gnn_ref(_layernorm(x, axis=-1), edge_attr_256, L1_gnn_W1, L1_gnn_b1, L1_gnn_W2, L1_gnn_b2, L1_gnn_W3, L1_gnn_b3, L1_gnn_W4, L1_gnn_b4, L1_gnn_W5, L1_gnn_b5, src, dst)
    x = x + _L1_ffn_ref(_layernorm(x, axis=-1)[None], L1_ffn_Wr, L1_ffn_br, L1_ffn_W1, L1_ffn_b1, L1_ffn_W2, L1_ffn_b2, L1_ffn_gamma, L1_ffn_beta)[0]
    x = x + _L2_gnn_ref(_layernorm(x, axis=-1), edge_index, L2_gnn_W1, L2_gnn_b1, L2_gnn_bn1_gamma, L2_gnn_bn1_beta, L2_gnn_W2, L2_gnn_b2, L2_gnn_bn2_gamma, L2_gnn_bn2_beta)
    x = x + _L2_ffn_ref(_layernorm(x, axis=-1)[None], L2_ffn_Wg, L2_ffn_bg, L2_ffn_bias, L2_ffn_W1, L2_ffn_b1, L2_ffn_W2, L2_ffn_b2)[0]
    x = x + _L3_gnn_ref(_layernorm(x, axis=-1), edge_index, L3_gnn_W, L3_gnn_att_src, L3_gnn_att_dst, L3_gnn_bias, L3_gnn_ln_gamma, L3_gnn_ln_beta)
    x = x + _L3_ffn_ref(_layernorm(x, axis=-1)[None], L3_ffn_attention_mask, L3_ffn_wr, L3_ffn_br, L3_ffn_w1, L3_ffn_b1, L3_ffn_w2, L3_ffn_b2)[0]
    return x

_drawn_inputs = setup_inputs


def setup_inputs(seed=0):
    import zlib

    import numpy as np

    out = dict(_drawn_inputs(seed))
    spreads = {'L0_gnn_gat_bias': (0.0, 0.1),
     'L1_ffn_br': (0.0, 0.8),
     'L1_ffn_b1': (0.0, 0.1),
     'L1_ffn_b2': (0.0, 0.1),
     'L1_ffn_gamma': (1.0, 0.2),
     'L1_ffn_beta': (0.0, 0.1),
     'L2_gnn_bn1_gamma': (1.0, 0.2),
     'L2_gnn_bn1_beta': (0.0, 0.1),
     'L2_gnn_bn2_gamma': (1.0, 0.2),
     'L2_gnn_bn2_beta': (0.0, 0.1),
     'L2_ffn_bias': (0.0, 0.573),
     'L3_gnn_bias': (0.0, 0.1),
     'L3_gnn_ln_gamma': (1.0, 0.2),
     'L3_gnn_ln_beta': (0.0, 0.1),
     'L3_ffn_b1': (0.0, 0.8),
     'L3_ffn_b2': (0.0, 0.8)}
    factors = {'L0_gnn_attn_r': 2.972,
     'L0_ffn_b1': 5.592,
     'L1_gnn_b4': 8.0,
     'L1_gnn_W5': 8.0,
     'L1_gnn_b5': 8.0,
     'L2_gnn_b1': 8.0,
     'L2_gnn_b2': 8.0,
     'L2_ffn_bg': 8.0,
     'L2_ffn_b1': 8.0,
     'L2_ffn_b2': 8.0,
     'L3_ffn_wr': 7.183,
     'L3_ffn_w1': 8.0,
     'L3_ffn_w2': 8.0}
    for name, (base, spread) in spreads.items():
        noise = np.random.default_rng([zlib.crc32(name.encode()), seed]).standard_normal(out[name].shape)
        drawn = base * np.exp(spread * noise) if base else spread * noise
        out[name] = jnp.asarray(drawn.astype(out[name].dtype))
    for name, factor in factors.items():
        out[name] = (out[name] * factor).astype(out[name].dtype)
    return out
```

```python
from contextlib import ExitStack, contextmanager

import numpy as np

import concourse.bass as bass
from concourse import mybir

F32 = mybir.dt.float32
I32 = mybir.dt.int32
U32 = mybir.dt.uint32
ALU = mybir.AluOpType
ACT = mybir.ActivationFunctionType
AX = mybir.AxisListType

N, E, D = 3125, 50000, 256
P = 125
T = N // P
C = E // P
KD = D // 128
H = 8
HD = D // H
S = C + T - 1
SLOTS = 8
HALF = SLOTS // 2
RUNS = 16
RUN = E // RUNS
RC = RUN // P
GRP = 5
BIG = 1e30
EPS = 1e-5
assert S % SLOTS == 0 and RUNS * H == 128 and RC == T and T % GRP == 0


class Core:
    pass


class Tools:

    def __init__(self, steps, loads=()):
        self.steps, self.loads = steps, loads


class Steps:

    def __init__(self, eng, sem):
        self.eng, self.sem, self.n, self.i, self.per = eng, sem, 0, None, 0

    def mark(self, ins):
        ins.then_inc(self.sem, 1)
        self.n += 1
        return self.n

    def value(self, n=None):
        n = self.n if n is None else n
        return n if self.i is None else self.i * self.per + n

    def wait(self, n=None):
        self.eng.wait_ge(self.sem, self.value(n))

    def then(self, ins):
        self.mark(ins)
        self.wait()

    @contextmanager
    def loop(self, count, per):
        start = self.n
        with self.eng.Fori(0, count) as i:
            self.i, self.per = i, per
            yield i
            assert self.n - start == per, (self.n - start, per)
        self.i, self.n = None, start + count * per


def at(i, n):
    return bass.ds(i * n, n)


class Stage:

    def __init__(self, nc, g, name):
        self.nc, self.g, self.name, self.ctx, self.taken = nc, g, name, ExitStack(), []

    def __enter__(self):
        return self

    def __exit__(self, *a):
        if a[0] is None and self.taken:
            self.nc.all_engine_barrier(sems_to_clear=range(self.taken[0], self.taken[-1] + 1))
        self.ctx.close()

    def sb(self, name, shape, dt=F32):
        return self.ctx.enter_context(self.nc.sbuf_tensor(f"{self.name}_{name}", shape, dt))

    def ps(self, name, shape, dt=F32):
        return self.ctx.enter_context(self.nc.psum_tensor(f"{self.name}_{name}", shape, dt))

    def sem(self, name):
        number = self.g.first_sem + len(self.taken)
        self.taken.append(number)
        return self.ctx.enter_context(self.nc.semaphore(f"{self.name}_{name}", number))

    def sems(self, name, n):
        return [self.sem(f"{name}{i}") for i in range(n)]

    def gathers(self, n, count):
        got = [(self.g.gather_sems[i], self.g.gathered[i]) for i in range(n)]
        for i in range(n):
            self.g.gathered[i] += 16 * count
        return [s for s, _ in got], [v for _, v in got]

    def dram(self, name, shape, dt=F32):
        return self.nc.dram_tensor(f"{self.name}_{name}", shape, dt, kind="Internal").ap()

    def block(self):
        return self.nc.Block()


def row(ap):
    return ap.rearrange("(a n) -> a n", a=1)


def spread(ap, p=P):
    n = ap.shape[0]
    return bass.AP(ap.tensor, ap.offset, [[0, p], [1, n]])



def prepare(nc, g, A):
    with Stage(nc, g, "prep") as st:
        PS = S // 4
        thr = st.sb("thr", [T, 1])
        first_i = st.sb("first_i", [1, C], I32)
        first = st.sb("first", [1, C])
        ones = st.sb("ones", [T, 128])
        past = st.sb("past", [T, C])
        kio = st.sb("kio", [128, C])
        begin = st.sb("begin", [128, C])
        sio = st.sb("sio", [PS, 4])
        junk = st.sb("junk", [128, C])
        cnt = st.sb("cnt", [PS, 4])
        kf = st.sb("kf", [PS, 4])
        tf = st.sb("tf", [PS, 4])
        ki = st.sb("ki", [PS, 4], I32)
        ti = st.sb("ti", [PS, 4], I32)
        base = st.sb("base", [PS, 4])
        src_rows = st.sb("src_rows", [PS, 4, P], I32)
        dst_rows = st.sb("dst_rows", [PS, 4, P], I32)
        src_f = st.sb("src_f", [PS, 4, P])
        dst_f = st.sb("dst_f", [PS, 4, P])
        win_i = st.sb("win_i", [128, RUN + 2], I32)
        win = st.sb("win", [128, RUN + 2])
        b1 = st.ps("b1", [T, C])
        b2 = st.ps("b2", [128, C])
        tp = [st.ps(f"tp{j}", [128, 128]) for j in range(2)]
        k_dram = st.dram("k", (PS, 4), I32)
        t_dram = st.dram("t", (PS, 4), I32)

        x_in, small_in, win_in, rows_in = st.sem("x_in"), st.sem("small_in"), st.sem("win_in"), st.gathers(8, 1)[0]
        tabs_out, tabs_in, made = st.sem("tabs_out"), st.sem("tabs_in"), st.sem("made")
        spread_first, summed, dv, steps_known = st.sem("spread_first"), st.sem("summed"), st.sem("dv"), st.sem("steps_known")
        first_ready, past_ready, rows_ready, turned, wset = st.sem("first_ready"), st.sem("past_ready"), st.sem("rows_ready"), st.sem("turned"), st.sem("wset")

        with st.block() as block:
            @block.sync
            def _(sp):
                sp.dma_start(first_i[:], row(A["dst_by_place"][0, :])).then_inc(small_in, 16)
                sp.dma_start(g.ident[:], A["ident"]).then_inc(small_in, 16)
                sp.dma_start(g.src_e[:], A["src_by_place"].bitcast(U32)).then_inc(small_in, 16)
                sp.dma_start(g.dst_e[:], A["dst_by_place"].bitcast(U32)).then_inc(small_in, 16)
                for t in range(T):
                    sp.dma_start(g.x[:, t, :], A["x"][t * P:(t + 1) * P, :]).then_inc(x_in, 16)
                sp.wait_ge(wset, 1)
                flat = A["dst"]
                for r in range(RUNS):
                    lo, n, off = r * RUN - 1, RUN + 2, 0
                    if r == 0:
                        lo, n, off = 0, n - 1, 1
                    if r == RUNS - 1:
                        n -= 1
                    sp.dma_start(win_i[r * H:(r + 1) * H, off:off + n],
                                 bass.AP(flat.tensor, flat.offset + lo, [[0, H], [1, n]])).then_inc(win_in, 16)
                sp.wait_ge(steps_known, 1)
                sp.dma_start(k_dram, ki[:]).then_inc(tabs_out, 16)
                sp.dma_start(t_dram, ti[:]).then_inc(tabs_out, 16)
                sp.wait_ge(tabs_out, 32)
                sp.dma_start(g.chunk_of[:], k_dram.rearrange("(o p) j -> o (p j)", o=1)).then_inc(tabs_in, 16)
                sp.dma_start(g.tile_of[:], t_dram.rearrange("(o p) j -> o (p j)", o=1)).then_inc(tabs_in, 16)
                sp.wait_ge(tabs_in, 32)
                sp.wait_ge(x_in, 16 * T)

            @block.gpsimd
            def _(pool):
                pool.iota(thr[:], pattern=[[0, 1]], base=P, channel_multiplier=P,
                          allow_small_or_imprecise_dtypes=True).then_inc(made, 1)
                pool.iota(kio[:], pattern=[[1, C]], base=0, channel_multiplier=0,
                          allow_small_or_imprecise_dtypes=True).then_inc(made, 1)
                pool.iota(sio[:], pattern=[[1, 4]], base=0, channel_multiplier=4,
                          allow_small_or_imprecise_dtypes=True).then_inc(made, 1)
                pool.iota(g.iota[:], pattern=[[1, 128]], base=0, channel_multiplier=0,
                          allow_small_or_imprecise_dtypes=True).then_inc(made, 1)
                pool.memset(ones[:], 1.0).then_inc(made, 1)
                pool.memset(g.ones[:], 1.0).then_inc(made, 1)
                pool.memset(win_i[:], -1).then_inc(wset, 1)
                pool.wait_ge(steps_known, 1)
                src_c, dst_c = (a.rearrange("(c p) -> c p", p=P) for a in (A["src"], A["dst"]))
                for j in range(4):
                    for n, (rows, table) in enumerate(((src_rows, src_c), (dst_rows, dst_c))):
                        pool.indirect_dma_start(
                            out=rows[:, j, :], out_offset=None, in_=table,
                            in_offset=bass.IndirectOffsetOnAxis(ap=ki[:, j:j + 1].bitcast(U32), axis=0),
                        ).then_inc(rows_in[2 * j + n], 16)

            @block.tensor
            def _(pe):
                pe.wait_ge(made, 6)
                pe.wait_ge(first_ready, 1)
                pe.matmul(b1[:], ones[0:1, 0:T], first[:], start=True, stop=True).then_inc(spread_first, 1)
                pe.wait_ge(past_ready, 1)
                pe.matmul(b2[:], ones[:], past[:], start=True, stop=True).then_inc(summed, 1)
                for n in range(8):
                    f = (src_f, dst_f)[n % 2]
                    pe.wait_ge(rows_ready, n + 1)
                    pe.wait_ge(small_in, 64)
                    if n >= 2:
                        pe.wait_ge(turned, n - 1)
                    pe.transpose(tp[n % 2][0:P, 0:PS], f[:, n // 2, :], g.ident[0:PS, 0:PS]).then_inc(summed, 1)

            @block.vector
            def _(v):
                q = Steps(v, dv)
                v.wait_ge(small_in, 64)
                v.tensor_copy(first[:], first_i[:]).then_inc(first_ready, 1)
                v.wait_ge(made, 6)
                v.wait_ge(spread_first, 1)
                v.tensor_scalar(past[:], b1[:], thr[:, 0:1], None, ALU.is_ge).then_inc(past_ready, 1)
                v.wait_ge(summed, 1)
                q.then(v.tensor_tensor(begin[:], kio[:], b2[:], ALU.add))
                for j in range(4):
                    q.then(v.tensor_scalar(junk[0:PS, :], begin[0:PS, :], sio[:, j:j + 1], None, ALU.is_le, ALU.add,
                                           accum_out=cnt[:, j:j + 1]))
                q.then(v.tensor_scalar(kf[:], cnt[:], -1.0, 0.0, ALU.add, ALU.max))
                q.then(v.tensor_tensor(tf[:], sio[:], kf[:], ALU.subtract))
                q.then(v.tensor_scalar(tf[:], tf[:], float(T - 1), None, ALU.min))
                q.then(v.tensor_scalar(base[:], tf[:], float(P), None, ALU.mult))
                q.then(v.tensor_copy(ki[:], kf[:]))
                v.tensor_copy(ti[:], tf[:]).then_inc(steps_known, 1)
                for j in range(4):
                    v.wait_ge(rows_in[2 * j], 16)
                    v.tensor_copy(src_f[:, j, :], src_rows[:, j, :]).then_inc(rows_ready, 1)
                    v.wait_ge(rows_in[2 * j + 1], 16)
                    v.tensor_scalar(dst_f[:, j, :], dst_rows[:, j, :], base[:, j:j + 1], None,
                                    ALU.subtract).then_inc(rows_ready, 1)
                for n in range(8):
                    v.wait_ge(summed, n + 2)
                    out = (g.src_s, g.place_s)[n % 2][:].rearrange("p (s j) -> p s j", j=4)[:, :, n // 2]
                    v.tensor_copy(out, tp[n % 2][0:P, 0:PS]).then_inc(turned, 1)
                v.wait_ge(win_in, 16 * RUNS)
                q.then(v.tensor_copy(win[:], win_i[:]))
                q.then(v.tensor_tensor(g.border[:], win[:, 1:RUN + 2], win[:, 0:RUN + 1], ALU.not_equal))
                q.then(v.tensor_reduce(g.has_border[:], g.border[:, 0:RUN], AX.X, ALU.max))
                q.then(v.tensor_reduce(g.has_border_back[:], g.border[:, 1:RUN + 1], AX.X, ALU.max))



def norm_stats(nc, g, name, values=None):
    with Stage(nc, g, name) as st:
        raw = st.sb("raw", [P, T * 6])
        gap = st.sb("gap", [P, T])
        var = st.sb("var", [P, T])
        sd = st.sb("sd", [P, T])
        eps = st.sb("eps", [P, 1])
        dv, var_ready, sd_ready = st.sem("dv"), st.sem("var_ready"), st.sem("sd_ready")
        x = g.x if values is None else values
        r = raw[:].rearrange("p (t s) -> p s t", s=6)
        with st.block() as block:
            @block.vector
            def _(v):
                q = Steps(v, dv)
                q.mark(v.memset(eps[:], EPS))
                with q.loop(T, 1) as t:
                    q.mark(v.bn_stats(raw[:, at(t, 6)], x[:, bass.ds(t, 1), 0:D].rearrange("p t d -> p (t d)")))
                q.wait()
                q.then(v.tensor_tensor(g.mean[:], r[:, 1, :], r[:, 4, :], ALU.add))
                q.then(v.tensor_tensor(gap[:], r[:, 1, :], r[:, 4, :], ALU.subtract))
                q.then(v.tensor_scalar(g.mean[:], g.mean[:], 0.5, None, ALU.mult))
                q.then(v.tensor_tensor(var[:], r[:, 2, :], r[:, 5, :], ALU.add))
                q.then(v.tensor_scalar(var[:], var[:], 1.0 / D, None, ALU.mult))
                q.then(v.scalar_tensor_tensor(gap[:], gap[:], 0.25, gap[:], ALU.mult, ALU.mult))
                v.tensor_tensor(var[:], var[:], gap[:], ALU.add).then_inc(var_ready, 1)
                v.wait_ge(sd_ready, 1)
                q.then(v.reciprocal(g.rstd[:], sd[:]))

            @block.scalar
            def _(act):
                act.wait_ge(var_ready, 1)
                act.activation(sd[:], var[:], ACT.Sqrt, bias=eps[:]).then_inc(sd_ready, 1)



def sum_rows(nc, g, name, table, acc):
    with Stage(nc, g, name) as st:
        idx = st.sb("idx", [P, SLOTS], U32)
        rows = st.sb("rows", [P, SLOTS, D])
        hot = st.sb("hot", [P, HALF, P])
        part = [st.ps(f"part{j}", [P, 512]) for j in range(HALF)]
        idx_ready, idx_taken = st.sem("idx_ready"), st.sem("idx_taken")
        rows_in, before = st.gathers(SLOTS, S // SLOTS)
        hot_ready, summed, added = st.sem("hot_ready"), st.sem("summed"), st.sem("added")
        with st.block() as block:
            @block.scalar
            def _(act):
                with act.Fori(0, S // SLOTS) as i:
                    for j in range(SLOTS):
                        act.wait_ge(rows_in[j], i * 16 + before[j])
                        act.activation(idx[:, j:j + 1], g.src_s[:, bass.ds(i * SLOTS + j, 1)], ACT.Copy).then_inc(idx_ready, 1)

            @block.gpsimd
            def _(pool):
                pool.sem_inc(summed, SLOTS)
                with pool.Fori(0, S // SLOTS) as i:
                    for j in range(SLOTS):
                        pool.wait_ge(summed, i * SLOTS + j + 1)
                        pool.wait_ge(idx_ready, i * SLOTS + j + 1)
                        pool.sem_inc(idx_taken, 1)
                        pool.indirect_dma_start(out=rows[:, j, :], out_offset=None, in_=table,
                                                in_offset=bass.IndirectOffsetOnAxis(ap=idx[:, j:j + 1], axis=0),
                                                ).then_inc(rows_in[j], 16)

            @block.tensor
            def _(pe):
                with pe.Fori(0, S // SLOTS) as i:
                    for j in range(SLOTS):
                        pe.wait_ge(hot_ready, i * SLOTS + j + 1)
                        pe.wait_ge(rows_in[j], i * 16 + (before[j] + 16))
                        pe.matmul(part[j % HALF][:, 0:D], hot[:, j % HALF, :], rows[:, j, :], start=True, stop=True,
                                  ).then_inc(summed, 1)

            @block.vector
            def _(v):
                flat = acc[:].rearrange("p t w -> p (t w)")
                with v.Fori(0, S // SLOTS) as i:
                    for h in range(2):
                        for j in range(h * HALF, h * HALF + HALF):
                            v.tensor_scalar(hot[:, j % HALF, :], g.iota[0:P, 0:P], g.place_s[:, bass.ds(i * SLOTS + j, 1)], None,
                                            ALU.is_equal).then_inc(hot_ready, 1)
                        for j in range(h * HALF, h * HALF + HALF):
                            t = v.value_load(g.tile_of[0:1, bass.ds(i * SLOTS + j, 1)], min_val=0, max_val=T - 1)
                            v.wait_ge(summed, i * SLOTS + j + 1 + SLOTS)
                            v.wait_ge(added, i * SLOTS + j)
                            tile = flat[:, at(t, D)]
                            v.tensor_tensor(tile, tile, part[j % HALF][:, 0:D], ALU.add).then_inc(added, 1)



def gin(nc, g, A):
    L, EMB = A["L2_gnn_W1"].shape[0], A["L2_gnn_W1"].shape[2]
    F1 = EMB // 128
    norm_stats(nc, g, "gin_norm")
    with Stage(nc, g, "gin") as st0:
        acc = st0.sb("acc", [P, T, D])
        table = st0.dram("table", (N, D))
        with Stage(nc, g, "gin_in") as st:
            normed, dv, table_out = st.sem("normed"), st.sem("dv"), st.sem("table_out")
            with st.block() as block:
                @block.vector
                def _(v):
                    x, flat = (a[:].rearrange("p t d -> p (t d)") for a in (g.x, acc))
                    with v.Fori(0, T) as t:
                        v.tensor_scalar(flat[:, at(t, D)], x[:, at(t, D)], g.mean[:, bass.ds(t, 1)], g.rstd[:, bass.ds(t, 1)],
                                        ALU.subtract, ALU.mult).then_inc(normed, 1)

                @block.sync
                def _(sp):
                    with sp.Fori(0, T) as t:
                        sp.wait_ge(normed, t + 1)
                        sp.dma_start(table.rearrange("(t p) d -> p t d", p=P)[:, bass.ds(t, 1), :], acc[:, bass.ds(t, 1), :],
                                     ).then_inc(table_out, 16)
                    sp.wait_ge(table_out, 16 * T)
        for layer in range(L):
            sum_rows(nc, g, f"gin_sum{layer}", table, acc)
            gin_mlp(nc, g, A, layer, L, F1, acc, table)


PARTS = ((0, 3), (3, 2))
W = 3 * P
UNITS = T // GRP * len(PARTS)


def nodes(i, h, offset=0):
    t0, n = PARTS[h]
    return bass.ds(i * (GRP * P) + (t0 * P + offset), n * P)


def gin_mlp(nc, g, A, layer, L, F1, acc, table):
    with Stage(nc, g, f"gin_mlp{layer}") as st:
        z1 = st.sb("z1", [128, F1, N])
        z2 = st.sb("z2", [128, KD, N])
        cols = st.sb("cols", [128, 3, F1 + KD])
        scale = st.sb("scale", [128, F1 + KD])
        shift = st.sb("shift", [128, F1 + KD])
        bias, gamma, beta = (cols[:, n, :] for n in range(3))
        gin_up(nc, g, A, layer, F1, acc, z1, cols, scale, shift)
        gin_down(nc, g, A, layer, F1, z1, z2, bias, gamma, beta, scale, shift)
        gin_back(nc, g, layer == L - 1, layer, F1, z2, scale, shift, acc, table)


def norm_affine(v, q, stat, mv, sd, scale, shift, gamma, beta, var_ready, sd_ready):
    n = mv.shape[1]
    for f in range(n):
        q.mark(v.bn_aggr(mv[:, f, :], stat[:, f, :]))
    q.wait()
    v.tensor_copy(sd[:], mv[:, :, 1]).then_inc(var_ready, 1)
    v.wait_ge(sd_ready, 1)
    q.then(v.reciprocal(scale, sd[:]))
    q.then(v.tensor_tensor(scale, scale, gamma, ALU.mult))
    q.then(v.tensor_tensor(shift, mv[:, :, 0], scale, ALU.mult))
    q.then(v.tensor_tensor(shift, beta, shift, ALU.subtract))


def gin_up(nc, g, A, layer, F1, acc, z1, cols, scale, shift):
    with Stage(nc, g, f"gin_up{layer}") as st:
        w1 = st.sb("w1", [128, KD, F1 * 128])
        eps = st.sb("eps", [128, 1])
        tile = st.sb("tile", [P, GRP, D])
        turn = st.sb("turn", [128, 2, KD, W])
        stat = st.sb("stat", [128, F1, UNITS * 6])
        mv = st.sb("mv", [128, F1, 2])
        sd = st.sb("sd", [128, F1])
        tp = [[st.ps(f"tp{h}{k}", [128, 512]) for k in range(KD)] for h in range(2)]
        zp = [st.ps(f"zp{f}", [128, 512]) for f in range(F1)]
        w_in, tiles, turned, turn_ready, z_done, z_out = (st.sem(n) for n in ("w_in", "tiles", "turned", "turn_ready", "z_done", "z_out"))
        stats, dv, var_ready, sd_ready = (st.sem(n) for n in ("stats", "dv", "var_ready", "sd_ready"))
        accf, z1f, statf = acc[:].rearrange("p t d -> p (t d)"), z1[:].rearrange("p f n -> p (f n)"), stat[:].rearrange("p f c -> p (f c)")
        with st.block() as block:
            @block.sync
            def _(sp):
                for k in range(KD):
                    sp.dma_start(w1[:, k, :], A["L2_gnn_W1"][layer, k * 128:(k + 1) * 128, :]).then_inc(w_in, 16)
                sp.dma_start(cols[:], A["L2_gnn_cols"][layer]).then_inc(w_in, 16)

            @block.vector
            def _(v):
                q = Steps(v, dv)
                q.then(v.memset(eps[:], EPS))
                with v.Fori(0, T // GRP) as i:
                    for h, (t0, n) in enumerate(PARTS):
                        v.wait_ge(turned, i * 2 + h + 1)
                        for j in range(t0, t0 + n):
                            v.tensor_copy(tile[:, j, :], accf[:, at(i * GRP + j, D)]).then_inc(tiles, 1)
                    for h, (t0, n) in enumerate(PARTS):
                        for f in range(F1):
                            v.wait_ge(z_out, (i * 2 + h) * F1 + f + 1 + F1)
                            v.bn_stats(statf[:, bass.ds(i * 12 + (h * 6 + f * UNITS * 6), 6)], z1f[:, nodes(i, h, f * N)]).then_inc(stats, 1)
                v.wait_ge(stats, UNITS * F1)
                v.wait_ge(w_in, 16 * (KD + 1))
                norm_affine(v, q, stat, mv, sd, scale[:, 0:F1], shift[:, 0:F1], cols[:, 1, 0:F1], cols[:, 2, 0:F1], var_ready, sd_ready)

            @block.tensor
            def _(pe):
                pe.sem_inc(turned, 2)
                pe.wait_ge(w_in, 16 * (KD + 1))
                with pe.Fori(0, T // GRP) as i:
                    for h, (t0, n) in enumerate(PARTS):
                        pe.wait_ge(tiles, i * GRP + t0 + n)
                        pe.wait_ge(turn_ready, i * 4 + 2 * h)
                        for k in range(KD):
                            for j in range(n):
                                mm = pe.transpose(tp[h][k][:, j * P:(j + 1) * P], tile[:, t0 + j, k * 128:(k + 1) * 128], g.ident[0:P, 0:P])
                        mm.then_inc(turned, 1)
                    for h, (t0, n) in enumerate(PARTS):
                        pe.wait_ge(turn_ready, i * 4 + 2 * h + 2)
                        for f in range(F1):
                            pe.wait_ge(z_out, (i * 2 + h) * F1 + f + 1)
                            for k in range(KD):
                                mm = pe.matmul(zp[f][:, 0:n * P], w1[:, k, f * 128:(f + 1) * 128], turn[:, h, k, 0:n * P],
                                               start=(k == 0), stop=(k == KD - 1))
                            mm.then_inc(z_done, 1)

            @block.scalar
            def _(act):
                act.sem_inc(z_out, F1)
                act.wait_ge(w_in, 16 * (KD + 1))
                with act.Fori(0, T // GRP) as i:
                    for h, (t0, n) in enumerate(PARTS):
                        act.wait_ge(turned, i * 2 + h + 1 + 2)
                        act.wait_ge(z_done, i * (2 * F1))
                        for k in range(KD):
                            act.activation(turn[:, h, k, 0:n * P], tp[h][k][:, 0:n * P], ACT.Copy).then_inc(turn_ready, 1)
                    for h, (t0, n) in enumerate(PARTS):
                        for f in range(F1):
                            act.wait_ge(z_done, (i * 2 + h) * F1 + f + 1)
                            act.activation(z1f[:, nodes(i, h, f * N)], zp[f][:, 0:n * P], ACT.Identity,
                                           bias=cols[:, 0, f:f + 1]).then_inc(z_out, 1)
                act.wait_ge(var_ready, 1)
                act.activation(sd[:], sd[:], ACT.Sqrt, bias=eps[:]).then_inc(sd_ready, 1)


def gin_down(nc, g, A, layer, F1, z1, z2, bias, gamma, beta, scale, shift):
    with Stage(nc, g, f"gin_down{layer}") as st:
        w2 = st.sb("w2", [128, F1, D])
        eps = st.sb("eps", [128, 1])
        hid = st.sb("hid", [128, 2, F1, W])
        stat = st.sb("stat", [128, KD, UNITS * 6])
        mv = st.sb("mv", [128, KD, 2])
        sd = st.sb("sd", [128, KD])
        zp = [[st.ps(f"zp{h}{d}", [128, 512]) for d in range(KD)] for h in range(2)]
        w_in, hid_ready, z_done, z_out = (st.sem(n) for n in ("w_in", "hid_ready", "z_done", "z_out"))
        stats, dv, var_ready, sd_ready = (st.sem(n) for n in ("stats", "dv", "var_ready", "sd_ready"))
        z1f, z2f, statf = z1[:].rearrange("p f n -> p (f n)"), z2[:].rearrange("p f n -> p (f n)"), stat[:].rearrange("p f c -> p (f c)")
        with st.block() as block:
            @block.sync
            def _(sp):
                for f in range(F1):
                    sp.dma_start(w2[:, f, :], A["L2_gnn_W2"][layer, f * 128:(f + 1) * 128, :]).then_inc(w_in, 16)

            @block.scalar
            def _(act):
                with act.Fori(0, T // GRP) as i:
                    for h, (t0, n) in enumerate(PARTS):
                        act.wait_ge(z_done, i * (2 * KD) + h * KD)
                        for f in range(F1):
                            act.activation(hid[:, h, f, 0:n * P], z1f[:, nodes(i, h, f * N)], ACT.Relu,
                                           scale=scale[:, f:f + 1], bias=shift[:, f:f + 1]).then_inc(hid_ready, 1)
                act.wait_ge(var_ready, 1)
                act.activation(sd[:], sd[:], ACT.Sqrt, bias=eps[:]).then_inc(sd_ready, 1)

            @block.tensor
            def _(pe):
                pe.wait_ge(w_in, 16 * F1)
                with pe.Fori(0, T // GRP) as i:
                    for h, (t0, n) in enumerate(PARTS):
                        for d in range(KD):
                            pe.wait_ge(z_out, i * (2 * KD) + h * KD + d)
                            for f in range(F1):
                                pe.wait_ge(hid_ready, (i * 2 + h) * F1 + f + 1)
                                mm = pe.matmul(zp[h][d][:, 0:n * P], w2[:, f, d * 128:(d + 1) * 128], hid[:, h, f, 0:n * P],
                                               start=(f == 0), stop=(f == F1 - 1))
                            mm.then_inc(z_done, 1)

            @block.vector
            def _(v):
                q = Steps(v, dv)
                q.then(v.memset(eps[:], EPS))
                with v.Fori(0, T // GRP) as i:
                    for h, (t0, n) in enumerate(PARTS):
                        for d in range(KD):
                            v.wait_ge(z_done, (i * 2 + h) * KD + d + 1)
                            v.tensor_scalar(z2f[:, nodes(i, h, d * N)], zp[h][d][:, 0:n * P], bias[:, F1 + d:F1 + d + 1], None,
                                            ALU.add).then_inc(z_out, 1)
                            v.wait_ge(z_out, (i * 2 + h) * KD + d + 1)
                            v.bn_stats(statf[:, bass.ds(i * 12 + (h * 6 + d * UNITS * 6), 6)], z2f[:, nodes(i, h, d * N)]).then_inc(stats, 1)
                v.wait_ge(stats, UNITS * KD)
                norm_affine(v, q, stat, mv, sd, scale[:, F1:], shift[:, F1:], gamma[:, F1:], beta[:, F1:], var_ready, sd_ready)


def gin_back(nc, g, last, layer, F1, z2, scale, shift, acc, table):
    with Stage(nc, g, f"gin_back{layer}") as st:
        hid = st.sb("hid", [128, GRP, KD, P])
        tp = [st.ps(f"tp{j}", [P, 512]) for j in range(GRP)]
        hid_ready, turned, put, table_out = (st.sem(n) for n in ("hid_ready", "turned", "put", "table_out"))
        z2f = z2[:].rearrange("p f n -> p (f n)")
        with st.block() as block:
            @block.scalar
            def _(act):
                with act.Fori(0, T // GRP) as i:
                    for j in range(GRP):
                        act.wait_ge(turned, i * GRP)
                        for d in range(KD):
                            act.activation(hid[:, j, d, :], z2f[:, bass.ds(i * (GRP * P) + (j * P + d * N), P)], ACT.Identity if last else ACT.Relu,
                                           scale=scale[:, F1 + d:F1 + d + 1], bias=shift[:, F1 + d:F1 + d + 1]).then_inc(hid_ready, 1)

            @block.tensor
            def _(pe):
                with pe.Fori(0, T // GRP) as i:
                    for j in range(GRP):
                        pe.wait_ge(put, i * GRP)
                        pe.wait_ge(hid_ready, (i * GRP + j) * KD + KD)
                        for d in range(KD):
                            mm = pe.transpose(tp[j][:, d * 128:(d + 1) * 128], hid[:, j, d, :], g.ident[:])
                        mm.then_inc(turned, 1)

            @block.vector
            def _(v):
                to = (g.x if last else acc)[:].rearrange("p t d -> p (t d)")
                with v.Fori(0, T // GRP) as i:
                    for j in range(GRP):
                        v.wait_ge(turned, i * GRP + j + 1)
                        tile = to[:, at(i * GRP + j, D)]
                        if last:
                            v.tensor_tensor(tile, tile, tp[j][:, 0:D], ALU.add).then_inc(put, 1)
                        else:
                            v.tensor_copy(tile, tp[j][:, 0:D]).then_inc(put, 1)

            @block.sync
            def _(sp):
                if not last:
                    with sp.Fori(0, T) as t:
                        sp.wait_ge(put, t + 1)
                        sp.dma_start(table.rearrange("(t p) d -> p t d", p=P)[:, bass.ds(t, 1), :], acc[:, bass.ds(t, 1), :],
                                     ).then_inc(table_out, 16)
                    sp.wait_ge(table_out, 16 * T)



def store_tables(sp, done, tables):
    for table, values in tables:
        sp.dma_start(table.rearrange("(t p) d -> p t d", p=P), values).then_inc(done, 16)


def edge_logits(nc, g, name, src_table, dst_table, logit, edge=None):
    with Stage(nc, g, name) as st:
        idx = st.sb("idx", [P, GRP, 2 * RUNS], U32)
        of_src = st.sb("of_src", [P, GRP, 128])
        of_dst = st.sb("of_dst", [P, GRP, 128])
        both = st.sb("both", [P, GRP, 128])
        tp = [st.ps(f"tp{j}", [128, 512]) for j in range(2)]
        idx_ready, idx_taken, added, turned, put = (st.sem(n) for n in ("idx_ready", "idx_taken", "added", "turned", "put"))
        rows_in, before = st.gathers(GRP, T // GRP * 2 * RUNS)
        ALL = 2 * RUNS * 16
        src_v, dst_v = (a[:].rearrange("p (r c) -> p c r", r=RUNS) for a in (g.src_e, g.dst_e))
        SUB, PLACES = 4, 4
        LOADS = RUNS // SUB
        if edge is not None:
            feats, proj = edge
            ef = st.sb("ef", [P, PLACES, SUB, D])
            ef_t = st.sb("ef_t", [128, 2, 4 * P])
            ep = [st.ps(f"ep{j}", [128, 512]) for j in range(2)]
            own = [st.ps(f"own{j}", [P, 512]) for j in range(2)]
            ef_in = st.sems("ef_in", PLACES)
            ef_turned, ef_t_ready, projected = (st.sem(n) for n in ("ef_turned", "ef_t_ready", "projected"))
            ef_v = feats.rearrange("(r c p) d -> p c r d", r=RUNS, c=RC)
        PAIRS = RUNS // 2

        with st.block() as block:
            @block.scalar
            def _(act):
                with act.Fori(0, T // GRP) as i:
                    for j in range(GRP):
                        act.wait_ge(rows_in[j], i * ALL + before[j])
                        for n, v in enumerate((src_v, dst_v)):
                            act.activation(idx[:, j:j + 1, n * RUNS:(n + 1) * RUNS], v[:, bass.ds(i * GRP + j, 1), :], ACT.Copy,
                                           ).then_inc(idx_ready, 1)
                    if edge is not None:
                        for u in range(GRP * PAIRS):
                            act.wait_ge(ef_turned, i * (GRP * PAIRS) + u + 1 + 2 * PLACES)
                            act.wait_ge(projected, i * (GRP * PAIRS) + u + 1)
                            act.activation(ef_t[:, u % 2, 0:4 * P], ep[u % 2][:, 0:4 * P], ACT.Copy).then_inc(ef_t_ready, 1)

            @block.gpsimd
            def _(pool):
                pool.sem_inc(added, GRP)
                with pool.Fori(0, T // GRP) as i:
                    for j in range(GRP):
                        pool.wait_ge(added, i * GRP + j + 1)
                        pool.wait_ge(idx_ready, i * (2 * GRP) + 2 * j + 2)
                        pool.sem_inc(idx_taken, 1)
                        for n, (rows, table) in enumerate(((of_src, src_table), (of_dst, dst_table))):
                            for r in range(RUNS):
                                pool.indirect_dma_start(
                                    out=rows[:, j, r * H:(r + 1) * H], out_offset=None, in_=table,
                                    in_offset=bass.IndirectOffsetOnAxis(ap=idx[:, j, n * RUNS + r:n * RUNS + r + 1], axis=0),
                                ).then_inc(rows_in[j], 16)

            @block.vector
            def _(v):
                with v.Fori(0, T // GRP) as i:
                    for j in range(GRP):
                        v.wait_ge(rows_in[j], i * ALL + (before[j] + ALL))
                        if edge is None:
                            v.wait_ge(turned, i * GRP + j)
                            v.tensor_tensor(both[:, j, :], of_src[:, j, :], of_dst[:, j, :], ALU.add).then_inc(added, 1)
                        else:
                            v.wait_ge(turned, i * GRP + j)
                            v.tensor_tensor(of_src[:, j, :], of_src[:, j, :], of_dst[:, j, :], ALU.add).then_inc(put, 1)
                            v.wait_ge(put, i * (2 * GRP) + 2 * j + 1)
                            v.wait_ge(projected, i * (GRP * PAIRS) + ((j + 1) * PAIRS + 2))
                            v.tensor_tensor(both[:, j, :], of_src[:, j, :], own[j % 2][:, 0:128], ALU.add).then_inc(added, 1)
                        v.wait_ge(turned, i * GRP + j + 1)
                        v.tensor_copy(logit[:, at(i * GRP + j, P)], tp[j % 2][:, 0:P]).then_inc(put, 1)

            @block.tensor
            def _(pe):
                if edge is not None:
                    pe.sem_inc(projected, 2)
                    pe.sem_inc(ef_turned, 2 * PLACES)
                with pe.Fori(0, T // GRP) as i:
                    for j in range(GRP):
                        if edge is not None:
                            for m in range(PAIRS):
                                u = j * PAIRS + m
                                s = u // 2
                                if m % 2 == 0:
                                    pe.wait_ge(ef_in[s % PLACES], i * (16 * GRP * LOADS // PLACES) + (16 * (s // PLACES) + 16))
                                for a in range(2):
                                    for k in range(KD):
                                        mm = pe.transpose(ep[u % 2][:, (a * KD + k) * P:(a * KD + k + 1) * P],
                                                          ef[:, s % PLACES, m % 2 * 2 + a, k * 128:(k + 1) * 128], g.ident[0:P, 0:P])
                                mm.then_inc(ef_turned, 1)
                                if m == 0:
                                    pe.wait_ge(added, i * GRP + (j + GRP))
                                pe.wait_ge(ef_t_ready, i * (GRP * PAIRS) + u + 1)
                                for a in range(2):
                                    for k in range(KD):
                                        mm = pe.matmul(own[j % 2][:, (2 * m + a) * H:(2 * m + a + 1) * H],
                                                       ef_t[:, u % 2, (a * KD + k) * P:(a * KD + k + 1) * P], proj[:, k, :],
                                                       start=(k == 0), stop=(k == KD - 1))
                                mm.then_inc(projected, 1)
                        pe.wait_ge(added, i * GRP + (j + 1 + GRP))
                        pe.transpose(tp[j % 2][:, 0:P], both[:, j, :], g.ident[0:P, 0:P]).then_inc(turned, 1)

            if edge is not None:
                @block.sync
                def _(sp):
                    with sp.Fori(0, T // GRP) as i:
                        for s in range(GRP * LOADS):
                            sp.wait_ge(ef_turned, i * (GRP * PAIRS) + 2 * s + 2)
                            sp.dma_start(ef[:, s % PLACES, :, :],
                                         ef_v[:, bass.ds(i * GRP + s // LOADS, 1), s % LOADS * SUB:(s % LOADS + 1) * SUB, :]
                                         .rearrange("p c r d -> p (c r) d")).then_inc(ef_in[s % PLACES], 16)


def segment_scans(nc, g, name, values, gate, op, out_f, out_b):
    inner, outer, empty = (ALU.add, ALU.max, -BIG) if op == "max" else (ALU.mult, ALU.add, 0.0)
    with Stage(nc, g, name) as st:
        gates = st.sb("gates", [128, 2])
        rows = st.sb("rows", [1, 4, 128])
        carry = st.sb("carry", [1, 2, 128])
        col = st.sb("col", [128, 2])
        rp = st.ps("rp", [1, 512])
        cp = st.ps("cp", [128, 512])
        dv, ends, turned, carried, spread_out = (st.sem(n) for n in ("dv", "ends", "turned", "carried", "spread_out"))
        ways = ((out_f[:], gate[:, 0:RUN], values[:]),
                (out_b[:, ::-1], gate[:, RUN:0:-1], values[:, ::-1]))
        with st.block() as block:
            @block.vector
            def _(v):
                q = Steps(v, dv)
                for n, has in enumerate((g.has_border, g.has_border_back)):
                    if op == "max":
                        q.mark(v.tensor_scalar(gates[:, n:n + 1], has[:], -BIG, None, ALU.mult))
                    else:
                        q.mark(v.tensor_scalar(gates[:, n:n + 1], has[:], -1.0, 1.0, ALU.mult, ALU.add))
                q.mark(v.memset(carry[:], empty))
                for out, between, x in ways:
                    q.mark(v.tensor_tensor_scan(out, between, x, empty, inner, outer))
                q.wait()
                v.sem_inc(ends, 1)
                v.wait_ge(turned, 4)
                q.then(v.tensor_copy(rows[:].rearrange("p a n -> p (a n)"), rp[:]))
                runs = [rows[0:1, n, :].rearrange("p (r h) -> p h r", h=H) for n in range(4)]
                into = [carry[0:1, n, :].rearrange("p (r h) -> p h r", h=H) for n in range(2)]
                for h in range(H):
                    q.mark(v.tensor_tensor_scan(into[0][:, h, 1:RUNS], runs[2][:, h, 0:RUNS - 1], runs[0][:, h, 0:RUNS - 1],
                                                empty, inner, outer))
                    q.mark(v.tensor_tensor_scan(into[1][:, h, RUNS - 2::-1], runs[3][:, h, RUNS - 1:0:-1], runs[1][:, h, RUNS - 1:0:-1],
                                                empty, inner, outer))
                q.wait()
                v.sem_inc(carried, 1)
                v.wait_ge(spread_out, 2)
                q.then(v.tensor_copy(col[:], cp[:, 0:2]))
                for n, (out, between, x) in enumerate(ways):
                    q.mark(v.tensor_tensor_scan(out, between, x, col[:, n:n + 1], inner, outer))

            @block.tensor
            def _(pe):
                pe.wait_ge(ends, 1)
                for n, c in enumerate((out_f[:, RUN - 1:RUN], out_b[:, 0:1], gates[:, 0:1], gates[:, 1:2])):
                    pe.transpose(rp[0:1, n * 128:(n + 1) * 128], c, g.ident[:]).then_inc(turned, 1)
                pe.wait_ge(carried, 1)
                for n in range(2):
                    pe.matmul(cp[:, n:n + 1], carry[0:1, n, :], g.ones[0:1, :], start=True, stop=True).then_inc(spread_out, 1)


def edge_weights(nc, g, name, logit, weight, slope=None, mean=None, top=False):
    with Stage(nc, g, name) as st0:
        gate = st0.sb("gate", [128, RUN + 1])
        fwd = st0.sb("fwd", [128, RUN])
        bwd = st0.sb("bwd", [128, RUN])

        def step(tag, body):
            with Stage(nc, g, f"{name}_{tag}") as st:
                dv, before_exp, exps = st.sem("dv"), st.sem("before_exp"), st.sem("exps")
                with st.block() as block:
                    @block.vector
                    def _(v):
                        q = Steps(v, dv)
                        body(v, q)
                        v.sem_inc(before_exp, 1)

                    if tag == "exp":
                        @block.scalar
                        def _(act):
                            act.wait_ge(before_exp, 1)
                            act.activation(logit[:], logit[:], ACT.Exp).then_inc(exps, 1)

        def first(v, q):
            q.mark(v.tensor_scalar(gate[:], g.border[:], -BIG, None, ALU.mult))
            if slope is not None:
                q.mark(v.scalar_tensor_tensor(logit[:], logit[:], slope, logit[:], ALU.mult, ALU.max))
            q.wait()

        def second(v, q):
            q.then(v.tensor_tensor(fwd[:], fwd[:], bwd[:], ALU.max))
            q.mark(v.tensor_tensor(logit[:], logit[:], fwd[:], ALU.subtract))
            if top:
                q.mark(v.tensor_tensor(bwd[:], fwd[:], g.border[:, 1:RUN + 1], ALU.mult))
            q.wait()

        def third(v, q):
            q.then(v.tensor_scalar(gate[:], g.border[:], -1.0, 1.0, ALU.mult, ALU.add))

        def fourth(v, q):
            q.then(v.tensor_tensor(fwd[:], fwd[:], bwd[:], ALU.add))
            q.then(v.tensor_tensor(fwd[:], fwd[:], logit[:], ALU.subtract))
            q.then(v.reciprocal(fwd[:], fwd[:]))
            q.then(v.tensor_tensor(logit[:], logit[:], fwd[:], ALU.mult))

        step("leaky", first)
        segment_scans(nc, g, f"{name}_max", logit, gate, "max", fwd, bwd)
        step("exp", second)
        if mean is not None:
            step("gates", third)
            segment_scans(nc, g, f"{name}_sum", logit, gate, "add", fwd, bwd)
            step("divide", fourth)
        with Stage(nc, g, f"{name}_turn") as st:
            tp = [st.ps(f"tp{j}", [P, 512]) for j in range(4)]
            turned, put, dv = st.sem("turned"), st.sem("put"), st.sem("dv")
            blocks = [(x, n, c) for c in range(RC) for n, x in enumerate((logit, bwd) if top else (logit,))]
            wv = weight[:].rearrange("p (r c) w -> p c r w", r=RUNS)
            with st.block() as block:
                @block.tensor
                def _(pe):
                    for m, (x, n, c) in enumerate(blocks):
                        if m >= 4:
                            pe.wait_ge(put, m - 3)
                        pe.transpose(tp[m % 4][:, 0:128], x[:, c * P:(c + 1) * P], g.ident[:]).then_inc(turned, 1)

                @block.vector
                def _(v):
                    for m, (x, n, c) in enumerate(blocks):
                        v.wait_ge(turned, m + 1)
                        v.tensor_copy(wv[:, c, :, n * H:(n + 1) * H], tp[m % 4][:, 0:128].rearrange("p (r h) -> p r h", h=H)).then_inc(put, 1)
                    if mean is not None:
                        v.wait_ge(put, len(blocks))
                        q = Steps(v, dv)
                        q.then(v.tensor_reduce(mean[:], weight[:], AX.X, ALU.add))
                        q.then(v.tensor_scalar(mean[:], mean[:], 1.0 / H, None, ALU.mult))


def sum_heads(nc, g, name, table, weight, acc):
    WH = weight.shape[2]
    with Stage(nc, g, name) as st:
        idx = st.sb("idx", [P, SLOTS], U32)
        rows = st.sb("rows", [P, SLOTS, D])
        msg = st.sb("msg", [P, HALF, D])
        hot = st.sb("hot", [P, HALF, P])
        part = [st.ps(f"part{j}", [P, 512]) for j in range(HALF)]
        idx_ready, idx_taken, hot_ready, msg_ready, summed, added = (
            st.sem(n) for n in ("idx_ready", "idx_taken", "hot_ready", "msg_ready", "summed", "added"))
        rows_in, before = st.gathers(SLOTS, S // SLOTS)
        accf = acc[:].rearrange("p t w -> p (t w)")
        with st.block() as block:
            @block.scalar
            def _(act):
                with act.Fori(0, S // SLOTS) as i:
                    for j in range(SLOTS):
                        act.wait_ge(rows_in[j], i * 16 + before[j])
                        act.activation(idx[:, j:j + 1], g.src_s[:, bass.ds(i * SLOTS + j, 1)], ACT.Copy).then_inc(idx_ready, 1)

            @block.gpsimd
            def _(pool):
                pool.sem_inc(msg_ready, SLOTS)
                with pool.Fori(0, S // SLOTS) as i:
                    for j in range(SLOTS):
                        pool.wait_ge(msg_ready, i * SLOTS + j + 1)
                        pool.wait_ge(idx_ready, i * SLOTS + j + 1)
                        pool.sem_inc(idx_taken, 1)
                        pool.indirect_dma_start(out=rows[:, j, :], out_offset=None, in_=table,
                                                in_offset=bass.IndirectOffsetOnAxis(ap=idx[:, j:j + 1], axis=0),
                                                ).then_inc(rows_in[j], 16)

            @block.vector
            def _(v):
                with v.Fori(0, S // SLOTS) as i:
                    for h in range(2):
                        for j in range(h * HALF, h * HALF + HALF):
                            v.tensor_scalar(hot[:, j % HALF, :], g.iota[0:P, 0:P], g.place_s[:, bass.ds(i * SLOTS + j, 1)], None,
                                            ALU.is_equal).then_inc(hot_ready, 1)
                            c = v.value_load(g.chunk_of[0:1, bass.ds(i * SLOTS + j, 1)], min_val=0, max_val=C - 1)
                            w = weight[:, bass.ds(c, 1), 0:H].rearrange("p a h -> p (a h)").unsqueeze(2).to_broadcast([P, H, HD])
                            v.wait_ge(rows_in[j], i * 16 + (before[j] + 16))
                            v.tensor_tensor(msg[:, j % HALF, :].rearrange("p (h d) -> p h d", h=H),
                                            rows[:, j, :].rearrange("p (h d) -> p h d", h=H), w, ALU.mult).then_inc(msg_ready, 1)
                        for j in range(h * HALF, h * HALF + HALF):
                            t = v.value_load(g.tile_of[0:1, bass.ds(i * SLOTS + j, 1)], min_val=0, max_val=T - 1)
                            v.wait_ge(summed, i * SLOTS + j + 1)
                            v.wait_ge(added, i * SLOTS + j)
                            tile = accf[:, at(t, D + WH)]
                            v.tensor_tensor(tile, tile, part[j % HALF][:, 0:D + WH], ALU.add).then_inc(added, 1)

            @block.tensor
            def _(pe):
                with pe.Fori(0, S // SLOTS) as i:
                    for j in range(SLOTS):
                        c = pe.value_load(g.chunk_of[0:1, bass.ds(i * SLOTS + j, 1)], min_val=0, max_val=C - 1)
                        pe.wait_ge(hot_ready, i * SLOTS + j + 1)
                        pe.matmul(part[j % HALF][:, D:D + WH], hot[:, j % HALF, :],
                                  weight[:, bass.ds(c, 1), :].rearrange("p a w -> p (a w)"), start=True, stop=True)
                        pe.wait_ge(msg_ready, i * SLOTS + j + 1 + SLOTS)
                        pe.matmul(part[j % HALF][:, 0:D], hot[:, j % HALF, :], msg[:, j % HALF, :], start=True, stop=True,
                                  ).then_inc(summed, 1)


def attention_in(nc, g, name, A, lin, w, att, feat, ends, table):
    with Stage(nc, g, name) as st:
        wl = st.sb("wl", [128, KD, D])
        wg = st.sb("wg", [128, KD, D])
        bl = st.sb("bl", [P, D])
        attb = st.sb("attb", [P, 2, D])
        tile = st.sb("tile", [P, GRP, D])
        h_tile = st.sb("h_tile", [P, GRP, D])
        x_t = st.sb("x_t", [128, GRP, KD, P])
        h_t = st.sb("h_t", [128, GRP, KD, P])
        prod = st.sb("prod", [P, 2, D])
        tp = [st.ps(f"tp{j}", [128, 512]) for j in range(2)]
        hp = [st.ps(f"hp{j}", [P, 512]) for j in range(2)]
        ht = [st.ps(f"ht{j}", [128, 512]) for j in range(2)]
        fp = [st.ps(f"fp{j}", [P, 512]) for j in range(2)]
        w_in, normed, x_turned, x_t_ready, h_done, h_ready, h_turned, h_t_ready, f_done, f_out, dv, out = (
            st.sem(n) for n in ("w_in", "normed", "x_turned", "x_t_ready", "h_done", "h_ready", "h_turned", "h_t_ready",
                                "f_done", "f_out", "dv", "out"))
        xf, ff = g.x[:].rearrange("p t d -> p (t d)"), feat[:].rearrange("p t d -> p (t d)")
        LOADS = 1 + (2 if lin else 0) + 2
        x_h = lin is not None
        with st.block() as block:
            @block.sync
            def _(sp):
                sp.dma_start(wg[:], w.rearrange("(k p) n -> p k n", p=128)).then_inc(w_in, 16)
                for n in range(2):
                    sp.dma_start(attb[:, n, :], spread(att[n])).then_inc(w_in, 16)
                if x_h:
                    sp.dma_start(wl[:], lin[0].rearrange("(k p) n -> p k n", p=128)).then_inc(w_in, 16)
                    sp.dma_start(bl[:], spread(lin[1])).then_inc(w_in, 16)
                with sp.Fori(0, T) as t:
                    sp.wait_ge(f_out, t + 1)
                    sp.dma_start(table.rearrange("(t p) d -> p t d", p=P)[:, bass.ds(t, 1), :], feat[:, bass.ds(t, 1), :]).then_inc(out, 16)
                sp.wait_ge(out, 16 * T)

            @block.vector
            def _(v):
                q = Steps(v, dv)
                v.wait_ge(w_in, 16 * LOADS)
                with q.loop(T // GRP, 4 * GRP + (GRP if x_h else 0)) as i:
                    for j in range(GRP):
                        v.wait_ge(x_turned, i * GRP)
                        t = i * GRP + j
                        v.tensor_scalar(tile[:, j, :], xf[:, at(t, D)], g.mean[:, bass.ds(t, 1)], g.rstd[:, bass.ds(t, 1)],
                                        ALU.subtract, ALU.mult).then_inc(normed, 1)
                    if x_h:
                        for j in range(GRP):
                            v.wait_ge(h_done, i * GRP + j + 1)
                            v.wait_ge(h_turned, i * GRP)
                            v.tensor_tensor(h_tile[:, j, :], hp[j % 2][:, 0:D], bl[:], ALU.add).then_inc(h_ready, 1)
                            v.wait_ge(h_ready, i * GRP + j + 1)
                            to = xf[:, at(i * GRP + j, D)]
                            q.mark(v.tensor_tensor(to, to, h_tile[:, j, :], ALU.add))
                    for j in range(GRP):
                        v.wait_ge(f_done, i * GRP + j + 1)
                        for n in range(2):
                            q.mark(v.tensor_tensor(prod[:, n, :], fp[j % 2][:, 0:D], attb[:, n, :], ALU.mult))
                        v.tensor_copy(ff[:, at(i * GRP + j, D)], fp[j % 2][:, 0:D]).then_inc(f_out, 1)
                        q.wait()
                        for n in range(2):
                            q.mark(v.tensor_reduce(ends[:, bass.ds(i * GRP + j, 1), n * H:(n + 1) * H].rearrange("p t h -> p (t h)"),
                                                   prod[:, n, :].rearrange("p (h d) -> p h d", h=H), AX.X, ALU.add))
                        q.wait()

            @block.tensor
            def _(pe):
                pe.wait_ge(w_in, 16 * LOADS)
                with pe.Fori(0, T // GRP) as i:
                    for j in range(GRP):
                        pe.wait_ge(normed, i * GRP + j + 1)
                        if j < 2:
                            pe.wait_ge(x_t_ready, i * GRP)
                        else:
                            pe.wait_ge(x_t_ready, i * GRP + j - 1)
                        for k in range(KD):
                            mm = pe.transpose(tp[j % 2][:, k * P:(k + 1) * P], tile[:, j, k * 128:(k + 1) * 128], g.ident[0:P, 0:P])
                        mm.then_inc(x_turned, 1)
                    if x_h:
                        for j in range(GRP):
                            pe.wait_ge(x_t_ready, i * GRP + j + 1)
                            if j < 2:
                                pe.wait_ge(h_ready, i * GRP)
                            else:
                                pe.wait_ge(h_ready, i * GRP + j - 1)
                            for k in range(KD):
                                mm = pe.matmul(hp[j % 2][:, 0:D], x_t[:, j, k, :], wl[:, k, :], start=(k == 0), stop=(k == KD - 1))
                            mm.then_inc(h_done, 1)
                        for j in range(GRP):
                            pe.wait_ge(h_ready, i * GRP + j + 1)
                            if j < 2:
                                pe.wait_ge(h_t_ready, i * GRP)
                            else:
                                pe.wait_ge(h_t_ready, i * GRP + j - 1)
                            for k in range(KD):
                                mm = pe.transpose(ht[j % 2][:, k * P:(k + 1) * P], h_tile[:, j, k * 128:(k + 1) * 128], g.ident[0:P, 0:P])
                            mm.then_inc(h_turned, 1)
                    for j in range(GRP):
                        if x_h:
                            pe.wait_ge(h_t_ready, i * GRP + j + 1)
                        else:
                            pe.wait_ge(x_t_ready, i * GRP + j + 1)
                        if j < 2:
                            pe.wait_ge(f_out, i * GRP)
                        else:
                            pe.wait_ge(f_out, i * GRP + j - 1)
                        for k in range(KD):
                            mm = pe.matmul(fp[j % 2][:, 0:D], (h_t if x_h else x_t)[:, j, k, :], wg[:, k, :], start=(k == 0), stop=(k == KD - 1))
                        mm.then_inc(f_done, 1)

            @block.scalar
            def _(act):
                with act.Fori(0, T // GRP) as i:
                    for j in range(GRP):
                        act.wait_ge(x_turned, i * GRP + j + 1)
                        act.wait_ge((h_done if x_h else f_done), i * GRP)
                        act.activation(x_t[:, j, :, :].rearrange("p k n -> p (k n)"), tp[j % 2][:, 0:KD * P], ACT.Copy).then_inc(x_t_ready, 1)
                    if x_h:
                        for j in range(GRP):
                            act.wait_ge(h_turned, i * GRP + j + 1)
                            act.wait_ge(f_done, i * GRP)
                            act.activation(h_t[:, j, :, :].rearrange("p k n -> p (k n)"), ht[j % 2][:, 0:KD * P], ACT.Copy).then_inc(h_t_ready, 1)


def store_ends(nc, g, name, tables):
    with Stage(nc, g, name) as st:
        out = st.sem("out")
        with st.block() as block:
            @block.sync
            def _(sp):
                store_tables(sp, out, tables)
                sp.wait_ge(out, 16 * len(tables))



def gat(nc, g, A):
    norm_stats(nc, g, "gat_norm")
    with Stage(nc, g, "gat") as st0:
        table, src_end, dst_end = st0.dram("table", (N, D)), st0.dram("src_end", (N, H)), st0.dram("dst_end", (N, H))
        with Stage(nc, g, "gat_feat") as st:
            feat = st.sb("feat", [P, T, D])
            ends = st.sb("ends", [P, T, 2 * H])
            attention_in(nc, g, "gat_in", A, (A["L0_gnn_W_lin"], A["L0_gnn_b_lin"]), A["L0_gnn_W_gat"],
                         [a.rearrange("h d -> (h d)") for a in (A["L0_gnn_attn_l"], A["L0_gnn_attn_r"])], feat, ends, table)
            store_ends(nc, g, "gat_ends", ((src_end, ends[:, :, 0:H]), (dst_end, ends[:, :, H:])))
        weight = st0.sb("weight", [P, C, H])
        with Stage(nc, g, "gat_soft") as st:
            logit = st.sb("logit", [128, RUN])
            edge_logits(nc, g, "gat_logits", src_end, dst_end, logit)
            edge_weights(nc, g, "gat_weights", logit, weight, slope=0.2)
        acc = st0.sb("acc", [P, T, D + H])
        clear(nc, g, "gat_clear", acc)
        sum_heads(nc, g, "gat_sum", table, weight, acc)
        with Stage(nc, g, "gat_out") as st:
            bias = st.sb("bias", [P, D])
            share = st.sb("share", [P, T, H])
            z = st.sb("z", [P, D])
            b_in, dv = st.sem("b_in"), st.sem("dv")
            with st.block() as block:
                @block.sync
                def _(sp):
                    sp.dma_start(bias[:], spread(A["L0_gnn_gat_bias"])).then_inc(b_in, 16)

                @block.vector
                def _(v):
                    q = Steps(v, dv)
                    v.wait_ge(b_in, 16)
                    q.then(v.tensor_scalar(share[:], acc[:, :, D:], 1e-30, None, ALU.max))
                    q.then(v.reciprocal(share[:], share[:]))
                    xf, zh = g.x[:].rearrange("p t d -> p (t d)"), z[:].rearrange("p (h d) -> p h d", h=H)
                    with q.loop(T, 4) as t:
                        q.then(v.tensor_tensor(zh, acc[:, bass.ds(t, 1), 0:D].rearrange("p t (h d) -> p (t h) d", h=H),
                                               share[:, bass.ds(t, 1), :].rearrange("p t h -> p (t h)").unsqueeze(2).to_broadcast([P, H, HD]), ALU.mult))
                        q.then(v.tensor_tensor(z[:], z[:], bias[:], ALU.add))
                        q.then(v.scalar_tensor_tensor(z[:], z[:], 0.01, z[:], ALU.mult, ALU.max))
                        q.then(v.tensor_tensor(xf[:, at(t, D)], xf[:, at(t, D)], z[:], ALU.add))


def clear(nc, g, name, acc):
    with Stage(nc, g, name) as st:
        dv = st.sem("dv")
        with st.block() as block:
            @block.vector
            def _(v):
                v.memset(acc[:], 0.0).then_inc(dv, 1)
                v.wait_ge(dv, 1)



def gat_loops(nc, g, A):
    norm_stats(nc, g, "loops_norm")
    with Stage(nc, g, "loops") as st0:
        table, src_end, dst_end = st0.dram("table", (N, D)), st0.dram("src_end", (N, H)), st0.dram("dst_end", (N, H))
        feat = st0.sb("feat", [P, T, D])
        ends = st0.sb("ends", [P, T, 2 * H])
        attention_in(nc, g, "loops_in", A, None, A["L3_gnn_W"],
                     [a.rearrange("h d -> (h d)") for a in (A["L3_gnn_att_src"], A["L3_gnn_att_dst"])], feat, ends, table)
        store_ends(nc, g, "loops_ends", ((src_end, ends[:, :, 0:H]), (dst_end, ends[:, :, H:])))
        weight = st0.sb("weight", [P, C, 2 * H])
        with Stage(nc, g, "loops_soft") as st:
            logit = st.sb("logit", [128, RUN])
            edge_logits(nc, g, "loops_logits", src_end, dst_end, logit)
            edge_weights(nc, g, "loops_weights", logit, weight, slope=0.2, top=True)
        acc = st0.sb("acc", [P, T, D + 2 * H])
        clear(nc, g, "loops_clear", acc)
        sum_heads(nc, g, "loops_sum", table, weight, acc)
        with Stage(nc, g, "loops_join") as st:
            own, most, edge_scale, own_scale, den = (st.sb(n, [P, T, H]) for n in ("own", "most", "edge_scale", "own_scale", "den"))
            bias = st.sb("bias", [P, D])
            z = st.sb("z", [P, 2, D])
            b_in, dv, before_exp, exps = st.sem("b_in"), st.sem("dv"), st.sem("before_exp"), st.sem("exps")
            with st.block() as block:
                @block.sync
                def _(sp):
                    sp.dma_start(bias[:], spread(A["L3_gnn_bias"])).then_inc(b_in, 16)

                @block.scalar
                def _(act):
                    act.wait_ge(before_exp, 1)
                    act.activation(edge_scale[:], edge_scale[:], ACT.Exp).then_inc(exps, 1)
                    act.activation(own_scale[:], own_scale[:], ACT.Exp).then_inc(exps, 1)

                @block.vector
                def _(v):
                    q = Steps(v, dv)
                    q.then(v.tensor_tensor(own[:], ends[:, :, 0:H], ends[:, :, H:], ALU.add))
                    q.then(v.scalar_tensor_tensor(own[:], own[:], 0.2, own[:], ALU.mult, ALU.max))
                    q.then(v.tensor_scalar(den[:], acc[:, :, D:D + H], 0.0, -BIG, ALU.is_equal, ALU.mult))
                    q.then(v.tensor_tensor(edge_scale[:], acc[:, :, D + H:], den[:], ALU.add))
                    q.then(v.tensor_tensor(most[:], edge_scale[:], own[:], ALU.max))
                    q.mark(v.tensor_tensor(edge_scale[:], edge_scale[:], most[:], ALU.subtract))
                    q.then(v.tensor_tensor(own_scale[:], own[:], most[:], ALU.subtract))
                    v.sem_inc(before_exp, 1)
                    v.wait_ge(exps, 2)
                    q.then(v.tensor_tensor(den[:], acc[:, :, D:D + H], edge_scale[:], ALU.mult))
                    q.then(v.tensor_tensor(den[:], den[:], own_scale[:], ALU.add))
                    q.then(v.tensor_scalar(den[:], den[:], 1e-16, None, ALU.add))
                    q.then(v.reciprocal(den[:], den[:]))
                    q.mark(v.tensor_tensor(edge_scale[:], edge_scale[:], den[:], ALU.mult))
                    q.then(v.tensor_tensor(own_scale[:], own_scale[:], den[:], ALU.mult))
                    v.wait_ge(b_in, 16)

                    def by_head(a, t):
                        return a[:, bass.ds(t, 1), 0:D].rearrange("p t (h d) -> p (t h) d", h=H)

                    def over(a, t):
                        return a[:, bass.ds(t, 1), :].rearrange("p t h -> p (t h)").unsqueeze(2).to_broadcast([P, H, HD])

                    with q.loop(T, 4) as t:
                        q.mark(v.tensor_tensor(z[:, 0, :].rearrange("p (h d) -> p h d", h=H), by_head(acc, t), over(edge_scale, t), ALU.mult))
                        q.then(v.tensor_tensor(z[:, 1, :].rearrange("p (h d) -> p h d", h=H), by_head(feat, t), over(own_scale, t), ALU.mult))
                        q.then(v.tensor_tensor(z[:, 0, :], z[:, 0, :], z[:, 1, :], ALU.add))
                        q.then(v.tensor_tensor(acc[:, bass.ds(t, 1), 0:D].rearrange("p t d -> p (t d)"), z[:, 0, :], bias[:], ALU.add))
        norm_stats(nc, g, "loops_out_norm", acc)
        add_normed(nc, g, "loops_out", acc, A["L3_gnn_ln_gamma"], A["L3_gnn_ln_beta"])


def add_normed(nc, g, name, values, gamma, beta):
    with Stage(nc, g, name) as st:
        gb = st.sb("gb", [P, 2, D])
        z = st.sb("z", [P, D])
        c_in, dv = st.sem("c_in"), st.sem("dv")
        with st.block() as block:
            @block.sync
            def _(sp):
                sp.dma_start(gb[:, 0, :], spread(gamma)).then_inc(c_in, 16)
                sp.dma_start(gb[:, 1, :], spread(beta)).then_inc(c_in, 16)

            @block.vector
            def _(v):
                q = Steps(v, dv)
                v.wait_ge(c_in, 32)
                xf = g.x[:].rearrange("p t d -> p (t d)")
                with q.loop(T, 4) as t:
                    q.then(v.tensor_scalar(z[:], values[:, bass.ds(t, 1), 0:D].rearrange("p t d -> p (t d)"), g.mean[:, bass.ds(t, 1)],
                                           g.rstd[:, bass.ds(t, 1)], ALU.subtract, ALU.mult))
                    q.then(v.tensor_tensor(z[:], z[:], gb[:, 0, :], ALU.mult))
                    q.then(v.tensor_tensor(z[:], z[:], gb[:, 1, :], ALU.add))
                    q.then(v.tensor_tensor(xf[:, at(t, D)], xf[:, at(t, D)], z[:], ALU.add))



def sum_edges(nc, g, name, table, feats, mean, acc):
    with Stage(nc, g, name) as st:
        idx = st.sb("idx", [P, SLOTS], U32)
        rows = st.sb("rows", [P, SLOTS, D])
        own = st.sb("own", [P, SLOTS, D + 1])
        hot = st.sb("hot", [P, HALF, P])
        part = [st.ps(f"part{j}", [P, 512]) for j in range(HALF)]
        idx_ready, idx_taken, hot_ready, summed, added, one = (st.sem(n) for n in ("idx_ready", "idx_taken", "hot_ready", "summed", "added", "one"))
        own_in = st.sems("own_in", SLOTS)
        rows_in, before = st.gathers(SLOTS, S // SLOTS)
        accf = acc[:].rearrange("p t w -> p (t w)")
        feats_v = feats.rearrange("(c p) d -> p c d", p=P)
        with st.block() as block:
            @block.scalar
            def _(act):
                with act.Fori(0, S // SLOTS) as i:
                    for j in range(SLOTS):
                        act.wait_ge(rows_in[j], i * 16 + before[j])
                        act.activation(idx[:, j:j + 1], g.src_s[:, bass.ds(i * SLOTS + j, 1)], ACT.Copy).then_inc(idx_ready, 1)

            @block.gpsimd
            def _(pool):
                pool.sem_inc(summed, SLOTS)
                with pool.Fori(0, S // SLOTS) as i:
                    for j in range(SLOTS):
                        pool.wait_ge(summed, i * SLOTS + j + 1)
                        pool.wait_ge(idx_ready, i * SLOTS + j + 1)
                        pool.sem_inc(idx_taken, 1)
                        pool.indirect_dma_start(out=rows[:, j, :], out_offset=None, in_=table,
                                                in_offset=bass.IndirectOffsetOnAxis(ap=idx[:, j:j + 1], axis=0),
                                                ).then_inc(rows_in[j], 16)

            @block.sync
            def _(sp):
                with sp.Fori(0, S // SLOTS) as i:
                    for j in range(SLOTS):
                        c = sp.value_load(g.chunk_of[0:1, bass.ds(i * SLOTS + j, 1)], min_val=0, max_val=C - 1)
                        sp.wait_ge(summed, i * SLOTS + j + 1)
                        sp.dma_start(own[:, j:j + 1, 0:D], feats_v[:, bass.ds(c, 1), :]).then_inc(own_in[j], 16)

            @block.vector
            def _(v):
                v.memset(own[:, :, D:D + 1], 1.0).then_inc(one, 1)
                with v.Fori(0, S // SLOTS) as i:
                    for h in range(2):
                        for j in range(h * HALF, h * HALF + HALF):
                            c = v.value_load(g.chunk_of[0:1, bass.ds(i * SLOTS + j, 1)], min_val=0, max_val=C - 1)
                            v.tensor_scalar(hot[:, j % HALF, :], g.iota[0:P, 0:P], g.place_s[:, bass.ds(i * SLOTS + j, 1)], mean[:, bass.ds(c, 1)],
                                            ALU.is_equal, ALU.mult).then_inc(hot_ready, 1)
                        for j in range(h * HALF, h * HALF + HALF):
                            t = v.value_load(g.tile_of[0:1, bass.ds(i * SLOTS + j, 1)], min_val=0, max_val=T - 1)
                            v.wait_ge(summed, i * SLOTS + j + 1 + SLOTS)
                            v.wait_ge(added, i * SLOTS + j)
                            tile = accf[:, at(t, D + 1)]
                            v.tensor_tensor(tile, tile, part[j % HALF][:, 0:D + 1], ALU.add).then_inc(added, 1)

            @block.tensor
            def _(pe):
                pe.wait_ge(one, 1)
                with pe.Fori(0, S // SLOTS) as i:
                    for j in range(SLOTS):
                        pe.wait_ge(hot_ready, i * SLOTS + j + 1)
                        pe.wait_ge(own_in[j], i * 16 + 16)
                        pe.matmul(part[j % HALF][:, 0:D + 1], hot[:, j % HALF, :], own[:, j, :], start=True, stop=False)
                        pe.wait_ge(rows_in[j], i * 16 + (before[j] + 16))
                        pe.matmul(part[j % HALF][:, 0:D], hot[:, j % HALF, :], rows[:, j, :], start=False, stop=True,
                                  ).then_inc(summed, 1)


def edge_gat(nc, g, A):
    norm_stats(nc, g, "edge_norm")
    with Stage(nc, g, "edge") as st0:
        table, src_end, dst_end = st0.dram("table", (N, D)), st0.dram("src_end", (N, H)), st0.dram("dst_end", (N, H))
        mean = st0.sb("mean", [P, C])
        with Stage(nc, g, "edge_soft") as st1:
            proj = st1.sb("proj", [128, KD, 2 * H])
            ends = st1.sb("ends", [P, T, 2 * H])
            logit = st1.sb("logit", [128, RUN])
            edge_in(nc, g, A, proj, ends, table)
            store_ends(nc, g, "edge_ends", ((src_end, ends[:, :, 0:H]), (dst_end, ends[:, :, H:])))
            edge_logits(nc, g, "edge_logits", src_end, dst_end, logit, (A["edge_attr_256"], proj[:, :, 0:H]))
            weight = st1.sb("weight", [P, C, H])
            edge_weights(nc, g, "edge_weights", logit, weight, mean=mean)
        acc = st0.sb("acc", [P, T, D + 1])
        clear(nc, g, "edge_clear", acc)
        sum_edges(nc, g, "edge_sum", table, A["edge_attr_256"], mean, acc)
        edge_out(nc, g, A, acc)


def edge_in(nc, g, A, proj, ends, table):
    with Stage(nc, g, "edge_in") as st:
        w1 = st.sb("w1", [128, KD, D])
        w4 = st.sb("w4", [128, KD, H])
        b1 = st.sb("b1", [128, KD])
        b45 = st.sb("b45", [1, 2 * H])
        const = st.sb("const", [1, 2 * H])
        one_row = st.sb("one_row", [1, P])
        tile = st.sb("tile", [P, GRP, D])
        x_t = st.sb("x_t", [128, GRP, KD, P])
        pp = [st.ps(f"pp{k}", [128, 512]) for k in range(KD)]
        bp = st.ps("bp", [1, 512])
        tp = [st.ps(f"tp{j}", [128, 512]) for j in range(2)]
        ep = [st.ps(f"ep{j}", [P, 512]) for j in range(2)]
        w_in, made, proj_done, proj_ready, dv, normed, x_turned, x_t_ready, e_done, e_out, out = (
            st.sem(n) for n in ("w_in", "made", "proj_done", "proj_ready", "dv", "normed", "x_turned", "x_t_ready", "e_done", "e_out", "out"))
        xf = g.x[:].rearrange("p t d -> p (t d)")
        with st.block() as block:
            @block.sync
            def _(sp):
                sp.dma_start(w1[:], A["L1_gnn_W1"].rearrange("(k p) n -> p k n", p=128)).then_inc(w_in, 16)
                sp.dma_start(w4[:], A["L1_gnn_W4_t"].rearrange("(k p) n -> p k n", p=128)).then_inc(w_in, 16)
                sp.dma_start(proj[:, :, H:], A["L1_gnn_W5_t"].rearrange("(k p) n -> p k n", p=128)).then_inc(w_in, 16)
                sp.dma_start(b1[:], A["L1_gnn_b1_col"]).then_inc(w_in, 16)
                sp.dma_start(b45[0:1, 0:H], row(A["L1_gnn_b4"])).then_inc(w_in, 16)
                sp.dma_start(b45[0:1, H:], row(A["L1_gnn_b5"])).then_inc(w_in, 16)
                tv = table.rearrange("(t p) d -> p t d", p=P)
                with sp.Fori(0, T // GRP) as i:
                    for j in range(GRP):
                        sp.wait_ge(normed, i * GRP + j + 1)
                        sp.dma_start(tv[:, bass.ds(i * GRP + j, 1), :], tile[:, j:j + 1, :]).then_inc(out, 16)
                sp.wait_ge(out, 16 * T)

            @block.vector
            def _(v):
                q = Steps(v, dv)
                v.memset(one_row[:], 1.0).then_inc(made, 1)
                q.then(v.memset(const[:], 0.0))
                v.wait_ge(w_in, 16 * 6)
                v.wait_ge(proj_done, KD + 1)
                for k in range(KD):
                    q.mark(v.tensor_copy(proj[:, k, 0:H], pp[k][:, 0:H]))
                q.then(v.tensor_tensor(const[0:1, H:], b45[0:1, 0:H], b45[0:1, H:], ALU.add))
                q.then(v.tensor_tensor(const[0:1, H:], const[0:1, H:], bp[0:1, 0:H], ALU.add))
                v.sem_inc(proj_ready, 1)
                with v.Fori(0, T // GRP) as i:
                    for j in range(GRP):
                        v.wait_ge(x_turned, i * GRP)
                        v.wait_ge(out, i * (16 * GRP))
                        t = i * GRP + j
                        v.tensor_scalar(tile[:, j, :], xf[:, at(t, D)], g.mean[:, bass.ds(t, 1)], g.rstd[:, bass.ds(t, 1)],
                                        ALU.subtract, ALU.mult).then_inc(normed, 1)
                    for j in range(GRP):
                        v.wait_ge(e_done, i * GRP + j + 1)
                        v.tensor_copy(ends[:, bass.ds(i * GRP + j, 1), :].rearrange("p t h -> p (t h)"), ep[j % 2][:, 0:2 * H]).then_inc(e_out, 1)

            @block.scalar
            def _(act):
                with act.Fori(0, T // GRP) as i:
                    for j in range(GRP):
                        act.wait_ge(x_turned, i * GRP + j + 1)
                        act.wait_ge(e_done, i * GRP)
                        act.activation(x_t[:, j, :, :].rearrange("p k n -> p (k n)"), tp[j % 2][:, 0:KD * P], ACT.Copy).then_inc(x_t_ready, 1)

            @block.tensor
            def _(pe):
                pe.wait_ge(w_in, 16 * 6)
                pe.wait_ge(made, 1)
                for k in range(KD):
                    for m in range(KD):
                        mm = pe.matmul(pp[k][:, 0:H], w1[:, m, k * 128:(k + 1) * 128], w4[:, m, :], start=(m == 0), stop=(m == KD - 1))
                    mm.then_inc(proj_done, 1)
                for m in range(KD):
                    mm = pe.matmul(bp[0:1, 0:H], b1[:, m:m + 1], w4[:, m, :], start=(m == 0), stop=(m == KD - 1))
                mm.then_inc(proj_done, 1)
                pe.wait_ge(proj_ready, 1)
                with pe.Fori(0, T // GRP) as i:
                    for j in range(GRP):
                        pe.wait_ge(normed, i * GRP + j + 1)
                        pe.wait_ge(x_t_ready, i * GRP + max(j - 1, 0))
                        for k in range(KD):
                            mm = pe.transpose(tp[j % 2][:, k * P:(k + 1) * P], tile[:, j, k * 128:(k + 1) * 128], g.ident[0:P, 0:P])
                        mm.then_inc(x_turned, 1)
                    for j in range(GRP):
                        pe.wait_ge(x_t_ready, i * GRP + j + 1)
                        pe.wait_ge(e_out, i * GRP + max(j - 1, 0))
                        for k in range(KD):
                            pe.matmul(ep[j % 2][:, 0:2 * H], x_t[:, j, k, :], proj[:, k, :], start=(k == 0), stop=False)
                        pe.matmul(ep[j % 2][:, 0:2 * H], one_row[:], const[:], start=False, stop=True).then_inc(e_done, 1)


def edge_out(nc, g, A, acc):
    SLOPE = 11.0 / 48.0
    with Stage(nc, g, "edge_out") as st:
        w23 = st.sb("w23", [128, KD, 2 * D])
        w1 = st.sb("w1", [128, KD, D])
        b = st.sb("b", [P, 3, D])
        tile = st.sb("tile", [P, GRP, 2, D])
        x_t = st.sb("x_t", [128, GRP, 2, KD, P])
        z = st.sb("z", [P, GRP, 2 * D])
        iso = st.sb("iso", [P, T])
        linked = st.sb("linked", [P, T])
        tp = [st.ps(f"tp{j}", [128, 512]) for j in range(2)]
        sp_ = [st.ps(f"sp{j}", [P, 512]) for j in range(2)]
        ap_ = [st.ps(f"ap{j}", [P, 512]) for j in range(2)]
        w_in, normed, turned, x_t_ready, done, z_out, dv = (
            st.sem(n) for n in ("w_in", "normed", "turned", "x_t_ready", "done", "z_out", "dv"))
        xf = g.x[:].rearrange("p t d -> p (t d)")
        with st.block() as block:
            @block.sync
            def _(sp):
                sp.dma_start(w23[:, :, 0:D], A["L1_gnn_W2_t"].rearrange("(k p) n -> p k n", p=128)).then_inc(w_in, 16)
                sp.dma_start(w23[:, :, D:], A["L1_gnn_W3_t"].rearrange("(k p) n -> p k n", p=128)).then_inc(w_in, 16)
                sp.dma_start(w1[:], A["L1_gnn_W1_t"].rearrange("(k p) n -> p k n", p=128)).then_inc(w_in, 16)
                for n, v in enumerate((A["L1_gnn_b2"], A["L1_gnn_b3"], A["L1_gnn_b1"])):
                    sp.dma_start(b[:, n, :], spread(v)).then_inc(w_in, 16)

            @block.vector
            def _(v):
                q = Steps(v, dv)
                sums = acc[:, :, D]
                q.mark(v.tensor_scalar(iso[:], sums, 0.0, None, ALU.is_equal))
                q.then(v.tensor_scalar(linked[:], sums, 0.0, None, ALU.not_equal))
                v.wait_ge(w_in, 16 * 6)
                with q.loop(T // GRP, GRP * 7) as i:
                    for j in range(GRP):
                        v.wait_ge(turned, i * (2 * GRP))
                        t = i * GRP + j
                        v.tensor_scalar(tile[:, j, 0, :], xf[:, at(t, D)], g.mean[:, bass.ds(t, 1)], g.rstd[:, bass.ds(t, 1)],
                                        ALU.subtract, ALU.mult).then_inc(normed, 1)
                        v.tensor_copy(tile[:, j, 1, :], acc[:, bass.ds(t, 1), 0:D].rearrange("p t d -> p (t d)")).then_inc(normed, 1)
                    for j in range(GRP):
                        t = i * GRP + j
                        v.wait_ge(done, i * GRP + j + 1)
                        zj = z[:, j, 0:D]
                        q.then(v.tensor_tensor(z[:, j, :], sp_[j % 2][:], b[:, 0:2, :].rearrange("p a d -> p (a d)"), ALU.add))
                        q.then(v.tensor_scalar(zj, zj, linked[:, bass.ds(t, 1)], None, ALU.mult))
                        q.then(v.scalar_tensor_tensor(zj, z[:, j, D:], iso[:, bass.ds(t, 1)], zj, ALU.mult, ALU.add))
                        q.then(v.scalar_tensor_tensor(zj, b[:, 2, :], acc[:, bass.ds(t, 1), D:D + 1].rearrange("p t d -> p (t d)"), zj, ALU.mult, ALU.add))
                        q.then(v.tensor_tensor(zj, zj, ap_[j % 2][:, 0:D], ALU.add))
                        v.sem_inc(z_out, 1)
                        q.then(v.scalar_tensor_tensor(zj, zj, SLOPE, zj, ALU.mult, ALU.max))
                        q.then(v.tensor_tensor(xf[:, at(t, D)], xf[:, at(t, D)], zj, ALU.add))

            @block.scalar
            def _(act):
                with act.Fori(0, T // GRP) as i:
                    for j in range(GRP):
                        for n in range(2):
                            act.wait_ge(turned, i * (2 * GRP) + 2 * j + n + 1)
                            act.wait_ge(done, i * GRP)
                            act.activation(x_t[:, j, n, :, :].rearrange("p k n -> p (k n)"), tp[n][:, 0:KD * P], ACT.Copy).then_inc(x_t_ready, 1)

            @block.tensor
            def _(pe):
                pe.wait_ge(w_in, 16 * 6)
                with pe.Fori(0, T // GRP) as i:
                    for j in range(GRP):
                        for n in range(2):
                            pe.wait_ge(normed, i * (2 * GRP) + 2 * j + n + 1)
                            pe.wait_ge(x_t_ready, i * (2 * GRP) + max(2 * j + n - 1, 0))
                            for k in range(KD):
                                mm = pe.transpose(tp[n][:, k * P:(k + 1) * P], tile[:, j, n, k * 128:(k + 1) * 128], g.ident[0:P, 0:P])
                            mm.then_inc(turned, 1)
                    for j in range(GRP):
                        pe.wait_ge(x_t_ready, i * (2 * GRP) + 2 * j + 2)
                        pe.wait_ge(z_out, i * GRP + max(j - 1, 0))
                        for k in range(KD):
                            pe.matmul(sp_[j % 2][:], x_t[:, j, 0, k, :], w23[:, k, :], start=(k == 0), stop=(k == KD - 1))
                        for k in range(KD):
                            mm = pe.matmul(ap_[j % 2][:, 0:D], x_t[:, j, 1, k, :], w1[:, k, :], start=(k == 0), stop=(k == KD - 1))
                        mm.then_inc(done, 1)



def nodes_turned(nc, g, name, x_t, heads, head_out, width, bias=None):
    with Stage(nc, g, name) as st:
        w = st.sb("w", [128, KD, width])
        b = st.sb("b", [P, width])
        bias_two = st.sb("bias_two", [P, width])
        tile = st.sb("tile", [P, GRP, D])
        part = st.sb("part", [128, GRP, KD, P])
        tp = [st.ps(f"tp{j}", [128, 512]) for j in range(2)]
        hp = [st.ps(f"hp{j}", [P, 512]) for j in range(2)]
        w_in, normed, turned, part_ready, kept, done, out = (
            st.sem(n) for n in ("w_in", "normed", "turned", "part_ready", "kept", "done", "out"))
        LOADS = (heads is not None) + len(bias or ())
        with st.block() as block:
            @block.sync
            def _(sp):
                if heads is not None:
                    sp.dma_start(w[:], heads).then_inc(w_in, 16)
                for n, v in enumerate(bias or ()):
                    sp.dma_start(b[:] if n == 0 else bias_two[:], spread(v)).then_inc(w_in, 16)

            @block.vector
            def _(v):
                xf = g.x[:].rearrange("p t d -> p (t d)")
                if bias:
                    v.wait_ge(w_in, 16 * LOADS)
                    if len(bias) == 2:
                        v.tensor_tensor(b[:], b[:], bias_two[:], ALU.add).then_inc(out, 1)
                    else:
                        v.sem_inc(out, 1)
                else:
                    v.sem_inc(out, 1)
                v.wait_ge(out, 1)
                with v.Fori(0, T // GRP) as i:
                    for j in range(GRP):
                        t = i * GRP + j
                        v.wait_ge(turned, i * GRP)
                        v.tensor_scalar(tile[:, j, :], xf[:, at(t, D)], g.mean[:, bass.ds(t, 1)], g.rstd[:, bass.ds(t, 1)],
                                        ALU.subtract, ALU.mult).then_inc(normed, 1)
                    if heads is not None:
                        for j in range(GRP):
                            v.wait_ge(done, i * GRP + j + 1)
                            to = head_out[:, bass.ds(i * GRP + j, 1), :].rearrange("p t h -> p (t h)")
                            if bias:
                                v.tensor_tensor(to, hp[j % 2][:, 0:width], b[:], ALU.add).then_inc(out, 1)
                            else:
                                v.tensor_copy(to, hp[j % 2][:, 0:width]).then_inc(out, 1)

            @block.scalar
            def _(act):
                with act.Fori(0, T // GRP) as i:
                    for j in range(GRP):
                        cols = tp[j % 2][:, 0:KD * P].rearrange("p (k n) -> p k n", k=KD)
                        act.wait_ge(turned, i * GRP + j + 1)
                        if heads is not None:
                            act.wait_ge(done, i * GRP)
                            act.activation(part[:, j, :, :], cols, ACT.Copy).then_inc(part_ready, 1)
                        act.activation(x_t[:, :, bass.ds(i * (GRP * P) + j * P, P)], cols, ACT.Copy).then_inc(kept, 1)

            @block.tensor
            def _(pe):
                if heads is not None:
                    pe.wait_ge(w_in, 16 * LOADS)
                with pe.Fori(0, T // GRP) as i:
                    for j in range(GRP):
                        pe.wait_ge(normed, i * GRP + j + 1)
                        pe.wait_ge(kept, i * GRP + max(j - 1, 0))
                        for k in range(KD):
                            mm = pe.transpose(tp[j % 2][:, k * P:(k + 1) * P], tile[:, j, k * 128:(k + 1) * 128], g.ident[0:P, 0:P])
                        mm.then_inc(turned, 1)
                    if heads is not None:
                        for j in range(GRP):
                            pe.wait_ge(part_ready, i * GRP + j + 1)
                            pe.wait_ge(out, i * GRP + max(j - 1, 0) + 1)
                            for k in range(KD):
                                mm = pe.matmul(hp[j % 2][:, 0:width], part[:, j, k, :], w[:, k, :], start=(k == 0), stop=(k == KD - 1))
                            mm.then_inc(done, 1)


def ffn(nc, g, name, x_t, w1, b1, w2, FB, func, finish, scratch, gate=None):
    with Stage(nc, g, name) as st:
        hid = st.sb("hid", [128, 2, W])
        used = st.sb("used", [128, 2, W]) if gate else hid
        if gate:
            coef_t, sel, b2, experts = gate
            spans = sel.shape[1]
            share = FB // spans
            coef = st.sb("coef", [experts, 2, W])
        hp = [st.ps(f"hp{j}", [128, 512]) for j in range(2)]
        cp = [st.ps(f"cp{j}", [128, 512]) for j in range(2)]
        ap = [st.ps(f"ap{j}", [P, 512]) for j in range(3)]
        coef_ready, spread_out, hid_done, hid_ready, gated, taken, put, dv = (
            st.sem(n) for n in ("coef_ready", "spread_out", "hid_done", "hid_ready", "gated", "taken", "put", "dv"))
        b_in = st.sem("b_in")
        tools = scratch(st, b_in)
        loads = tools.loads
        with st.block() as block:
            if loads:
                @block.sync
                def _(sp):
                    for to, of in loads:
                        sp.dma_start(to, of).then_inc(b_in, 16)

            @block.scalar
            def _(act):
                act.sem_inc(hid_ready, 2)
                with act.Fori(0, T // GRP) as i:
                    for h, (t0, n) in enumerate(PARTS):
                        for f in range(FB):
                            u = h * FB + f
                            act.wait_ge(hid_done, i * (2 * FB) + u + 1)
                            act.wait_ge(gated if gate else taken, i * (2 * FB) + u + 1)
                            act.activation(hid[:, f % 2, 0:n * P], hp[f % 2][:, 0:n * P], func, bias=b1[:, f:f + 1]).then_inc(hid_ready, 1)

            @block.vector
            def _(v):
                q = Steps(v, dv)
                if loads:
                    v.wait_ge(b_in, 16 * len(loads))
                if gate:
                    v.sem_inc(gated, 2)
                with q.loop(T // GRP, GRP * tools.steps) as i:
                    for h, (t0, n) in enumerate(PARTS):
                        if gate:
                            v.tensor_copy(coef[:, h, 0:n * P], coef_t[:, nodes(i, h)]).then_inc(coef_ready, 1)
                            for f in range(FB):
                                u = h * FB + f
                                v.wait_ge(hid_ready, i * (2 * FB) + u + 1 + 2)
                                v.wait_ge(spread_out, i * (2 * spans) + h * spans + f // share + 1)
                                v.wait_ge(taken, i * (2 * FB) + u + 1)
                                v.tensor_tensor(used[:, f % 2, 0:n * P], hid[:, f % 2, 0:n * P], cp[f // share % 2][:, 0:n * P],
                                                ALU.mult).then_inc(gated, 1)
                        v.wait_ge(taken, i * (2 * FB) + (h * FB + FB + 2))
                        for j in range(n):
                            finish(v, q, tools, i * GRP + t0 + j, ap[j][:, 0:D])
                        v.sem_inc(put, 1)

            @block.tensor
            def _(pe):
                pe.sem_inc(taken, 2)
                with pe.Fori(0, T // GRP) as i:
                    for h, (t0, n) in enumerate(PARTS):
                        def up(f):
                            u = h * FB + f
                            if gate and f % share == 0:
                                if f == 0:
                                    pe.wait_ge(coef_ready, i * 2 + h + 1)
                                pe.wait_ge(gated, i * (2 * FB) + (h * FB + max(f - share, 0) + 2))
                                pe.matmul(cp[f // share % 2][:, 0:n * P], sel[:, f // share, :], coef[:, h, 0:n * P], start=True, stop=True,
                                          ).then_inc(spread_out, 1)
                            pe.wait_ge(hid_ready, i * (2 * FB) + u + 1)
                            for k in range(KD):
                                mm = pe.matmul(hp[f % 2][:, 0:n * P], w1[:, k, f * 128:(f + 1) * 128], x_t[:, k, nodes(i, h)],
                                               start=(k == 0), stop=(k == KD - 1))
                            mm.then_inc(hid_done, 1)

                        def down(f):
                            u = h * FB + f
                            pe.wait_ge(gated if gate else hid_ready, i * (2 * FB) + u + 1 + 2)
                            for j in range(n):
                                mm = pe.matmul(ap[j][:, 0:D], used[:, f % 2, j * P:(j + 1) * P], w2[:, f, :],
                                               start=(f == 0 and not gate), stop=(f == FB - 1))
                            mm.then_inc(taken, 1)

                        up(0)
                        pe.wait_ge(put, i * 2 + h)
                        if gate:
                            for j in range(n):
                                pe.matmul(ap[j][:, 0:D], coef[:, h, j * P:(j + 1) * P], b2, start=True, stop=False)
                        for f in range(FB):
                            if f + 1 < FB:
                                up(f + 1)
                            down(f)


def add_result(relu):
    def scratch(st, b_in):
        return Tools(1)

    def finish(v, q, tools, t, result):
        x = tools.x[:, at(t, D)]
        if relu:
            q.then(v.scalar_tensor_tensor(x, result, 0.0, x, ALU.max, ALU.add))
        else:
            q.then(v.tensor_tensor(x, x, result, ALU.add))
    return scratch, finish


def load_all(nc, g, name, loads):
    with Stage(nc, g, name) as st:
        w_in = st.sem("w_in")
        with st.block() as block:
            @block.sync
            def _(sp):
                for to, of in loads:
                    sp.dma_start(to, of).then_inc(w_in, 16)
                sp.wait_ge(w_in, 16 * len(loads))


def choose(nc, g, name, logit, coef_t, experts, top):
    with Stage(nc, g, name) as st:
        l = st.sb("l", [P, GRP, experts])
        best = st.sb("best", [P, GRP, 8])
        where = st.sb("where", [P, GRP, 8], U32)
        place = st.sb("place", [P, GRP, 2])
        share = st.sb("share", [P, GRP, 2])
        den = st.sb("den", [P, GRP])
        mask = st.sb("mask", [P, GRP, 2, experts])
        tp = [st.ps(f"tp{j}", [experts, 512]) for j in range(2)]
        dv, waited, gap_ready, exp_ready, mask_ready, turned, put = (st.sem(n) for n in ("dv", "waited", "gap_ready", "exp_ready", "mask_ready", "turned", "put"))
        with st.block() as block:
            @block.vector
            def _(v):
                q = Steps(v, dv)
                with q.loop(T // GRP, 4 * GRP + (0 if top == 1 else 3 + 2 * GRP)) as i:
                    v.wait_ge(turned, i * GRP)
                    for j in range(GRP):
                        q.mark(v.tensor_copy(l[:, j, :], logit[:, bass.ds(i * GRP + j, 1), :].rearrange("p t e -> p (t e)")))
                    q.wait()
                    v.sem_inc(waited, 1)
                    for j in range(GRP):
                        q.mark(v.max(best[:, j, :], l[:, j, :]))
                    q.wait()
                    v.sem_inc(waited, 1)
                    for j in range(GRP):
                        q.mark(v.max_index(where[:, j, :], best[:, j, :], l[:, j, :]))
                    q.wait()
                    for j in range(GRP):
                        q.mark(v.tensor_copy(place[:, j, :], where[:, j, 0:2]))
                    q.wait()
                    if top == 1:
                        for j in range(GRP):
                            v.tensor_scalar(mask[:, j, 0, :], g.iota[0:P, 0:experts], place[:, j, 0:1], None, ALU.is_equal).then_inc(mask_ready, 1)
                    else:
                        v.tensor_tensor(share[:, :, 1], best[:, :, 1], best[:, :, 0], ALU.subtract).then_inc(gap_ready, 1)
                        v.wait_ge(exp_ready, i + 1)
                        q.then(v.tensor_scalar(den[:], share[:, :, 1], 1.0, None, ALU.add))
                        q.then(v.reciprocal(share[:, :, 0], den[:]))
                        q.then(v.tensor_tensor(share[:, :, 1], share[:, :, 1], share[:, :, 0], ALU.mult))
                        for j in range(GRP):
                            for n in range(2):
                                q.mark(v.tensor_scalar(mask[:, j, n, :], g.iota[0:P, 0:experts], place[:, j, n:n + 1], share[:, j, n:n + 1],
                                                       ALU.is_equal, ALU.mult))
                        q.wait()
                        for j in range(GRP):
                            v.tensor_tensor(mask[:, j, 0, :], mask[:, j, 0, :], mask[:, j, 1, :], ALU.add).then_inc(mask_ready, 1)
                    for j in range(GRP):
                        v.wait_ge(turned, i * GRP + j + 1)
                        v.tensor_copy(coef_t[:, bass.ds(i * (GRP * P) + j * P, P)], tp[j % 2][:, 0:P]).then_inc(put, 1)

            if top == 2:
                @block.scalar
                def _(act):
                    with act.Fori(0, T // GRP) as i:
                        act.wait_ge(gap_ready, i + 1)
                        act.activation(share[:, :, 1], share[:, :, 1], ACT.Exp).then_inc(exp_ready, 1)

            @block.tensor
            def _(pe):
                with pe.Fori(0, T // GRP) as i:
                    for j in range(GRP):
                        pe.wait_ge(mask_ready, i * GRP + j + 1)
                        pe.wait_ge(put, i * GRP + max(j - 1, 0))
                        pe.transpose(tp[j % 2][:, 0:P], mask[:, j, 0, :], g.ident[0:P, 0:P]).then_inc(turned, 1)


def moe(nc, g, name, heads, bias, w1, b1_col, w2, b2, sel_in, experts, hidden, top, relu):
    FB = experts * hidden // 128
    norm_stats(nc, g, f"{name}_norm")
    with Stage(nc, g, name) as st:
        x_t = st.sb("x_t", [128, KD, N])
        coef_t = st.sb("coef_t", [experts, N])
        w1s = st.sb("w1s", [128, KD, FB * 128])
        w2s = st.sb("w2s", [128, FB, D])
        b1s = st.sb("b1s", [128, FB])
        b2s = st.sb("b2s", [experts, D])
        sel = st.sb("sel", list(sel_in.shape))
        with Stage(nc, g, f"{name}_gate") as st1:
            logit = st1.sb("logit", [P, T, experts])
            nodes_turned(nc, g, f"{name}_in", x_t, heads, logit, experts, bias)
            choose(nc, g, f"{name}_choose", logit, coef_t, experts, top)
        load_all(nc, g, f"{name}_load",
                 [(w1s[:, k, :].rearrange("p (e h) -> p e h", h=hidden), w1[:, k * 128:(k + 1) * 128, :].rearrange("e p h -> p e h")) for k in range(KD)]
                 + [(w2s[:], w2.rearrange("e h d -> (e h) d").rearrange("(f p) d -> p f d", p=128)),
                    (b1s[:], b1_col), (b2s[:], b2), (sel[:], sel_in)])
        scratch, finish = add_result(relu)

        def with_x(st, b_in):
            tools = scratch(st, b_in)
            tools.x = g.x[:].rearrange("p t d -> p (t d)")
            return tools

        ffn(nc, g, f"{name}_ffn", x_t, w1s, b1s, w2s, FB, ACT.Relu, finish, with_x, (coef_t, sel, b2s[:], experts))


def moe_one(nc, g, A):
    moe(nc, g, "one", A["L0_ffn_router_w_t"].rearrange("(k p) n -> p k n", p=128), [A["L0_ffn_router_b"]], A["L0_ffn_W1"], A["L0_ffn_b1_col"], A["L0_ffn_W2"], A["L0_ffn_b2"], A["sel_one"], 32, 64, 1, True)


def moe_two(nc, g, A):
    moe(nc, g, "two", A["L2_ffn_Wg"].rearrange("(k p) n -> p k n", p=128), [A["L2_ffn_bg"], A["L2_ffn_bias"]], A["L2_ffn_W1"], A["L2_ffn_b1_col"], A["L2_ffn_W2"], A["L2_ffn_b2"], A["sel_two"], 8, 512, 2, False)



def moe_all(nc, g, A):
    EX, F = A["L1_ffn_W1"].shape[0], A["L1_ffn_W1"].shape[2]
    FE = F // 128
    CAPACITY = float(-(-N * 5 // (4 * EX)))
    norm_stats(nc, g, "all_norm")
    with Stage(nc, g, "all") as st0:
        x_t = st0.sb("x_t", [128, KD, N])
        w1s = st0.sb("w1s", [128, KD, 2 * F])
        w2s = st0.sb("w2s", [128, 2 * FE, D])
        b1s = st0.sb("b1s", [128, 2 * FE])
        b2s = st0.sb("b2s", [P, D])
        y = st0.sb("y", [P, T, D])
        nodes_turned(nc, g, "all_in", x_t, None, None, 1)
        with Stage(nc, g, "all_route") as st:
            wr = st.sb("wr", [128, KD, EX])
            br = st.sb("br", [1, EX])
            b2 = st.sb("b2", [EX, D])
            mean = st.sb("mean", [128, KD])
            p = st.sb("p", [1, EX])
            r = st.sb("r", [1, EX])
            one = st.sb("one", [1, 4])
            best = st.sb("best", [1, 8])
            where = st.sb("where", [1, 8], U32)
            place = st.sb("place", [1, 2])
            share = st.sb("share", [1, 2])
            dense = st.sb("dense", [1, 2, EX])
            dense_col = st.sb("dense_col", [EX, P])
            ones = st.sb("ones", [1, 128])
            share_col = st.sb("share_col", [128, 2])
            lp = st.ps("lp", [1, 512])
            dp = st.ps("dp", [EX, 512])
            sp_ = st.ps("sp", [128, 512])
            bp = st.ps("bp", [P, 512])
            c_in, w_in, dv, mean_ready, logit_ready, exp_in, exp_out, chosen, shared, ready, col_ready = (
                st.sem(n) for n in ("c_in", "w_in", "dv", "mean_ready", "logit_ready", "exp_in", "exp_out", "chosen", "shared", "ready", "col_ready"))
            with st.block() as block:
                @block.sync
                def _(sp):
                    sp.dma_start(wr[:], A["L1_ffn_Wr"].rearrange("(k p) n -> p k n", p=128)).then_inc(c_in, 16)
                    sp.dma_start(br[:], row(A["L1_ffn_br"])).then_inc(c_in, 16)
                    sp.dma_start(b2[:], A["L1_ffn_b2"]).then_inc(c_in, 16)
                    sp.wait_ge(chosen, 1)
                    for n in range(2):
                        e = sp.value_load(where[0:1, n:n + 1], min_val=0, max_val=EX - 1)
                        for k in range(KD):
                            sp.dma_start(w1s[:, k:k + 1, n * F:(n + 1) * F],
                                         A["L1_ffn_W1"][bass.ds(e, 1), k * 128:(k + 1) * 128, :].rearrange("e p h -> p e h")).then_inc(w_in, 16)
                        for f in range(FE):
                            sp.dma_start(w2s[:, n * FE + f:n * FE + f + 1, :],
                                         A["L1_ffn_W2"][bass.ds(e, 1), f * 128:(f + 1) * 128, :].rearrange("e p d -> p e d")).then_inc(w_in, 16)
                        sp.dma_start(b1s[:, n * FE:(n + 1) * FE].rearrange("p (e f) -> p e f", e=1),
                                     A["L1_ffn_b1_col"][bass.ds(e, 1), :, :].rearrange("e p f -> p e f")).then_inc(w_in, 16)

                LOADS = 2 * (KD + FE + 1)

                @block.scalar
                def _(act):
                    for n, x in enumerate((p, r, share)):
                        act.wait_ge(exp_in, n + 1)
                        act.activation(x[:], x[:], ACT.Exp).then_inc(exp_out, 1)

                @block.vector
                def _(v):
                    q = Steps(v, dv)

                    def softmax(x, turn):
                        q.then(v.tensor_reduce(one[:, 0:1], x[:], AX.X, ALU.max))
                        q.then(v.tensor_scalar(x[:], x[:], one[:, 0:1], None, ALU.subtract))
                        v.sem_inc(exp_in, 1)
                        v.wait_ge(exp_out, turn)
                        q.then(v.tensor_reduce(one[:, 0:1], x[:], AX.X, ALU.add))
                        q.then(v.reciprocal(one[:, 1:2], one[:, 0:1]))
                        q.then(v.tensor_scalar(x[:], x[:], one[:, 1:2], None, ALU.mult))

                    q.mark(v.memset(ones[:], 1.0))
                    for k in range(KD):
                        q.mark(v.tensor_reduce(mean[:, k:k + 1], x_t[:, k, :], AX.X, ALU.add))
                    q.wait()
                    q.then(v.tensor_scalar(mean[:], mean[:], 1.0 / N, None, ALU.mult))
                    v.sem_inc(mean_ready, 1)
                    v.wait_ge(logit_ready, 1)
                    v.wait_ge(c_in, 48)
                    q.then(v.tensor_tensor(p[:], lp[:, 0:EX], br[:], ALU.add))
                    softmax(p, 1)
                    q.then(v.tensor_scalar(r[:], p[:], float(N), None, ALU.mult))
                    q.then(v.reciprocal(r[:], r[:]))
                    q.then(v.tensor_scalar(r[:], r[:], CAPACITY, 1.0, ALU.mult, ALU.min))
                    q.then(v.tensor_tensor(r[:], r[:], p[:], ALU.mult))
                    softmax(r, 2)
                    q.then(v.max(best[:], r[:]))
                    q.then(v.max_index(where[:], best[:], r[:]))
                    v.sem_inc(chosen, 1)
                    q.then(v.tensor_copy(place[:], where[:, 0:2]))
                    q.then(v.memset(share[:, 0:1], 0.0))
                    q.then(v.tensor_tensor(share[:, 1:2], best[:, 1:2], best[:, 0:1], ALU.subtract))
                    v.sem_inc(exp_in, 1)
                    v.wait_ge(exp_out, 3)
                    q.then(v.tensor_reduce(one[:, 0:1], share[:], AX.X, ALU.add))
                    q.then(v.reciprocal(one[:, 1:2], one[:, 0:1]))
                    q.then(v.tensor_scalar(share[:], share[:], one[:, 1:2], None, ALU.mult))
                    for n in range(2):
                        q.mark(v.tensor_scalar(dense[:, n, :], g.iota[0:1, 0:EX], place[:, n:n + 1], share[:, n:n + 1], ALU.is_equal, ALU.mult))
                    q.wait()
                    q.then(v.tensor_tensor(dense[:, 0, :], dense[:, 0, :], dense[:, 1, :], ALU.add))
                    v.sem_inc(shared, 1)
                    v.wait_ge(ready, 2)
                    q.mark(v.tensor_copy(share_col[:], sp_[:, 0:2]))
                    v.tensor_copy(dense_col[:], dp[:, 0:1].to_broadcast([EX, P])).then_inc(col_ready, 1)
                    v.wait_ge(ready, 3)
                    q.then(v.tensor_copy(b2s[:], bp[:, 0:D]))
                    v.wait_ge(w_in, 16 * LOADS)
                    for n in range(2):
                        q.mark(v.tensor_scalar(w2s[:, n * FE:(n + 1) * FE, :], w2s[:, n * FE:(n + 1) * FE, :], share_col[:, n:n + 1], None, ALU.mult))
                    q.wait()

                @block.tensor
                def _(pe):
                    pe.wait_ge(c_in, 48)
                    pe.wait_ge(mean_ready, 1)
                    for k in range(KD):
                        mm = pe.matmul(lp[:, 0:EX], mean[:, k:k + 1], wr[:, k, :], start=(k == 0), stop=(k == KD - 1))
                    mm.then_inc(logit_ready, 1)
                    pe.wait_ge(shared, 1)
                    pe.matmul(sp_[:, 0:2], ones[:], share[:], start=True, stop=True).then_inc(ready, 1)
                    pe.matmul(dp[:, 0:1], dense[:, 0, :], ones[:, 0:1], start=True, stop=True).then_inc(ready, 1)
                    pe.wait_ge(col_ready, 1)
                    pe.matmul(bp[:, 0:D], dense_col[:], b2[:], start=True, stop=True).then_inc(ready, 1)

        def scratch(st, b_in):
            tools = Tools(3)
            tools.n = st.sb("n", [P, D])
            return tools

        def finish(v, q, tools, t, result):
            q.then(v.tensor_scalar(tools.n[:], g.x[:, bass.ds(t, 1), :].rearrange("p t d -> p (t d)"), g.mean[:, bass.ds(t, 1)],
                                   g.rstd[:, bass.ds(t, 1)], ALU.subtract, ALU.mult))
            q.then(v.tensor_tensor(tools.n[:], tools.n[:], b2s[:], ALU.add))
            q.then(v.tensor_tensor(y[:, bass.ds(t, 1), :].rearrange("p t d -> p (t d)"), tools.n[:], result, ALU.add))

        ffn(nc, g, "all_ffn", x_t, w1s, b1s, w2s, 2 * FE, ACT.Gelu, finish, scratch)
        norm_stats(nc, g, "all_out_norm", y)
        add_normed(nc, g, "all_out", y, A["L1_ffn_gamma"], A["L1_ffn_beta"])



def ffn_top(nc, g, A):
    HID = A["L3_ffn_w1"].shape[1]
    FB = HID // 128
    KEEP = int(0.5 * N) - 1
    norm_stats(nc, g, "top_norm")
    with Stage(nc, g, "top") as st0:
        x_t = st0.sb("x_t", [128, KD, N])
        w1s = st0.sb("w1s", [128, KD, HID])
        w2s = st0.sb("w2s", [128, FB, D])
        b1s = st0.sb("b1s", [128, FB])
        coef = st0.sb("coef", [P, T])
        with Stage(nc, g, "top_rank") as st1:
            weight = st1.sb("weight", [P, T, 1])
            nodes_turned(nc, g, "top_in", x_t, A["L3_ffn_wr_col"], weight, 1, [A["L3_ffn_br"]])
            with Stage(nc, g, "top_count") as st:
                all_w = st.sb("all_w", [P, N])
                junk = st.sb("junk", [P, N])
                pid = st.sb("pid", [P, 1])
                before = st.sb("before", [P, P])
                count = st.sb("count", [P, 4, T])
                rows = st.sb("rows", [T, P])
                rp = st.ps("rp", [T, 512])
                row_d = st.dram("row", (N,))
                out, w_in, made, dv, turned, rows_ready = (st.sem(n) for n in ("out", "w_in", "made", "dv", "turned", "rows_ready"))
                with st.block() as block:
                    @block.sync
                    def _(sp):
                        sp.dma_start(w1s[:], A["L3_ffn_w1"].rearrange("(k p) n -> p k n", p=128)).then_inc(out, 16)
                        sp.dma_start(w2s[:], A["L3_ffn_w2"].rearrange("(f p) n -> p f n", p=128)).then_inc(out, 16)
                        sp.dma_start(b1s[:], A["L3_ffn_b1_col"]).then_inc(out, 16)
                        sp.wait_ge(rows_ready, 1)
                        sp.dma_start(row_d.rearrange("(t p) -> t p", p=P), rows[:]).then_inc(out, 16)
                        sp.wait_ge(out, 64)
                        sp.dma_start(all_w[:], spread(row_d)).then_inc(w_in, 16)

                    @block.gpsimd
                    def _(pool):
                        pool.iota(pid[:], pattern=[[0, 1]], base=0, channel_multiplier=1, allow_small_or_imprecise_dtypes=True).then_inc(made, 1)

                    @block.tensor
                    def _(pe):
                        pe.transpose(rp[:, 0:P], weight[:, :, 0], g.ident[0:P, 0:P]).then_inc(turned, 1)

                    @block.vector
                    def _(v):
                        q = Steps(v, dv)
                        v.wait_ge(turned, 1)
                        v.tensor_copy(rows[:], rp[:, 0:P]).then_inc(rows_ready, 1)
                        v.wait_ge(made, 1)
                        q.then(v.tensor_scalar(before[:], g.iota[0:P, 0:P], pid[:, 0:1], None, ALU.is_lt))
                        q.then(v.memset(count[:], 0.0))
                        v.wait_ge(w_in, 16)
                        for t in range(T):
                            w = weight[:, t, :]
                            if t:
                                q.then(v.tensor_scalar(junk[:, 0:t * P], all_w[:, 0:t * P], w, None, ALU.is_ge, ALU.add, accum_out=count[:, 0, t:t + 1]))
                            q.then(v.tensor_scalar(junk[:, t * P:], all_w[:, t * P:], w, None, ALU.is_gt, ALU.add, accum_out=count[:, 1, t:t + 1]))
                            q.then(v.scalar_tensor_tensor(junk[:, 0:P], all_w[:, t * P:(t + 1) * P], w, before[:], ALU.is_equal, ALU.mult,
                                                          accum_out=count[:, 2, t:t + 1]))
                        q.then(v.tensor_tensor(count[:, 0, :], count[:, 0, :], count[:, 1, :], ALU.add))
                        q.then(v.tensor_tensor(count[:, 0, :], count[:, 0, :], count[:, 2, :], ALU.add))
                        q.then(v.scalar_tensor_tensor(coef[:], count[:, 0, :], float(KEEP), weight[:, :, 0], ALU.is_lt, ALU.mult))

        def scratch(st, b_in):
            b2, y, n = (st.sb(name, [P, D]) for name in ("b2", "y", "n"))
            tools = Tools(4, ((b2[:], spread(A["L3_ffn_b2"])),))
            tools.b2, tools.y, tools.n = b2, y, n
            return tools

        def finish(v, q, tools, t, result):
            x = g.x[:, bass.ds(t, 1), :].rearrange("p t d -> p (t d)")
            q.mark(v.tensor_tensor(tools.y[:], result, tools.b2[:], ALU.add))
            q.then(v.tensor_scalar(tools.n[:], x, g.mean[:, bass.ds(t, 1)], g.rstd[:, bass.ds(t, 1)], ALU.subtract, ALU.mult))
            q.then(v.scalar_tensor_tensor(tools.y[:], tools.y[:], coef[:, bass.ds(t, 1)], tools.n[:], ALU.mult, ALU.add))
            q.then(v.tensor_tensor(x, x, tools.y[:], ALU.add))

        ffn(nc, g, "top_ffn", x_t, w1s, b1s, w2s, FB, ACT.Gelu_apprx_tanh, finish, scratch)



def build(nc, A, out, layers):
    with ExitStack() as ctx:
        g = Core()
        g.first_sem = min(nc.free_semaphores)
        g.gather_sems = [ctx.enter_context(nc.semaphore(f"gathered{i}", max(nc.free_semaphores))) for i in range(32)]
        g.gathered = [0] * 32

        def sb(name, shape, dt=F32):
            return ctx.enter_context(nc.sbuf_tensor(name, shape, dt))

        g.x = sb("x", [P, T, D])
        g.ident = sb("ident", [128, 128])
        g.iota = sb("iota", [128, 128])
        g.ones = sb("ones", [128, 1])
        g.src_e = sb("src_e", [P, C], U32)
        g.dst_e = sb("dst_e", [P, C], U32)
        g.src_s = sb("src_s", [P, S], U32)
        g.place_s = sb("place_s", [P, S])
        g.chunk_of = sb("chunk_of", [1, S], I32)
        g.tile_of = sb("tile_of", [1, S], I32)
        g.border = sb("border", [128, RUN + 1])
        g.has_border = sb("has_border", [128, 1])
        g.has_border_back = sb("has_border_back", [128, 1])
        g.mean = sb("mean", [P, T])
        g.rstd = sb("rstd", [P, T])

        prepare(nc, g, A)
        for layer in layers:
            layer(nc, g, A)
        with Stage(nc, g, "store") as st:
            stored = st.sem("stored")
            with st.block() as block:
                @block.sync
                def _(sp):
                    for t in range(T):
                        sp.dma_start(out[t * P:(t + 1) * P, :], g.x[:, t, :]).then_inc(stored, 16)
                    sp.wait_ge(stored, 16 * T)


LAYERS = (gat, moe_one, edge_gat, moe_all, gin, moe_two, gat_loops, ffn_top)


def laid_out(inputs):
    a = {n: np.ascontiguousarray(v) for n, v in inputs.items() if n != "L3_ffn_attention_mask"}

    def cols(v):
        return np.swapaxes(v.reshape(v.shape[0], -1, 128), 1, 2)

    def take(names):
        return [cols(a.pop(n)) for n in names]

    a["src_by_place"] = np.ascontiguousarray(a["src"].reshape(C, P).T)
    a["dst_by_place"] = np.ascontiguousarray(a["dst"].reshape(C, P).T)
    rows = [np.concatenate(take([f"L2_gnn_{m}1{n}", f"L2_gnn_{m}2{n}"]), 2) for m, n in (("b", ""), ("bn", "_gamma"), ("bn", "_beta"))]
    a["L2_gnn_cols"] = np.ascontiguousarray(np.stack(rows, 2))
    for n in ("W1", "W2", "W3", "W4", "W5"):
        a[f"L1_gnn_{n}_t"] = np.ascontiguousarray(a[f"L1_gnn_{n}"].T)
    a["L1_gnn_b1_col"] = np.ascontiguousarray(a["L1_gnn_b1"].reshape(KD, 128).T)
    a["L0_ffn_router_w_t"] = np.ascontiguousarray(a["L0_ffn_router_w"].T)
    for n in ("L0_ffn_b1", "L2_ffn_b1", "L3_ffn_b1"):
        a[n + "_col"] = np.ascontiguousarray(a[n].reshape(-1, 128).T)
    a["L3_ffn_wr_col"] = np.ascontiguousarray(a["L3_ffn_wr"].reshape(KD, 128, 1).swapaxes(0, 1))
    a["L1_ffn_b1_col"] = np.ascontiguousarray(cols(a["L1_ffn_b1"]))
    a["sel_one"] = np.ascontiguousarray(np.repeat(np.eye(32, dtype=np.float32), 64, 1).reshape(32, 16, 128))
    a["sel_two"] = np.ascontiguousarray(np.repeat(np.eye(8, dtype=np.float32), 128, 1).reshape(8, 8, 128))
    a["ident"] = np.eye(128, dtype=np.float32)
    return a


def kernel(**inputs):
    import concourse.bacc as bacc
    from concourse.bass_utils import run_bass_kernel_spmd

    nc = bacc.Bacc("TRN2", target_bir_lowering=False, num_devices=1)
    arrays = laid_out({n: np.asarray(v) for n, v in inputs.items()})
    A = {n: nc.dram_tensor(n + "_in", v.shape, mybir.dt.from_np(v.dtype), kind="ExternalInput").ap()
         for n, v in arrays.items()}
    out = nc.dram_tensor("out", (N, D), F32, kind="ExternalOutput").ap()
    build(nc, A, out, LAYERS)
    r = run_bass_kernel_spmd(nc, [{n + "_in": v for n, v in arrays.items()}], core_ids=[0])
    return r.results[0]["out"]
```

```python
from contextlib import ExitStack, contextmanager

import numpy as np

import concourse.bass as bass
from concourse import mybir

F32 = mybir.dt.float32
I32 = mybir.dt.int32
U32 = mybir.dt.uint32
ALU = mybir.AluOpType
ACT = mybir.ActivationFunctionType
AX = mybir.AxisListType
ENGINE = mybir.EngineType

N, E, D = 3125, 50000, 256
P = 125
T = N // P
C = E // P
KD = D // 128
H = 8
HD = D // H
S = C + T - 1
QUAD = 4
SLOTS = 4 * QUAD
QUADS = S // QUAD
BODIES = QUADS // 4
BANKS = 8
RUNS = 16
RUN = E // RUNS
RC = RUN // P
GRP = 5
BIG = 1e30
EPS = 1e-5
assert S % QUAD == 0 and QUADS % 4 == 2 and RUNS * H == 128 and RC == T and T % GRP == 0


class Core:
    pass


class Tools:

    def __init__(self, steps, loads=()):
        self.steps, self.loads = steps, loads


class Steps:

    def __init__(self, eng, sem):
        self.eng, self.sem, self.n, self.i, self.per = eng, sem, 0, None, 0

    def mark(self, ins):
        ins.then_inc(self.sem, 1)
        self.n += 1
        return self.n

    def value(self, n=None):
        n = self.n if n is None else n
        return n if self.i is None else self.i * self.per + n

    def wait(self, n=None):
        self.eng.wait_ge(self.sem, self.value(n))

    def then(self, ins):
        self.mark(ins)
        self.wait()

    @contextmanager
    def loop(self, count, per):
        start = self.n
        with self.eng.Fori(0, count) as i:
            self.i, self.per = i, per
            yield i
            assert self.n - start == per, (self.n - start, per)
        self.i, self.n = None, start + count * per


def at(i, n):
    return bass.ds(i * n, n)


class Stage:

    def __init__(self, nc, g, name):
        self.nc, self.g, self.name, self.ctx, self.taken = nc, g, name, ExitStack(), []

    def __enter__(self):
        return self

    def __exit__(self, *a):
        if a[0] is None and self.taken:
            self.nc.all_engine_barrier(sems_to_clear=range(self.taken[0], self.taken[-1] + 1))
        self.ctx.close()

    def sb(self, name, shape, dt=F32):
        return self.ctx.enter_context(self.nc.sbuf_tensor(f"{self.name}_{name}", shape, dt))

    def ps(self, name, shape, dt=F32):
        return self.ctx.enter_context(self.nc.psum_tensor(f"{self.name}_{name}", shape, dt))

    def sem(self, name):
        number = self.g.first_sem + len(self.taken)
        self.taken.append(number)
        return self.ctx.enter_context(self.nc.semaphore(f"{self.name}_{name}", number))

    def sems(self, name, n):
        return [self.sem(f"{name}{i}") for i in range(n)]

    def gathers(self, n, count, first=0):
        numbers = range(first, first + n)
        got = [self.g.gather_sems[i] for i in numbers], [self.g.gathered[i] for i in numbers]
        for k, i in enumerate(numbers):
            self.g.gathered[i] += 16 * (count[k] if isinstance(count, list) else count)
        return got

    def dram(self, name, shape, dt=F32):
        return self.nc.dram_tensor(f"{self.name}_{name}", shape, dt, kind="Internal").ap()

    def block(self):
        return self.nc.Block()


def for_quads(eng, quad):
    with eng.Fori(0, BODIES) as i:
        for q in range(4):
            quad(i * SLOTS, q)
    for q in range(QUADS % 4):
        quad(BODIES * SLOTS, q)


def for_quads_ahead(v, tiles, step, add):
    for j in range(QUAD):
        step(0, j)
    with v.Fori(0, BODIES) as i:
        for j, t in enumerate(tiles(i * SLOTS, SLOTS)):
            step(i * SLOTS, QUAD + j)
            add(i * SLOTS, j, t)
    s = BODIES * SLOTS
    for j, t in enumerate(tiles(s, S - s)):
        if s + QUAD + j < S:
            step(s, QUAD + j)
        add(s, j, t)


def load_steps(nc, eng, table, s, n, most):
    return nc.values_load_multi_w_load_instructions(table[0:1, bass.ds(s, n)], engines=(eng,), min_val=0, max_val=most)[1]


def row(ap):
    return ap.rearrange("(a n) -> a n", a=1)


def spread(ap, p=P):
    n = ap.shape[0]
    return bass.AP(ap.tensor, ap.offset, [[0, p], [1, n]])



def prepare(nc, g, A):
    with Stage(nc, g, "prep") as st:
        PS = S // 4
        thr = st.sb("thr", [T, 1])
        first_i = st.sb("first_i", [1, C], I32)
        first = st.sb("first", [1, C])
        ones = st.sb("ones", [T, 128])
        past = st.sb("past", [T, C])
        kio = st.sb("kio", [128, C])
        begin = st.sb("begin", [128, C])
        sio = st.sb("sio", [PS, 4])
        junk = st.sb("junk", [128, C])
        cnt = st.sb("cnt", [PS, 4])
        kf = st.sb("kf", [PS, 4])
        tf = st.sb("tf", [PS, 4])
        ki = st.sb("ki", [PS, 4], I32)
        ti = st.sb("ti", [PS, 4], I32)
        base = st.sb("base", [PS, 4])
        src_rows = st.sb("src_rows", [PS, 4, P], I32)
        dst_rows = st.sb("dst_rows", [PS, 4, P], I32)
        src_f = st.sb("src_f", [PS, 4, P])
        dst_f = st.sb("dst_f", [PS, 4, P])
        win_i = st.sb("win_i", [128, RUN + 2], I32)
        win = st.sb("win", [128, RUN + 2])
        last_i = st.sb("last_i", [P, C], I32)
        last = st.sb("last", [P, C])
        node = st.sb("node", [P, T])
        chunk_f = st.sb("chunk_f", [P, T])
        chunk_i = st.sb("chunk_i", [P, T], I32)
        chunk_dst = st.sb("chunk_dst", [P, T, P], I32)
        less = st.sb("less", [P, T])
        same = st.sb("same", [P, T])
        zeros = st.sb("zeros", [P, C * H])
        b1 = st.ps("b1", [T, C])
        b2 = st.ps("b2", [128, C])
        tp = [st.ps(f"tp{j}", [128, 128]) for j in range(2)]
        k_dram = st.dram("k", (PS, 4), I32)
        t_dram = st.dram("t", (PS, 4), I32)

        x_in, small_in, win_in, rows_in = st.sem("x_in"), st.sem("small_in"), st.sem("win_in"), st.gathers(8, 1)[0]
        tabs_out, tabs_in, made = st.sem("tabs_out"), st.sem("tabs_in"), st.sem("made")
        spread_first, summed, dv, steps_known = st.sem("spread_first"), st.sem("summed"), st.sem("dv"), st.sem("steps_known")
        node_in, node_set, chunks_known, last_in, zeroed = st.gathers(1, T, 8)[0][0], st.sem("node_set"), st.sem("chunks_known"), st.sem("last_in"), st.sem("zeroed")
        first_ready, past_ready, rows_ready, turned, wset = st.sem("first_ready"), st.sem("past_ready"), st.sem("rows_ready"), st.sem("turned"), st.sem("wset")

        with st.block() as block:
            @block.sync
            def _(sp):
                sp.dma_start(first_i[:], row(A["dst_by_place"][0, :])).then_inc(small_in, 16)
                sp.dma_start(g.ident[:], A["ident"]).then_inc(small_in, 16)
                sp.dma_start(g.src_e[:], A["src_by_place"].bitcast(U32)).then_inc(small_in, 16)
                sp.dma_start(g.dst_e[:], A["dst_by_place"].bitcast(U32)).then_inc(small_in, 16)
                sp.dma_start(last_i[:], spread(A["dst_by_place"][P - 1, :])).then_inc(last_in, 16)
                sp.wait_ge(node_set, 2)
                sp.dma_start(g.first_rows[0:E, :].rearrange("(p c) h -> p (c h)", p=P), zeros[:]).then_inc(zeroed, 16)
                for t in range(T):
                    sp.dma_start(g.x[:, t, :], A["x"][t * P:(t + 1) * P, :]).then_inc(x_in, 16)
                sp.wait_ge(wset, 1)
                flat = A["dst"]
                for r in range(RUNS):
                    lo, n, off = r * RUN - 1, RUN + 2, 0
                    if r == 0:
                        lo, n, off = 0, n - 1, 1
                    if r == RUNS - 1:
                        n -= 1
                    sp.dma_start(win_i[r * H:(r + 1) * H, off:off + n],
                                 bass.AP(flat.tensor, flat.offset + lo, [[0, H], [1, n]])).then_inc(win_in, 16)
                sp.wait_ge(steps_known, 1)
                sp.dma_start(k_dram, ki[:]).then_inc(tabs_out, 16)
                sp.dma_start(t_dram, ti[:]).then_inc(tabs_out, 16)
                sp.wait_ge(tabs_out, 32)
                sp.dma_start(g.chunk_of[:], k_dram.rearrange("(o p) j -> o (p j)", o=1)).then_inc(tabs_in, 16)
                sp.dma_start(g.tile_of[:], t_dram.rearrange("(o p) j -> o (p j)", o=1)).then_inc(tabs_in, 16)
                sp.wait_ge(tabs_in, 32)
                sp.wait_ge(x_in, 16 * T)
                sp.wait_ge(zeroed, 16)

            @block.gpsimd
            def _(pool):
                pool.iota(thr[:], pattern=[[0, 1]], base=P, channel_multiplier=P,
                          allow_small_or_imprecise_dtypes=True).then_inc(made, 1)
                pool.iota(kio[:], pattern=[[1, C]], base=0, channel_multiplier=0,
                          allow_small_or_imprecise_dtypes=True).then_inc(made, 1)
                pool.iota(sio[:], pattern=[[1, 4]], base=0, channel_multiplier=4,
                          allow_small_or_imprecise_dtypes=True).then_inc(made, 1)
                pool.iota(g.iota[:], pattern=[[1, 128]], base=0, channel_multiplier=0,
                          allow_small_or_imprecise_dtypes=True).then_inc(made, 1)
                pool.memset(ones[:], 1.0).then_inc(made, 1)
                pool.memset(g.ones[:], 1.0).then_inc(made, 1)
                pool.memset(win_i[:], -1).then_inc(wset, 1)
                pool.memset(zeros[:], 0.0).then_inc(node_set, 1)
                pool.iota(node[:], pattern=[[P, T]], base=0, channel_multiplier=1,
                          allow_small_or_imprecise_dtypes=True).then_inc(node_set, 1)
                src_c, dst_c = (a.rearrange("(c p) -> c p", p=P) for a in (A["src"], A["dst"]))
                pool.wait_ge(steps_known, 1)
                for j in range(4):
                    for n, (rows, table) in enumerate(((src_rows, src_c), (dst_rows, dst_c))):
                        pool.indirect_dma_start(
                            out=rows[:, j, :], out_offset=None, in_=table,
                            in_offset=bass.IndirectOffsetOnAxis(ap=ki[:, j:j + 1].bitcast(U32), axis=0),
                        ).then_inc(rows_in[2 * j + n], 16)

                pool.wait_ge(chunks_known, 1)
                for t in range(T):
                    pool.indirect_dma_start(out=chunk_dst[:, t, :], out_offset=None, in_=dst_c,
                                            in_offset=bass.IndirectOffsetOnAxis(ap=chunk_i[:, t:t + 1].bitcast(U32), axis=0),
                                            ).then_inc(node_in, 16)

            @block.tensor
            def _(pe):
                pe.wait_ge(made, 6)
                pe.wait_ge(first_ready, 1)
                pe.matmul(b1[:], ones[0:1, 0:T], first[:], start=True, stop=True).then_inc(spread_first, 1)
                pe.wait_ge(past_ready, 1)
                pe.matmul(b2[:], ones[:], past[:], start=True, stop=True).then_inc(summed, 1)
                for n in range(8):
                    f = (src_f, dst_f)[n % 2]
                    pe.wait_ge(rows_ready, n + 1)
                    pe.wait_ge(small_in, 64)
                    if n >= 2:
                        pe.wait_ge(turned, n - 1)
                    pe.transpose(tp[n % 2][0:P, 0:PS], f[:, n // 2, :], g.ident[0:PS, 0:PS]).then_inc(summed, 1)

            @block.vector
            def _(v):
                q = Steps(v, dv)
                v.wait_ge(small_in, 64)
                v.tensor_copy(first[:], first_i[:]).then_inc(first_ready, 1)
                v.wait_ge(made, 6)
                v.wait_ge(spread_first, 1)
                v.tensor_scalar(past[:], b1[:], thr[:, 0:1], None, ALU.is_ge).then_inc(past_ready, 1)
                v.wait_ge(summed, 1)
                q.then(v.tensor_tensor(begin[:], kio[:], b2[:], ALU.add))
                for j in range(4):
                    q.then(v.tensor_scalar(junk[0:PS, :], begin[0:PS, :], sio[:, j:j + 1], None, ALU.is_le, ALU.add,
                                           accum_out=cnt[:, j:j + 1]))
                q.then(v.tensor_scalar(kf[:], cnt[:], -1.0, 0.0, ALU.add, ALU.max))
                q.then(v.tensor_tensor(tf[:], sio[:], kf[:], ALU.subtract))
                q.then(v.tensor_scalar(tf[:], tf[:], float(T - 1), None, ALU.min))
                q.then(v.tensor_scalar(base[:], tf[:], float(P), None, ALU.mult))
                q.then(v.tensor_copy(ki[:], kf[:]))
                v.tensor_copy(ti[:], tf[:]).then_inc(steps_known, 1)
                v.wait_ge(last_in, 16)
                v.wait_ge(node_set, 2)
                q.then(v.tensor_copy(last[:], last_i[:]))
                for t in range(T):
                    q.mark(v.tensor_scalar(junk[0:P, :], last[:], node[:, t:t + 1], None, ALU.is_lt, ALU.add, accum_out=chunk_f[:, t:t + 1]))
                    q.wait()
                q.then(v.tensor_scalar(chunk_f[:], chunk_f[:], float(C - 1), None, ALU.min))
                v.tensor_copy(chunk_i[:], chunk_f[:]).then_inc(chunks_known, 1)
                for j in range(4):
                    v.wait_ge(rows_in[2 * j], 16)
                    v.tensor_copy(src_f[:, j, :], src_rows[:, j, :]).then_inc(rows_ready, 1)
                    v.wait_ge(rows_in[2 * j + 1], 16)
                    v.tensor_scalar(dst_f[:, j, :], dst_rows[:, j, :], base[:, j:j + 1], None,
                                    ALU.subtract).then_inc(rows_ready, 1)
                for n in range(8):
                    v.wait_ge(summed, n + 2)
                    out = (g.src_s, g.place_s)[n % 2][:].rearrange("p (s j) -> p s j", j=4)[:, :, n // 2]
                    v.tensor_copy(out, tp[n % 2][0:P, 0:PS]).then_inc(turned, 1)
                v.wait_ge(node_in, 16 * T)
                for t in range(T):
                    q.then(v.tensor_scalar(junk[0:P, 0:P], chunk_dst[:, t, :], node[:, t:t + 1], None, ALU.is_lt, ALU.add, accum_out=less[:, t:t + 1]))
                    q.then(v.tensor_scalar(junk[0:P, 0:P], chunk_dst[:, t, :], node[:, t:t + 1], None, ALU.is_equal, ALU.add, accum_out=same[:, t:t + 1]))
                q.mark(v.tensor_scalar(same[:], same[:], 1.0, None, ALU.min))
                q.mark(v.tensor_scalar(node[:], node[:], float(E), None, ALU.add))
                q.then(v.scalar_tensor_tensor(less[:], less[:], float(C), chunk_f[:], ALU.mult, ALU.add))
                q.then(v.tensor_tensor(less[:], less[:], node[:], ALU.subtract))
                q.then(v.tensor_tensor(less[:], less[:], same[:], ALU.mult))
                q.then(v.tensor_tensor(less[:], less[:], node[:], ALU.add))
                q.then(v.tensor_copy(g.first_row[:], less[:]))
                v.wait_ge(win_in, 16 * RUNS)
                q.then(v.tensor_copy(win[:], win_i[:]))
                q.then(v.tensor_tensor(g.border[:], win[:, 1:RUN + 2], win[:, 0:RUN + 1], ALU.not_equal))
                q.then(v.tensor_reduce(g.has_border[:], g.border[:, 0:RUN], AX.X, ALU.max))
                q.then(v.tensor_reduce(g.has_border_back[:], g.border[:, 1:RUN + 1], AX.X, ALU.max))



def norm_stats(nc, g, name, values=None):
    with Stage(nc, g, name) as st:
        raw = st.sb("raw", [P, T * 6])
        gap = st.sb("gap", [P, T])
        var = st.sb("var", [P, T])
        sd = st.sb("sd", [P, T])
        eps = st.sb("eps", [P, 1])
        dv, var_ready, sd_ready = st.sem("dv"), st.sem("var_ready"), st.sem("sd_ready")
        x = g.x if values is None else values
        r = raw[:].rearrange("p (t s) -> p s t", s=6)
        with st.block() as block:
            @block.vector
            def _(v):
                q = Steps(v, dv)
                q.mark(v.memset(eps[:], EPS))
                with q.loop(T, 1) as t:
                    q.mark(v.bn_stats(raw[:, at(t, 6)], x[:, bass.ds(t, 1), 0:D].rearrange("p t d -> p (t d)")))
                q.wait()
                q.then(v.tensor_tensor(g.mean[:], r[:, 1, :], r[:, 4, :], ALU.add))
                q.then(v.tensor_tensor(gap[:], r[:, 1, :], r[:, 4, :], ALU.subtract))
                q.then(v.tensor_scalar(g.mean[:], g.mean[:], 0.5, None, ALU.mult))
                q.then(v.tensor_tensor(var[:], r[:, 2, :], r[:, 5, :], ALU.add))
                q.then(v.tensor_scalar(var[:], var[:], 1.0 / D, None, ALU.mult))
                q.then(v.scalar_tensor_tensor(gap[:], gap[:], 0.25, gap[:], ALU.mult, ALU.mult))
                v.tensor_tensor(var[:], var[:], gap[:], ALU.add).then_inc(var_ready, 1)
                v.wait_ge(sd_ready, 1)
                q.then(v.reciprocal(g.rstd[:], sd[:]))

            @block.scalar
            def _(act):
                act.wait_ge(var_ready, 1)
                act.activation(sd[:], var[:], ACT.Sqrt, bias=eps[:]).then_inc(sd_ready, 1)



def sum_rows(nc, g, name, table, acc):
    with Stage(nc, g, name) as st:
        idx = st.sb("idx", [P, SLOTS], U32)
        rows = st.sb("rows", [P, SLOTS, D])
        hot = st.sb("hot", [P, BANKS, P])
        part = [st.ps(f"part{j}", [P, 512]) for j in range(BANKS)]
        idx_ready, idx_taken, hot_ready, summed, added = (st.sem(n) for n in ("idx_ready", "idx_taken", "hot_ready", "summed", "added"))
        rows_in, before = st.gathers(SLOTS, [-(-(S - j) // SLOTS) for j in range(SLOTS)])
        accf = acc[:].rearrange("p t d -> p (t d)")
        with st.block() as block:
            @block.scalar
            def _(act):
                def quad(s, q):
                    for j in range(q * QUAD, q * QUAD + QUAD):
                        act.wait_ge(rows_in[j], s + before[j])
                    act.activation(idx[:, at(q, QUAD)], g.src_s[:, bass.ds(s + q * QUAD, QUAD)], ACT.Copy).then_inc(idx_ready, 1)

                for_quads(act, quad)

            @block.gpsimd
            def _(pool):
                def quad(s, q):
                    pool.wait_ge(summed, s + (q * QUAD + QUAD))
                    pool.wait_ge(idx_ready, s // QUAD + (q + 1))
                    pool.sem_inc(idx_taken, 1)
                    for j in range(q * QUAD, q * QUAD + QUAD):
                        pool.indirect_dma_start(out=rows[:, j, :], out_offset=None, in_=table,
                                                in_offset=bass.IndirectOffsetOnAxis(ap=idx[:, j:j + 1], axis=0),
                                                ).then_inc(rows_in[j], 16)

                pool.sem_inc(summed, SLOTS)
                for_quads(pool, quad)

            @block.vector
            def _(v):
                def step(s, j):
                    v.tensor_scalar(hot[:, j % BANKS, :], g.iota[0:P, 0:P], g.place_s[:, bass.ds(s + j, 1)], None,
                                    ALU.is_equal).then_inc(hot_ready, 1)

                def add(s, j, t):
                    v.wait_ge(summed, s + (j + 1 + SLOTS))
                    v.wait_ge(added, s + (j + BANKS))
                    tile = accf[:, at(t, D)]
                    v.tensor_tensor(tile, tile, part[j % BANKS][:, 0:D], ALU.add).then_inc(added, 1)

                v.sem_inc(added, BANKS)
                for_quads_ahead(v, lambda s, n: load_steps(nc, ENGINE.DVE, g.tile_of, s, n, T - 1), step, add)

            @block.tensor
            def _(pe):
                def quad(s, q):
                    for j in range(q * QUAD, q * QUAD + QUAD):
                        pe.wait_ge(hot_ready, s + (j + 1))
                        pe.wait_ge(added, s + (j + 1))
                        pe.wait_ge(rows_in[j], s + (before[j] + 16))
                        pe.matmul(part[j % BANKS][:, 0:D], hot[:, j % BANKS, :], rows[:, j, :], start=True, stop=True).then_inc(summed, 1)

                for_quads(pe, quad)



def gin(nc, g, A):
    L, EMB = A["L2_gnn_W1"].shape[0], A["L2_gnn_W1"].shape[2]
    F1 = EMB // 128
    norm_stats(nc, g, "gin_norm")
    with Stage(nc, g, "gin") as st0:
        acc = st0.sb("acc", [P, T, D])
        table = st0.dram("table", (N, D))
        with Stage(nc, g, "gin_in") as st:
            normed, dv, table_out = st.sem("normed"), st.sem("dv"), st.sem("table_out")
            with st.block() as block:
                @block.vector
                def _(v):
                    x, flat = (a[:].rearrange("p t d -> p (t d)") for a in (g.x, acc))
                    with v.Fori(0, T) as t:
                        v.tensor_scalar(flat[:, at(t, D)], x[:, at(t, D)], g.mean[:, bass.ds(t, 1)], g.rstd[:, bass.ds(t, 1)],
                                        ALU.subtract, ALU.mult).then_inc(normed, 1)

                @block.sync
                def _(sp):
                    with sp.Fori(0, T) as t:
                        sp.wait_ge(normed, t + 1)
                        sp.dma_start(table.rearrange("(t p) d -> p t d", p=P)[:, bass.ds(t, 1), :], acc[:, bass.ds(t, 1), :],
                                     ).then_inc(table_out, 16)
                    sp.wait_ge(table_out, 16 * T)
        for layer in range(L):
            sum_rows(nc, g, f"gin_sum{layer}", table, acc)
            gin_mlp(nc, g, A, layer, L, F1, acc, table)


PARTS = ((0, 3), (3, 2))
W = 3 * P
UNITS = T // GRP * len(PARTS)


def nodes(i, h, offset=0):
    t0, n = PARTS[h]
    return bass.ds(i * (GRP * P) + (t0 * P + offset), n * P)


def gin_mlp(nc, g, A, layer, L, F1, acc, table):
    with Stage(nc, g, f"gin_mlp{layer}") as st:
        z1 = st.sb("z1", [128, F1, N])
        z2 = st.sb("z2", [128, KD, N])
        cols = st.sb("cols", [128, 3, F1 + KD])
        scale = st.sb("scale", [128, F1 + KD])
        shift = st.sb("shift", [128, F1 + KD])
        bias, gamma, beta = (cols[:, n, :] for n in range(3))
        gin_up(nc, g, A, layer, F1, acc, z1, cols, scale, shift)
        gin_down(nc, g, A, layer, F1, z1, z2, bias, gamma, beta, scale, shift)
        gin_back(nc, g, layer == L - 1, layer, F1, z2, scale, shift, acc, table)


def norm_affine(v, q, stat, mv, sd, scale, shift, gamma, beta, var_ready, sd_ready):
    n = mv.shape[1]
    for f in range(n):
        q.mark(v.bn_aggr(mv[:, f, :], stat[:, f, :]))
    q.wait()
    v.tensor_copy(sd[:], mv[:, :, 1]).then_inc(var_ready, 1)
    v.wait_ge(sd_ready, 1)
    q.then(v.reciprocal(scale, sd[:]))
    q.then(v.tensor_tensor(scale, scale, gamma, ALU.mult))
    q.then(v.tensor_tensor(shift, mv[:, :, 0], scale, ALU.mult))
    q.then(v.tensor_tensor(shift, beta, shift, ALU.subtract))


def gin_up(nc, g, A, layer, F1, acc, z1, cols, scale, shift):
    with Stage(nc, g, f"gin_up{layer}") as st:
        w1 = st.sb("w1", [128, KD, F1 * 128])
        eps = st.sb("eps", [128, 1])
        tile = st.sb("tile", [P, GRP, D])
        turn = st.sb("turn", [128, 2, KD, W])
        stat = st.sb("stat", [128, F1, UNITS * 6])
        mv = st.sb("mv", [128, F1, 2])
        sd = st.sb("sd", [128, F1])
        tp = [[st.ps(f"tp{h}{k}", [128, 512]) for k in range(KD)] for h in range(2)]
        zp = [st.ps(f"zp{f}", [128, 512]) for f in range(F1)]
        w_in, tiles, turned, turn_ready, z_done, z_out = (st.sem(n) for n in ("w_in", "tiles", "turned", "turn_ready", "z_done", "z_out"))
        stats, dv, var_ready, sd_ready = (st.sem(n) for n in ("stats", "dv", "var_ready", "sd_ready"))
        accf, z1f, statf = acc[:].rearrange("p t d -> p (t d)"), z1[:].rearrange("p f n -> p (f n)"), stat[:].rearrange("p f c -> p (f c)")
        with st.block() as block:
            @block.sync
            def _(sp):
                for k in range(KD):
                    sp.dma_start(w1[:, k, :], A["L2_gnn_W1"][layer, k * 128:(k + 1) * 128, :]).then_inc(w_in, 16)
                sp.dma_start(cols[:], A["L2_gnn_cols"][layer]).then_inc(w_in, 16)

            @block.vector
            def _(v):
                q = Steps(v, dv)
                q.then(v.memset(eps[:], EPS))
                with v.Fori(0, T // GRP) as i:
                    for h, (t0, n) in enumerate(PARTS):
                        v.wait_ge(turned, i * 2 + h + 1)
                        for j in range(t0, t0 + n):
                            v.tensor_copy(tile[:, j, :], accf[:, at(i * GRP + j, D)]).then_inc(tiles, 1)
                    for h, (t0, n) in enumerate(PARTS):
                        for f in range(F1):
                            v.wait_ge(z_out, (i * 2 + h) * F1 + f + 1 + F1)
                            v.bn_stats(statf[:, bass.ds(i * 12 + (h * 6 + f * UNITS * 6), 6)], z1f[:, nodes(i, h, f * N)]).then_inc(stats, 1)
                v.wait_ge(stats, UNITS * F1)
                v.wait_ge(w_in, 16 * (KD + 1))
                norm_affine(v, q, stat, mv, sd, scale[:, 0:F1], shift[:, 0:F1], cols[:, 1, 0:F1], cols[:, 2, 0:F1], var_ready, sd_ready)

            @block.tensor
            def _(pe):
                pe.sem_inc(turned, 2)
                pe.wait_ge(w_in, 16 * (KD + 1))
                with pe.Fori(0, T // GRP) as i:
                    for h, (t0, n) in enumerate(PARTS):
                        pe.wait_ge(tiles, i * GRP + t0 + n)
                        pe.wait_ge(turn_ready, i * 4 + 2 * h)
                        for k in range(KD):
                            for j in range(n):
                                mm = pe.transpose(tp[h][k][:, j * P:(j + 1) * P], tile[:, t0 + j, k * 128:(k + 1) * 128], g.ident[0:P, 0:P])
                        mm.then_inc(turned, 1)
                    for h, (t0, n) in enumerate(PARTS):
                        pe.wait_ge(turn_ready, i * 4 + 2 * h + 2)
                        for f in range(F1):
                            pe.wait_ge(z_out, (i * 2 + h) * F1 + f + 1)
                            for k in range(KD):
                                mm = pe.matmul(zp[f][:, 0:n * P], w1[:, k, f * 128:(f + 1) * 128], turn[:, h, k, 0:n * P],
                                               start=(k == 0), stop=(k == KD - 1))
                            mm.then_inc(z_done, 1)

            @block.scalar
            def _(act):
                act.sem_inc(z_out, F1)
                act.wait_ge(w_in, 16 * (KD + 1))
                with act.Fori(0, T // GRP) as i:
                    for h, (t0, n) in enumerate(PARTS):
                        act.wait_ge(turned, i * 2 + h + 1 + 2)
                        act.wait_ge(z_done, i * (2 * F1))
                        for k in range(KD):
                            act.activation(turn[:, h, k, 0:n * P], tp[h][k][:, 0:n * P], ACT.Copy).then_inc(turn_ready, 1)
                    for h, (t0, n) in enumerate(PARTS):
                        for f in range(F1):
                            act.wait_ge(z_done, (i * 2 + h) * F1 + f + 1)
                            act.activation(z1f[:, nodes(i, h, f * N)], zp[f][:, 0:n * P], ACT.Identity,
                                           bias=cols[:, 0, f:f + 1]).then_inc(z_out, 1)
                act.wait_ge(var_ready, 1)
                act.activation(sd[:], sd[:], ACT.Sqrt, bias=eps[:]).then_inc(sd_ready, 1)


def gin_down(nc, g, A, layer, F1, z1, z2, bias, gamma, beta, scale, shift):
    with Stage(nc, g, f"gin_down{layer}") as st:
        w2 = st.sb("w2", [128, F1, D])
        eps = st.sb("eps", [128, 1])
        hid = st.sb("hid", [128, 2, F1, W])
        stat = st.sb("stat", [128, KD, UNITS * 6])
        mv = st.sb("mv", [128, KD, 2])
        sd = st.sb("sd", [128, KD])
        zp = [[st.ps(f"zp{h}{d}", [128, 512]) for d in range(KD)] for h in range(2)]
        w_in, hid_ready, z_done, z_out = (st.sem(n) for n in ("w_in", "hid_ready", "z_done", "z_out"))
        stats, dv, var_ready, sd_ready = (st.sem(n) for n in ("stats", "dv", "var_ready", "sd_ready"))
        z1f, z2f, statf = z1[:].rearrange("p f n -> p (f n)"), z2[:].rearrange("p f n -> p (f n)"), stat[:].rearrange("p f c -> p (f c)")
        with st.block() as block:
            @block.sync
            def _(sp):
                for f in range(F1):
                    sp.dma_start(w2[:, f, :], A["L2_gnn_W2"][layer, f * 128:(f + 1) * 128, :]).then_inc(w_in, 16)

            @block.scalar
            def _(act):
                with act.Fori(0, T // GRP) as i:
                    for h, (t0, n) in enumerate(PARTS):
                        act.wait_ge(z_done, i * (2 * KD) + h * KD)
                        for f in range(F1):
                            act.activation(hid[:, h, f, 0:n * P], z1f[:, nodes(i, h, f * N)], ACT.Relu,
                                           scale=scale[:, f:f + 1], bias=shift[:, f:f + 1]).then_inc(hid_ready, 1)
                act.wait_ge(var_ready, 1)
                act.activation(sd[:], sd[:], ACT.Sqrt, bias=eps[:]).then_inc(sd_ready, 1)

            @block.tensor
            def _(pe):
                pe.wait_ge(w_in, 16 * F1)
                with pe.Fori(0, T // GRP) as i:
                    for h, (t0, n) in enumerate(PARTS):
                        for d in range(KD):
                            pe.wait_ge(z_out, i * (2 * KD) + h * KD + d)
                            for f in range(F1):
                                pe.wait_ge(hid_ready, (i * 2 + h) * F1 + f + 1)
                                mm = pe.matmul(zp[h][d][:, 0:n * P], w2[:, f, d * 128:(d + 1) * 128], hid[:, h, f, 0:n * P],
                                               start=(f == 0), stop=(f == F1 - 1))
                            mm.then_inc(z_done, 1)

            @block.vector
            def _(v):
                q = Steps(v, dv)
                q.then(v.memset(eps[:], EPS))
                with v.Fori(0, T // GRP) as i:
                    for h, (t0, n) in enumerate(PARTS):
                        for d in range(KD):
                            v.wait_ge(z_done, (i * 2 + h) * KD + d + 1)
                            v.tensor_scalar(z2f[:, nodes(i, h, d * N)], zp[h][d][:, 0:n * P], bias[:, F1 + d:F1 + d + 1], None,
                                            ALU.add).then_inc(z_out, 1)
                            v.wait_ge(z_out, (i * 2 + h) * KD + d + 1)
                            v.bn_stats(statf[:, bass.ds(i * 12 + (h * 6 + d * UNITS * 6), 6)], z2f[:, nodes(i, h, d * N)]).then_inc(stats, 1)
                v.wait_ge(stats, UNITS * KD)
                norm_affine(v, q, stat, mv, sd, scale[:, F1:], shift[:, F1:], gamma[:, F1:], beta[:, F1:], var_ready, sd_ready)


def gin_back(nc, g, last, layer, F1, z2, scale, shift, acc, table):
    with Stage(nc, g, f"gin_back{layer}") as st:
        hid = st.sb("hid", [128, GRP, KD, P])
        tp = [st.ps(f"tp{j}", [P, 512]) for j in range(GRP)]
        hid_ready, turned, put, table_out = (st.sem(n) for n in ("hid_ready", "turned", "put", "table_out"))
        z2f = z2[:].rearrange("p f n -> p (f n)")
        with st.block() as block:
            @block.scalar
            def _(act):
                with act.Fori(0, T // GRP) as i:
                    for j in range(GRP):
                        act.wait_ge(turned, i * GRP)
                        for d in range(KD):
                            act.activation(hid[:, j, d, :], z2f[:, bass.ds(i * (GRP * P) + (j * P + d * N), P)], ACT.Identity if last else ACT.Relu,
                                           scale=scale[:, F1 + d:F1 + d + 1], bias=shift[:, F1 + d:F1 + d + 1]).then_inc(hid_ready, 1)

            @block.tensor
            def _(pe):
                with pe.Fori(0, T // GRP) as i:
                    for j in range(GRP):
                        pe.wait_ge(put, i * GRP)
                        pe.wait_ge(hid_ready, (i * GRP + j) * KD + KD)
                        for d in range(KD):
                            mm = pe.transpose(tp[j][:, d * 128:(d + 1) * 128], hid[:, j, d, :], g.ident[:])
                        mm.then_inc(turned, 1)

            @block.vector
            def _(v):
                to = (g.x if last else acc)[:].rearrange("p t d -> p (t d)")
                with v.Fori(0, T // GRP) as i:
                    for j in range(GRP):
                        v.wait_ge(turned, i * GRP + j + 1)
                        tile = to[:, at(i * GRP + j, D)]
                        if last:
                            v.tensor_tensor(tile, tile, tp[j][:, 0:D], ALU.add).then_inc(put, 1)
                        else:
                            v.tensor_copy(tile, tp[j][:, 0:D]).then_inc(put, 1)

            @block.sync
            def _(sp):
                if not last:
                    with sp.Fori(0, T) as t:
                        sp.wait_ge(put, t + 1)
                        sp.dma_start(table.rearrange("(t p) d -> p t d", p=P)[:, bass.ds(t, 1), :], acc[:, bass.ds(t, 1), :],
                                     ).then_inc(table_out, 16)
                    sp.wait_ge(table_out, 16 * T)



def store_tables(sp, done, tables):
    for table, values in tables:
        sp.dma_start(table.rearrange("(t p) d -> p t d", p=P), values).then_inc(done, 16)


def edge_dst(nc, g, name, values, filled):
    with Stage(nc, g, name) as st0:
        gate = st0.sb("gate", [128, RUN + 1])
        with Stage(nc, g, f"{name}_put") as st:
            firsts = st.sb("firsts", [P, C, H])
            block_in = st.sb("block_in", [P, 4, RUNS * H])
            tp = [st.ps(f"tp{j}", [128, 512]) for j in range(4)]
            firsts_in, block_ready, turned, put, gated = (st.sem(n) for n in ("firsts_in", "block_ready", "turned", "put", "gated"))
            (scattered,), (before,) = st.gathers(1, T)
            by_run = firsts[:].rearrange("p (r c) h -> p c r h", r=RUNS)
            with st.block() as block:
                @block.gpsimd
                def _(pool):
                    for t in range(T):
                        pool.indirect_dma_start(out=g.first_rows, out_offset=bass.IndirectOffsetOnAxis(ap=g.first_row[:, t:t + 1], axis=0),
                                                in_=values[:, t, :], in_offset=None).then_inc(scattered, 16)

                @block.sync
                def _(sp):
                    sp.wait_ge(scattered, before + 16 * T)
                    sp.dma_start(firsts[:], g.first_rows[0:E, :].rearrange("(p c) h -> p c h", p=P)).then_inc(firsts_in, 16)

                @block.scalar
                def _(act):
                    act.wait_ge(firsts_in, 16)
                    for c in range(RC):
                        if c >= 4:
                            act.wait_ge(turned, c - 3)
                        act.activation(block_in[:, c % 4, :].rearrange("p (r h) -> p r h", h=H), by_run[:, c, :, :], ACT.Copy).then_inc(block_ready, 1)

                @block.tensor
                def _(pe):
                    for c in range(RC):
                        pe.wait_ge(block_ready, c + 1)
                        if c >= 4:
                            pe.wait_ge(put, c - 3)
                        pe.transpose(tp[c % 4][:, 0:P], block_in[:, c % 4, :], g.ident[0:P, 0:P]).then_inc(turned, 1)

                @block.vector
                def _(v):
                    v.tensor_scalar(gate[:], g.border[:], -1.0, 1.0, ALU.mult, ALU.add).then_inc(gated, 1)
                    for c in range(RC):
                        v.wait_ge(turned, c + 1)
                        v.tensor_copy(filled[:, c * P:(c + 1) * P], tp[c % 4][:, 0:P]).then_inc(put, 1)
                    v.wait_ge(gated, 1)
                    v.wait_ge(put, RC)
        segment_scans(nc, g, f"{name}_fill", filled, gate, "add", filled, None)


def edge_logits(nc, g, name, src_table, dst_part, logit, edge=None):
    with Stage(nc, g, name) as st:
        idx = st.sb("idx", [P, GRP, RUNS], U32)
        of_src = st.sb("of_src", [P, GRP, 128])
        both = st.sb("both", [P, GRP, 128])
        tp = [st.ps(f"tp{j}", [128, 512]) for j in range(2)]
        idx_ready, idx_taken, added, turned, put = (st.sem(n) for n in ("idx_ready", "idx_taken", "added", "turned", "put"))
        rows_in, before = st.gathers(GRP, T // GRP * RUNS)
        ALL = RUNS * 16
        src_v = g.src_e[:].rearrange("p (r c) -> p c r", r=RUNS)
        SUB, PLACES = 4, 4
        LOADS = RUNS // SUB
        if edge is not None:
            feats, proj = edge
            ef = st.sb("ef", [P, PLACES, SUB, D])
            ef_t = st.sb("ef_t", [128, 2, 4 * P])
            ep = [st.ps(f"ep{j}", [128, 512]) for j in range(2)]
            own = [st.ps(f"own{j}", [P, 512]) for j in range(2)]
            ef_in = st.sems("ef_in", PLACES)
            ef_turned, ef_t_ready, projected = (st.sem(n) for n in ("ef_turned", "ef_t_ready", "projected"))
            ef_v = feats.rearrange("(r c p) d -> p c r d", r=RUNS, c=RC)
        PAIRS = RUNS // 2

        with st.block() as block:
            @block.scalar
            def _(act):
                with act.Fori(0, T // GRP) as i:
                    for j in range(GRP):
                        act.wait_ge(rows_in[j], i * ALL + before[j])
                        act.activation(idx[:, j:j + 1, :], src_v[:, bass.ds(i * GRP + j, 1), :], ACT.Copy).then_inc(idx_ready, 1)
                    if edge is not None:
                        for u in range(GRP * PAIRS):
                            act.wait_ge(ef_turned, i * (GRP * PAIRS) + u + 1 + 2 * PLACES)
                            act.wait_ge(projected, i * (GRP * PAIRS) + u + 1)
                            act.activation(ef_t[:, u % 2, 0:4 * P], ep[u % 2][:, 0:4 * P], ACT.Copy).then_inc(ef_t_ready, 1)

            @block.gpsimd
            def _(pool):
                pool.sem_inc(added, GRP)
                with pool.Fori(0, T // GRP) as i:
                    for j in range(GRP):
                        pool.wait_ge(added, i * GRP + j + 1)
                        pool.wait_ge(idx_ready, i * GRP + j + 1)
                        pool.sem_inc(idx_taken, 1)
                        for r in range(RUNS):
                            pool.indirect_dma_start(out=of_src[:, j, r * H:(r + 1) * H], out_offset=None, in_=src_table,
                                                    in_offset=bass.IndirectOffsetOnAxis(ap=idx[:, j, r:r + 1], axis=0),
                                                    ).then_inc(rows_in[j], 16)

            @block.vector
            def _(v):
                with v.Fori(0, T // GRP) as i:
                    for j in range(GRP):
                        v.wait_ge(rows_in[j], i * ALL + (before[j] + ALL))
                        v.wait_ge(turned, i * GRP + j)
                        if edge is None:
                            v.tensor_copy(both[:, j, :], of_src[:, j, :]).then_inc(added, 1)
                        else:
                            v.wait_ge(projected, i * (GRP * PAIRS) + ((j + 1) * PAIRS + 2))
                            v.tensor_tensor(both[:, j, :], of_src[:, j, :], own[j % 2][:, 0:128], ALU.add).then_inc(added, 1)
                        v.wait_ge(turned, i * GRP + j + 1)
                        v.tensor_tensor(logit[:, at(i * GRP + j, P)], dst_part[:, at(i * GRP + j, P)], tp[j % 2][:, 0:P], ALU.add).then_inc(put, 1)

            @block.tensor
            def _(pe):
                if edge is not None:
                    pe.sem_inc(projected, 2)
                    pe.sem_inc(ef_turned, 2 * PLACES)
                with pe.Fori(0, T // GRP) as i:
                    for j in range(GRP):
                        if edge is not None:
                            for m in range(PAIRS):
                                u = j * PAIRS + m
                                s = u // 2
                                if m % 2 == 0:
                                    pe.wait_ge(ef_in[s % PLACES], i * (16 * GRP * LOADS // PLACES) + (16 * (s // PLACES) + 16))
                                for a in range(2):
                                    for k in range(KD):
                                        mm = pe.transpose(ep[u % 2][:, (a * KD + k) * P:(a * KD + k + 1) * P],
                                                          ef[:, s % PLACES, m % 2 * 2 + a, k * 128:(k + 1) * 128], g.ident[0:P, 0:P])
                                mm.then_inc(ef_turned, 1)
                                if m == 0:
                                    pe.wait_ge(added, i * GRP + (j + GRP))
                                pe.wait_ge(ef_t_ready, i * (GRP * PAIRS) + u + 1)
                                for a in range(2):
                                    for k in range(KD):
                                        mm = pe.matmul(own[j % 2][:, (2 * m + a) * H:(2 * m + a + 1) * H],
                                                       ef_t[:, u % 2, (a * KD + k) * P:(a * KD + k + 1) * P], proj[:, k, :],
                                                       start=(k == 0), stop=(k == KD - 1))
                                mm.then_inc(projected, 1)
                        pe.wait_ge(added, i * GRP + (j + 1 + GRP))
                        pe.transpose(tp[j % 2][:, 0:P], both[:, j, :], g.ident[0:P, 0:P]).then_inc(turned, 1)

            if edge is not None:
                @block.sync
                def _(sp):
                    with sp.Fori(0, T // GRP) as i:
                        for s in range(GRP * LOADS):
                            sp.wait_ge(ef_turned, i * (GRP * PAIRS) + 2 * s + 2)
                            sp.dma_start(ef[:, s % PLACES, :, :],
                                         ef_v[:, bass.ds(i * GRP + s // LOADS, 1), s % LOADS * SUB:(s % LOADS + 1) * SUB, :]
                                         .rearrange("p c r d -> p (c r) d")).then_inc(ef_in[s % PLACES], 16)


def segment_scans(nc, g, name, values, gate, op, out_f, out_b):
    inner, outer, empty = (ALU.add, ALU.max, -BIG) if op == "max" else (ALU.mult, ALU.add, 0.0)
    with Stage(nc, g, name) as st:
        gates = st.sb("gates", [128, 2])
        rows = st.sb("rows", [1, 4, 128])
        carry = st.sb("carry", [1, 2, 128])
        col = st.sb("col", [128, 2])
        rp = st.ps("rp", [1, 512])
        cp = st.ps("cp", [128, 512])
        dv, ends, turned, carried, spread_out = (st.sem(n) for n in ("dv", "ends", "turned", "carried", "spread_out"))
        first = st.sb("first", [128, RUN]) if out_b is None else None
        ways = [(out_f[:], gate[:, 0:RUN], values[:])]
        ends_at = [out_f[:, RUN - 1:RUN]]
        if out_b is None:
            ends_at = [first[:, RUN - 1:RUN]]
        else:
            ways.append((out_b[:, ::-1], gate[:, RUN:0:-1], values[:, ::-1]))
            ends_at.append(out_b[:, 0:1])
        n_ways = len(ways)
        with st.block() as block:
            @block.vector
            def _(v):
                q = Steps(v, dv)
                for n, has in enumerate((g.has_border, g.has_border_back)):
                    if op == "max":
                        q.mark(v.tensor_scalar(gates[:, n:n + 1], has[:], -BIG, None, ALU.mult))
                    else:
                        q.mark(v.tensor_scalar(gates[:, n:n + 1], has[:], -1.0, 1.0, ALU.mult, ALU.add))
                q.mark(v.memset(carry[:], empty))
                for out, between, x in ways:
                    q.mark(v.tensor_tensor_scan(out if first is None else first[:], between, x, empty, inner, outer))
                q.wait()
                v.sem_inc(ends, 1)
                v.wait_ge(turned, 2 * n_ways)
                q.then(v.tensor_copy(rows[:, 0:2 * n_ways, :].rearrange("p a n -> p (a n)"), rp[:, 0:2 * n_ways * 128]))
                runs = [rows[0:1, n, :].rearrange("p (r h) -> p h r", h=H) for n in range(2 * n_ways)]
                into = [carry[0:1, n, :].rearrange("p (r h) -> p h r", h=H) for n in range(2)]
                for h in range(H):
                    q.mark(v.tensor_tensor_scan(into[0][:, h, 1:RUNS], runs[1][:, h, 0:RUNS - 1], runs[0][:, h, 0:RUNS - 1],
                                                empty, inner, outer))
                    if n_ways == 2:
                        q.mark(v.tensor_tensor_scan(into[1][:, h, RUNS - 2::-1], runs[3][:, h, RUNS - 1:0:-1], runs[2][:, h, RUNS - 1:0:-1],
                                                    empty, inner, outer))
                q.wait()
                v.sem_inc(carried, 1)
                v.wait_ge(spread_out, n_ways)
                q.then(v.tensor_copy(col[:, 0:n_ways], cp[:, 0:n_ways]))
                for n, (out, between, x) in enumerate(ways):
                    q.mark(v.tensor_tensor_scan(out, between, x, col[:, n:n + 1], inner, outer))
                q.wait()

            @block.tensor
            def _(pe):
                pe.wait_ge(ends, 1)
                for n, end in enumerate(ends_at):
                    for m, c in enumerate((end, gates[:, n:n + 1])):
                        pe.transpose(rp[0:1, (2 * n + m) * 128:(2 * n + m + 1) * 128], c, g.ident[:]).then_inc(turned, 1)
                pe.wait_ge(carried, 1)
                for n in range(n_ways):
                    pe.matmul(cp[:, n:n + 1], carry[0:1, n, :], g.ones[0:1, :], start=True, stop=True).then_inc(spread_out, 1)


def edge_weights(nc, g, name, logit, weight, slope=None, mean=None, top=False):
    with Stage(nc, g, name) as st0:
        gate = st0.sb("gate", [128, RUN + 1])
        fwd = st0.sb("fwd", [128, RUN])
        bwd = st0.sb("bwd", [128, RUN])

        def step(tag, body):
            with Stage(nc, g, f"{name}_{tag}") as st:
                dv, before_exp, exps = st.sem("dv"), st.sem("before_exp"), st.sem("exps")
                with st.block() as block:
                    @block.vector
                    def _(v):
                        q = Steps(v, dv)
                        body(v, q)
                        v.sem_inc(before_exp, 1)

                    if tag == "exp":
                        @block.scalar
                        def _(act):
                            act.wait_ge(before_exp, 1)
                            act.activation(logit[:], logit[:], ACT.Exp).then_inc(exps, 1)

        def first(v, q):
            q.mark(v.tensor_scalar(gate[:], g.border[:], -BIG, None, ALU.mult))
            if slope is not None:
                q.mark(v.scalar_tensor_tensor(logit[:], logit[:], slope, logit[:], ALU.mult, ALU.max))
            q.wait()

        def second(v, q):
            q.then(v.tensor_tensor(fwd[:], fwd[:], bwd[:], ALU.max))
            q.mark(v.tensor_tensor(logit[:], logit[:], fwd[:], ALU.subtract))
            if top:
                q.mark(v.tensor_tensor(bwd[:], fwd[:], g.border[:, 1:RUN + 1], ALU.mult))
            q.wait()

        def third(v, q):
            q.then(v.tensor_scalar(gate[:], g.border[:], -1.0, 1.0, ALU.mult, ALU.add))

        def fourth(v, q):
            q.then(v.tensor_tensor(fwd[:], fwd[:], bwd[:], ALU.add))
            q.then(v.tensor_tensor(fwd[:], fwd[:], logit[:], ALU.subtract))
            q.then(v.reciprocal(fwd[:], fwd[:]))
            q.then(v.tensor_tensor(logit[:], logit[:], fwd[:], ALU.mult))

        step("leaky", first)
        segment_scans(nc, g, f"{name}_max", logit, gate, "max", fwd, bwd)
        step("exp", second)
        if mean is not None:
            step("gates", third)
            segment_scans(nc, g, f"{name}_sum", logit, gate, "add", fwd, bwd)
            step("divide", fourth)
        with Stage(nc, g, f"{name}_turn") as st:
            tp = [st.ps(f"tp{j}", [P, 512]) for j in range(4)]
            turned, put, dv = st.sem("turned"), st.sem("put"), st.sem("dv")
            blocks = [(x, n, c) for c in range(RC) for n, x in enumerate((logit, bwd) if top else (logit,))]
            wv = weight[:].rearrange("p (r c) w -> p c r w", r=RUNS)
            with st.block() as block:
                @block.tensor
                def _(pe):
                    for m, (x, n, c) in enumerate(blocks):
                        if m >= 4:
                            pe.wait_ge(put, m - 3)
                        pe.transpose(tp[m % 4][:, 0:128], x[:, c * P:(c + 1) * P], g.ident[:]).then_inc(turned, 1)

                @block.vector
                def _(v):
                    for m, (x, n, c) in enumerate(blocks):
                        v.wait_ge(turned, m + 1)
                        v.tensor_copy(wv[:, c, :, n * H:(n + 1) * H], tp[m % 4][:, 0:128].rearrange("p (r h) -> p r h", h=H)).then_inc(put, 1)
                    if mean is not None:
                        v.wait_ge(put, len(blocks))
                        q = Steps(v, dv)
                        q.then(v.tensor_reduce(mean[:], weight[:], AX.X, ALU.add))
                        q.then(v.tensor_scalar(mean[:], mean[:], 1.0 / H, None, ALU.mult))


def sum_heads(nc, g, name, table, weight, acc):
    WH = weight.shape[2]
    with Stage(nc, g, name) as st:
        idx = st.sb("idx", [P, SLOTS], U32)
        rows = st.sb("rows", [P, SLOTS, D])
        msg = st.sb("msg", [P, BANKS, D + WH])
        hot = st.sb("hot", [P, BANKS, P])
        part = [st.ps(f"part{j}", [P, 512]) for j in range(BANKS)]
        idx_ready, idx_taken, hot_ready, weight_ready, msg_ready, summed, added = (
            st.sem(n) for n in ("idx_ready", "idx_taken", "hot_ready", "weight_ready", "msg_ready", "summed", "added"))
        rows_in, before = st.gathers(SLOTS, [-(-(S - j) // SLOTS) for j in range(SLOTS)])
        accf = acc[:].rearrange("p t w -> p (t w)")
        with st.block() as block:
            @block.scalar
            def _(act):
                def quad(s, q):
                    for j in range(q * QUAD, q * QUAD + QUAD):
                        act.wait_ge(rows_in[j], s + before[j])
                    act.activation(idx[:, at(q, QUAD)], g.src_s[:, bass.ds(s + q * QUAD, QUAD)], ACT.Copy).then_inc(idx_ready, 1)
                    for j, c in enumerate(load_steps(nc, ENGINE.Activation, g.chunk_of, s + q * QUAD, QUAD, C - 1), q * QUAD):
                        act.wait_ge(summed, s + (j + 1))
                        act.activation(msg[:, j % BANKS, D:], weight[:, bass.ds(c, 1), :].rearrange("p a w -> p (a w)"), ACT.Copy).then_inc(weight_ready, 1)

                act.sem_inc(summed, BANKS)
                for_quads(act, quad)

            @block.gpsimd
            def _(pool):
                def quad(s, q):
                    pool.wait_ge(msg_ready, s + (q * QUAD + QUAD))
                    pool.wait_ge(idx_ready, s // QUAD + (q + 1))
                    pool.sem_inc(idx_taken, 1)
                    for j in range(q * QUAD, q * QUAD + QUAD):
                        pool.indirect_dma_start(out=rows[:, j, :], out_offset=None, in_=table,
                                                in_offset=bass.IndirectOffsetOnAxis(ap=idx[:, j:j + 1], axis=0),
                                                ).then_inc(rows_in[j], 16)

                pool.sem_inc(msg_ready, SLOTS)
                for_quads(pool, quad)

            @block.vector
            def _(v):
                def step(s, j):
                    v.tensor_scalar(hot[:, j % BANKS, :], g.iota[0:P, 0:P], g.place_s[:, bass.ds(s + j, 1)], None,
                                    ALU.is_equal).then_inc(hot_ready, 1)
                    by_head = "p (h d) -> p h d"
                    v.wait_ge(weight_ready, s + (j + 1))
                    v.wait_ge(rows_in[j % SLOTS], s + (j // SLOTS * SLOTS + before[j % SLOTS] + 16))
                    v.tensor_tensor(msg[:, j % BANKS, 0:D].rearrange(by_head, h=H), rows[:, j % SLOTS, :].rearrange(by_head, h=H),
                                    msg[:, j % BANKS, D:D + H].unsqueeze(2).to_broadcast([P, H, HD]), ALU.mult).then_inc(msg_ready, 1)

                def add(s, j, t):
                    v.wait_ge(summed, s + (j + 1 + BANKS))
                    v.wait_ge(added, s + (j + BANKS))
                    tile = accf[:, at(t, D + WH)]
                    v.tensor_tensor(tile, tile, part[j % BANKS][:, 0:D + WH], ALU.add).then_inc(added, 1)

                v.sem_inc(added, BANKS)
                for_quads_ahead(v, lambda s, n: load_steps(nc, ENGINE.DVE, g.tile_of, s, n, T - 1), step, add)

            @block.tensor
            def _(pe):
                def quad(s, q):
                    for j in range(q * QUAD, q * QUAD + QUAD):
                        pe.wait_ge(hot_ready, s + (j + 1))
                        pe.wait_ge(added, s + (j + 1))
                        pe.wait_ge(msg_ready, s + (j + 1 + SLOTS))
                        pe.matmul(part[j % BANKS][:, 0:D + WH], hot[:, j % BANKS, :], msg[:, j % BANKS, :], start=True, stop=True).then_inc(summed, 1)

                for_quads(pe, quad)


def attention_in(nc, g, name, A, lin, w, att, feat, ends, table):
    with Stage(nc, g, name) as st:
        wl = st.sb("wl", [128, KD, D])
        wg = st.sb("wg", [128, KD, D])
        bl = st.sb("bl", [P, D])
        attb = st.sb("attb", [P, 2, D])
        tile = st.sb("tile", [P, GRP, D])
        h_tile = st.sb("h_tile", [P, GRP, D])
        x_t = st.sb("x_t", [128, GRP, KD, P])
        h_t = st.sb("h_t", [128, GRP, KD, P])
        prod = st.sb("prod", [P, 2, D])
        tp = [st.ps(f"tp{j}", [128, 512]) for j in range(2)]
        hp = [st.ps(f"hp{j}", [P, 512]) for j in range(2)]
        ht = [st.ps(f"ht{j}", [128, 512]) for j in range(2)]
        fp = [st.ps(f"fp{j}", [P, 512]) for j in range(2)]
        w_in, normed, x_turned, x_t_ready, h_done, h_ready, h_turned, h_t_ready, f_done, f_out, dv, out = (
            st.sem(n) for n in ("w_in", "normed", "x_turned", "x_t_ready", "h_done", "h_ready", "h_turned", "h_t_ready",
                                "f_done", "f_out", "dv", "out"))
        xf, ff = g.x[:].rearrange("p t d -> p (t d)"), feat[:].rearrange("p t d -> p (t d)")
        LOADS = 1 + (2 if lin else 0) + 2
        x_h = lin is not None
        with st.block() as block:
            @block.sync
            def _(sp):
                sp.dma_start(wg[:], w.rearrange("(k p) n -> p k n", p=128)).then_inc(w_in, 16)
                for n in range(2):
                    sp.dma_start(attb[:, n, :], spread(att[n])).then_inc(w_in, 16)
                if x_h:
                    sp.dma_start(wl[:], lin[0].rearrange("(k p) n -> p k n", p=128)).then_inc(w_in, 16)
                    sp.dma_start(bl[:], spread(lin[1])).then_inc(w_in, 16)
                with sp.Fori(0, T) as t:
                    sp.wait_ge(f_out, t + 1)
                    sp.dma_start(table.rearrange("(t p) d -> p t d", p=P)[:, bass.ds(t, 1), :], feat[:, bass.ds(t, 1), :]).then_inc(out, 16)
                sp.wait_ge(out, 16 * T)

            @block.vector
            def _(v):
                q = Steps(v, dv)
                v.wait_ge(w_in, 16 * LOADS)
                with q.loop(T // GRP, 4 * GRP + (GRP if x_h else 0)) as i:
                    for j in range(GRP):
                        v.wait_ge(x_turned, i * GRP)
                        t = i * GRP + j
                        v.tensor_scalar(tile[:, j, :], xf[:, at(t, D)], g.mean[:, bass.ds(t, 1)], g.rstd[:, bass.ds(t, 1)],
                                        ALU.subtract, ALU.mult).then_inc(normed, 1)
                    if x_h:
                        for j in range(GRP):
                            v.wait_ge(h_done, i * GRP + j + 1)
                            v.wait_ge(h_turned, i * GRP)
                            v.tensor_tensor(h_tile[:, j, :], hp[j % 2][:, 0:D], bl[:], ALU.add).then_inc(h_ready, 1)
                            v.wait_ge(h_ready, i * GRP + j + 1)
                            to = xf[:, at(i * GRP + j, D)]
                            q.mark(v.tensor_tensor(to, to, h_tile[:, j, :], ALU.add))
                    for j in range(GRP):
                        v.wait_ge(f_done, i * GRP + j + 1)
                        for n in range(2):
                            q.mark(v.tensor_tensor(prod[:, n, :], fp[j % 2][:, 0:D], attb[:, n, :], ALU.mult))
                        v.tensor_copy(ff[:, at(i * GRP + j, D)], fp[j % 2][:, 0:D]).then_inc(f_out, 1)
                        q.wait()
                        for n in range(2):
                            q.mark(v.tensor_reduce(ends[:, bass.ds(i * GRP + j, 1), n * H:(n + 1) * H].rearrange("p t h -> p (t h)"),
                                                   prod[:, n, :].rearrange("p (h d) -> p h d", h=H), AX.X, ALU.add))
                        q.wait()

            @block.tensor
            def _(pe):
                pe.wait_ge(w_in, 16 * LOADS)
                with pe.Fori(0, T // GRP) as i:
                    for j in range(GRP):
                        pe.wait_ge(normed, i * GRP + j + 1)
                        if j < 2:
                            pe.wait_ge(x_t_ready, i * GRP)
                        else:
                            pe.wait_ge(x_t_ready, i * GRP + j - 1)
                        for k in range(KD):
                            mm = pe.transpose(tp[j % 2][:, k * P:(k + 1) * P], tile[:, j, k * 128:(k + 1) * 128], g.ident[0:P, 0:P])
                        mm.then_inc(x_turned, 1)
                    if x_h:
                        for j in range(GRP):
                            pe.wait_ge(x_t_ready, i * GRP + j + 1)
                            if j < 2:
                                pe.wait_ge(h_ready, i * GRP)
                            else:
                                pe.wait_ge(h_ready, i * GRP + j - 1)
                            for k in range(KD):
                                mm = pe.matmul(hp[j % 2][:, 0:D], x_t[:, j, k, :], wl[:, k, :], start=(k == 0), stop=(k == KD - 1))
                            mm.then_inc(h_done, 1)
                        for j in range(GRP):
                            pe.wait_ge(h_ready, i * GRP + j + 1)
                            if j < 2:
                                pe.wait_ge(h_t_ready, i * GRP)
                            else:
                                pe.wait_ge(h_t_ready, i * GRP + j - 1)
                            for k in range(KD):
                                mm = pe.transpose(ht[j % 2][:, k * P:(k + 1) * P], h_tile[:, j, k * 128:(k + 1) * 128], g.ident[0:P, 0:P])
                            mm.then_inc(h_turned, 1)
                    for j in range(GRP):
                        if x_h:
                            pe.wait_ge(h_t_ready, i * GRP + j + 1)
                        else:
                            pe.wait_ge(x_t_ready, i * GRP + j + 1)
                        if j < 2:
                            pe.wait_ge(f_out, i * GRP)
                        else:
                            pe.wait_ge(f_out, i * GRP + j - 1)
                        for k in range(KD):
                            mm = pe.matmul(fp[j % 2][:, 0:D], (h_t if x_h else x_t)[:, j, k, :], wg[:, k, :], start=(k == 0), stop=(k == KD - 1))
                        mm.then_inc(f_done, 1)

            @block.scalar
            def _(act):
                with act.Fori(0, T // GRP) as i:
                    for j in range(GRP):
                        act.wait_ge(x_turned, i * GRP + j + 1)
                        act.wait_ge((h_done if x_h else f_done), i * GRP)
                        act.activation(x_t[:, j, :, :].rearrange("p k n -> p (k n)"), tp[j % 2][:, 0:KD * P], ACT.Copy).then_inc(x_t_ready, 1)
                    if x_h:
                        for j in range(GRP):
                            act.wait_ge(h_turned, i * GRP + j + 1)
                            act.wait_ge(f_done, i * GRP)
                            act.activation(h_t[:, j, :, :].rearrange("p k n -> p (k n)"), ht[j % 2][:, 0:KD * P], ACT.Copy).then_inc(h_t_ready, 1)


def store_ends(nc, g, name, tables):
    with Stage(nc, g, name) as st:
        out = st.sem("out")
        with st.block() as block:
            @block.sync
            def _(sp):
                store_tables(sp, out, tables)
                sp.wait_ge(out, 16 * len(tables))



def gat(nc, g, A):
    norm_stats(nc, g, "gat_norm")
    with Stage(nc, g, "gat") as st0:
        table, src_end = st0.dram("table", (N, D)), st0.dram("src_end", (N, H))
        dst_part = st0.sb("dst_part", [128, RUN])
        with Stage(nc, g, "gat_feat") as st:
            feat = st.sb("feat", [P, T, D])
            ends = st.sb("ends", [P, T, 2 * H])
            attention_in(nc, g, "gat_in", A, (A["L0_gnn_W_lin"], A["L0_gnn_b_lin"]), A["L0_gnn_W_gat"],
                         [a.rearrange("h d -> (h d)") for a in (A["L0_gnn_attn_l"], A["L0_gnn_attn_r"])], feat, ends, table)
            store_ends(nc, g, "gat_ends", ((src_end, ends[:, :, 0:H]),))
            edge_dst(nc, g, "gat_dst", ends[:, :, H:], dst_part)
        weight = st0.sb("weight", [P, C, H])
        with Stage(nc, g, "gat_soft") as st:
            logit = st.sb("logit", [128, RUN])
            edge_logits(nc, g, "gat_logits", src_end, dst_part, logit)
            edge_weights(nc, g, "gat_weights", logit, weight, slope=0.2)
        acc = st0.sb("acc", [P, T, D + H])
        clear(nc, g, "gat_clear", acc)
        sum_heads(nc, g, "gat_sum", table, weight, acc)
        with Stage(nc, g, "gat_out") as st:
            bias = st.sb("bias", [P, D])
            share = st.sb("share", [P, T, H])
            z = st.sb("z", [P, D])
            b_in, dv = st.sem("b_in"), st.sem("dv")
            with st.block() as block:
                @block.sync
                def _(sp):
                    sp.dma_start(bias[:], spread(A["L0_gnn_gat_bias"])).then_inc(b_in, 16)

                @block.vector
                def _(v):
                    q = Steps(v, dv)
                    v.wait_ge(b_in, 16)
                    q.then(v.tensor_scalar(share[:], acc[:, :, D:], 1e-30, None, ALU.max))
                    q.then(v.reciprocal(share[:], share[:]))
                    xf, zh = g.x[:].rearrange("p t d -> p (t d)"), z[:].rearrange("p (h d) -> p h d", h=H)
                    with q.loop(T, 4) as t:
                        q.then(v.tensor_tensor(zh, acc[:, bass.ds(t, 1), 0:D].rearrange("p t (h d) -> p (t h) d", h=H),
                                               share[:, bass.ds(t, 1), :].rearrange("p t h -> p (t h)").unsqueeze(2).to_broadcast([P, H, HD]), ALU.mult))
                        q.then(v.tensor_tensor(z[:], z[:], bias[:], ALU.add))
                        q.then(v.scalar_tensor_tensor(z[:], z[:], 0.01, z[:], ALU.mult, ALU.max))
                        q.then(v.tensor_tensor(xf[:, at(t, D)], xf[:, at(t, D)], z[:], ALU.add))


def clear(nc, g, name, acc):
    with Stage(nc, g, name) as st:
        dv = st.sem("dv")
        with st.block() as block:
            @block.vector
            def _(v):
                v.memset(acc[:], 0.0).then_inc(dv, 1)
                v.wait_ge(dv, 1)



def gat_loops(nc, g, A):
    norm_stats(nc, g, "loops_norm")
    with Stage(nc, g, "loops") as st0:
        table, src_end = st0.dram("table", (N, D)), st0.dram("src_end", (N, H))
        feat = st0.sb("feat", [P, T, D])
        ends = st0.sb("ends", [P, T, 2 * H])
        attention_in(nc, g, "loops_in", A, None, A["L3_gnn_W"],
                     [a.rearrange("h d -> (h d)") for a in (A["L3_gnn_att_src"], A["L3_gnn_att_dst"])], feat, ends, table)
        store_ends(nc, g, "loops_ends", ((src_end, ends[:, :, 0:H]),))
        weight = st0.sb("weight", [P, C, 2 * H])
        with Stage(nc, g, "loops_soft") as st:
            logit = st.sb("logit", [128, RUN])
            edge_dst(nc, g, "loops_dst", ends[:, :, H:], logit)
            edge_logits(nc, g, "loops_logits", src_end, logit, logit)
            edge_weights(nc, g, "loops_weights", logit, weight, slope=0.2, top=True)
        acc = st0.sb("acc", [P, T, D + 2 * H])
        clear(nc, g, "loops_clear", acc)
        sum_heads(nc, g, "loops_sum", table, weight, acc)
        with Stage(nc, g, "loops_join") as st:
            own, most, edge_scale, own_scale, den = (st.sb(n, [P, T, H]) for n in ("own", "most", "edge_scale", "own_scale", "den"))
            bias = st.sb("bias", [P, D])
            z = st.sb("z", [P, 2, D])
            b_in, dv, before_exp, exps = st.sem("b_in"), st.sem("dv"), st.sem("before_exp"), st.sem("exps")
            with st.block() as block:
                @block.sync
                def _(sp):
                    sp.dma_start(bias[:], spread(A["L3_gnn_bias"])).then_inc(b_in, 16)

                @block.scalar
                def _(act):
                    act.wait_ge(before_exp, 1)
                    act.activation(edge_scale[:], edge_scale[:], ACT.Exp).then_inc(exps, 1)
                    act.activation(own_scale[:], own_scale[:], ACT.Exp).then_inc(exps, 1)

                @block.vector
                def _(v):
                    q = Steps(v, dv)
                    q.then(v.tensor_tensor(own[:], ends[:, :, 0:H], ends[:, :, H:], ALU.add))
                    q.then(v.scalar_tensor_tensor(own[:], own[:], 0.2, own[:], ALU.mult, ALU.max))
                    q.then(v.tensor_scalar(den[:], acc[:, :, D:D + H], 0.0, -BIG, ALU.is_equal, ALU.mult))
                    q.then(v.tensor_tensor(edge_scale[:], acc[:, :, D + H:], den[:], ALU.add))
                    q.then(v.tensor_tensor(most[:], edge_scale[:], own[:], ALU.max))
                    q.mark(v.tensor_tensor(edge_scale[:], edge_scale[:], most[:], ALU.subtract))
                    q.then(v.tensor_tensor(own_scale[:], own[:], most[:], ALU.subtract))
                    v.sem_inc(before_exp, 1)
                    v.wait_ge(exps, 2)
                    q.then(v.tensor_tensor(den[:], acc[:, :, D:D + H], edge_scale[:], ALU.mult))
                    q.then(v.tensor_tensor(den[:], den[:], own_scale[:], ALU.add))
                    q.then(v.tensor_scalar(den[:], den[:], 1e-16, None, ALU.add))
                    q.then(v.reciprocal(den[:], den[:]))
                    q.mark(v.tensor_tensor(edge_scale[:], edge_scale[:], den[:], ALU.mult))
                    q.then(v.tensor_tensor(own_scale[:], own_scale[:], den[:], ALU.mult))
                    v.wait_ge(b_in, 16)

                    def by_head(a, t):
                        return a[:, bass.ds(t, 1), 0:D].rearrange("p t (h d) -> p (t h) d", h=H)

                    def over(a, t):
                        return a[:, bass.ds(t, 1), :].rearrange("p t h -> p (t h)").unsqueeze(2).to_broadcast([P, H, HD])

                    with q.loop(T, 4) as t:
                        q.mark(v.tensor_tensor(z[:, 0, :].rearrange("p (h d) -> p h d", h=H), by_head(acc, t), over(edge_scale, t), ALU.mult))
                        q.then(v.tensor_tensor(z[:, 1, :].rearrange("p (h d) -> p h d", h=H), by_head(feat, t), over(own_scale, t), ALU.mult))
                        q.then(v.tensor_tensor(z[:, 0, :], z[:, 0, :], z[:, 1, :], ALU.add))
                        q.then(v.tensor_tensor(acc[:, bass.ds(t, 1), 0:D].rearrange("p t d -> p (t d)"), z[:, 0, :], bias[:], ALU.add))
        norm_stats(nc, g, "loops_out_norm", acc)
        add_normed(nc, g, "loops_out", acc, A["L3_gnn_ln_gamma"], A["L3_gnn_ln_beta"])


def add_normed(nc, g, name, values, gamma, beta):
    with Stage(nc, g, name) as st:
        gb = st.sb("gb", [P, 2, D])
        z = st.sb("z", [P, D])
        c_in, dv = st.sem("c_in"), st.sem("dv")
        with st.block() as block:
            @block.sync
            def _(sp):
                sp.dma_start(gb[:, 0, :], spread(gamma)).then_inc(c_in, 16)
                sp.dma_start(gb[:, 1, :], spread(beta)).then_inc(c_in, 16)

            @block.vector
            def _(v):
                q = Steps(v, dv)
                v.wait_ge(c_in, 32)
                xf = g.x[:].rearrange("p t d -> p (t d)")
                with q.loop(T, 4) as t:
                    q.then(v.tensor_scalar(z[:], values[:, bass.ds(t, 1), 0:D].rearrange("p t d -> p (t d)"), g.mean[:, bass.ds(t, 1)],
                                           g.rstd[:, bass.ds(t, 1)], ALU.subtract, ALU.mult))
                    q.then(v.tensor_tensor(z[:], z[:], gb[:, 0, :], ALU.mult))
                    q.then(v.tensor_tensor(z[:], z[:], gb[:, 1, :], ALU.add))
                    q.then(v.tensor_tensor(xf[:, at(t, D)], xf[:, at(t, D)], z[:], ALU.add))



def sum_edges(nc, g, name, table, feats, mean, acc):
    with Stage(nc, g, name) as st:
        idx = st.sb("idx", [P, SLOTS], U32)
        rows = st.sb("rows", [P, SLOTS, D])
        own = st.sb("own", [P, SLOTS, D])
        msg = st.sb("msg", [P, BANKS, D + 1])
        share = st.sb("share", [P, BANKS])
        hot = st.sb("hot", [P, BANKS, P])
        part = [st.ps(f"part{j}", [P, 512]) for j in range(BANKS)]
        one, idx_ready, idx_taken, share_ready, hot_ready, msg_ready, summed, added = (
            st.sem(n) for n in ("one", "idx_ready", "idx_taken", "share_ready", "hot_ready", "msg_ready", "summed", "added"))
        own_in = st.sems("own_in", SLOTS)
        rows_in, before = st.gathers(SLOTS, [-(-(S - j) // SLOTS) for j in range(SLOTS)])
        accf = acc[:].rearrange("p t w -> p (t w)")
        feats_v = feats.rearrange("(c p) d -> p c d", p=P)
        with st.block() as block:
            @block.scalar
            def _(act):
                def quad(s, q):
                    for j in range(q * QUAD, q * QUAD + QUAD):
                        act.wait_ge(rows_in[j], s + before[j])
                    act.activation(idx[:, at(q, QUAD)], g.src_s[:, bass.ds(s + q * QUAD, QUAD)], ACT.Copy).then_inc(idx_ready, 1)
                    for j, c in enumerate(load_steps(nc, ENGINE.Activation, g.chunk_of, s + q * QUAD, QUAD, C - 1), q * QUAD):
                        act.wait_ge(summed, s + (j + 1))
                        act.activation(share[:, j % BANKS:j % BANKS + 1], mean[:, bass.ds(c, 1)], ACT.Copy).then_inc(share_ready, 1)

                act.sem_inc(summed, BANKS)
                for_quads(act, quad)

            @block.gpsimd
            def _(pool):
                def quad(s, q):
                    pool.wait_ge(msg_ready, s + (q * QUAD + QUAD))
                    pool.wait_ge(idx_ready, s // QUAD + (q + 1))
                    pool.sem_inc(idx_taken, 1)
                    for j in range(q * QUAD, q * QUAD + QUAD):
                        pool.indirect_dma_start(out=rows[:, j, :], out_offset=None, in_=table,
                                                in_offset=bass.IndirectOffsetOnAxis(ap=idx[:, j:j + 1], axis=0),
                                                ).then_inc(rows_in[j], 16)

                pool.sem_inc(msg_ready, SLOTS)
                for_quads(pool, quad)

            @block.sync
            def _(sp):
                def quad(s, q):
                    for j, c in enumerate(load_steps(nc, ENGINE.SP, g.chunk_of, s + q * QUAD, QUAD, C - 1), q * QUAD):
                        sp.wait_ge(msg_ready, s + (j + 1))
                        sp.dma_start(own[:, j:j + 1, :], feats_v[:, bass.ds(c, 1), :]).then_inc(own_in[j], 16)

                for_quads(sp, quad)

            @block.vector
            def _(v):
                def step(s, j):
                    v.wait_ge(share_ready, s + (j + 1))
                    v.tensor_scalar(hot[:, j % BANKS, :], g.iota[0:P, 0:P], g.place_s[:, bass.ds(s + j, 1)], share[:, j % BANKS:j % BANKS + 1],
                                    ALU.is_equal, ALU.mult).then_inc(hot_ready, 1)
                    v.wait_ge(own_in[j % SLOTS], s + (j // SLOTS * SLOTS + 16))
                    v.wait_ge(rows_in[j % SLOTS], s + (j // SLOTS * SLOTS + before[j % SLOTS] + 16))
                    v.tensor_tensor(msg[:, j % BANKS, 0:D], rows[:, j % SLOTS, :], own[:, j % SLOTS, :], ALU.add).then_inc(msg_ready, 1)

                def add(s, j, t):
                    v.wait_ge(summed, s + (j + 1 + BANKS))
                    v.wait_ge(added, s + (j + BANKS))
                    tile = accf[:, at(t, D + 1)]
                    v.tensor_tensor(tile, tile, part[j % BANKS][:, 0:D + 1], ALU.add).then_inc(added, 1)

                v.memset(msg[:, :, D:D + 1], 1.0).then_inc(one, 1)
                v.sem_inc(added, BANKS)
                for_quads_ahead(v, lambda s, n: load_steps(nc, ENGINE.DVE, g.tile_of, s, n, T - 1), step, add)

            @block.tensor
            def _(pe):
                def quad(s, q):
                    for j in range(q * QUAD, q * QUAD + QUAD):
                        pe.wait_ge(hot_ready, s + (j + 1))
                        pe.wait_ge(added, s + (j + 1))
                        pe.wait_ge(msg_ready, s + (j + 1 + SLOTS))
                        pe.matmul(part[j % BANKS][:, 0:D + 1], hot[:, j % BANKS, :], msg[:, j % BANKS, :], start=True, stop=True).then_inc(summed, 1)

                pe.wait_ge(one, 1)
                for_quads(pe, quad)


def edge_gat(nc, g, A):
    norm_stats(nc, g, "edge_norm")
    with Stage(nc, g, "edge") as st0:
        table, src_end = st0.dram("table", (N, D)), st0.dram("src_end", (N, H))
        mean = st0.sb("mean", [P, C])
        with Stage(nc, g, "edge_soft") as st1:
            proj = st1.sb("proj", [128, KD, 2 * H])
            ends = st1.sb("ends", [P, T, 2 * H])
            logit = st1.sb("logit", [128, RUN])
            edge_in(nc, g, A, proj, ends, table)
            store_ends(nc, g, "edge_ends", ((src_end, ends[:, :, 0:H]),))
            edge_dst(nc, g, "edge_dst", ends[:, :, H:], logit)
            edge_logits(nc, g, "edge_logits", src_end, logit, logit, (A["edge_attr_256"], proj[:, :, 0:H]))
            weight = st1.sb("weight", [P, C, H])
            edge_weights(nc, g, "edge_weights", logit, weight, mean=mean)
        acc = st0.sb("acc", [P, T, D + 1])
        clear(nc, g, "edge_clear", acc)
        sum_edges(nc, g, "edge_sum", table, A["edge_attr_256"], mean, acc)
        edge_out(nc, g, A, acc)


def edge_in(nc, g, A, proj, ends, table):
    with Stage(nc, g, "edge_in") as st:
        w1 = st.sb("w1", [128, KD, D])
        w4 = st.sb("w4", [128, KD, H])
        b1 = st.sb("b1", [128, KD])
        b45 = st.sb("b45", [1, 2 * H])
        const = st.sb("const", [1, 2 * H])
        one_row = st.sb("one_row", [1, P])
        tile = st.sb("tile", [P, GRP, D])
        x_t = st.sb("x_t", [128, GRP, KD, P])
        pp = [st.ps(f"pp{k}", [128, 512]) for k in range(KD)]
        bp = st.ps("bp", [1, 512])
        tp = [st.ps(f"tp{j}", [128, 512]) for j in range(2)]
        ep = [st.ps(f"ep{j}", [P, 512]) for j in range(2)]
        w_in, made, proj_done, proj_ready, dv, normed, x_turned, x_t_ready, e_done, e_out, out = (
            st.sem(n) for n in ("w_in", "made", "proj_done", "proj_ready", "dv", "normed", "x_turned", "x_t_ready", "e_done", "e_out", "out"))
        xf = g.x[:].rearrange("p t d -> p (t d)")
        with st.block() as block:
            @block.sync
            def _(sp):
                sp.dma_start(w1[:], A["L1_gnn_W1"].rearrange("(k p) n -> p k n", p=128)).then_inc(w_in, 16)
                sp.dma_start(w4[:], A["L1_gnn_W4_t"].rearrange("(k p) n -> p k n", p=128)).then_inc(w_in, 16)
                sp.dma_start(proj[:, :, H:], A["L1_gnn_W5_t"].rearrange("(k p) n -> p k n", p=128)).then_inc(w_in, 16)
                sp.dma_start(b1[:], A["L1_gnn_b1_col"]).then_inc(w_in, 16)
                sp.dma_start(b45[0:1, 0:H], row(A["L1_gnn_b4"])).then_inc(w_in, 16)
                sp.dma_start(b45[0:1, H:], row(A["L1_gnn_b5"])).then_inc(w_in, 16)
                tv = table.rearrange("(t p) d -> p t d", p=P)
                with sp.Fori(0, T // GRP) as i:
                    for j in range(GRP):
                        sp.wait_ge(normed, i * GRP + j + 1)
                        sp.dma_start(tv[:, bass.ds(i * GRP + j, 1), :], tile[:, j:j + 1, :]).then_inc(out, 16)
                sp.wait_ge(out, 16 * T)

            @block.vector
            def _(v):
                q = Steps(v, dv)
                v.memset(one_row[:], 1.0).then_inc(made, 1)
                q.then(v.memset(const[:], 0.0))
                v.wait_ge(w_in, 16 * 6)
                v.wait_ge(proj_done, KD + 1)
                for k in range(KD):
                    q.mark(v.tensor_copy(proj[:, k, 0:H], pp[k][:, 0:H]))
                q.then(v.tensor_tensor(const[0:1, H:], b45[0:1, 0:H], b45[0:1, H:], ALU.add))
                q.then(v.tensor_tensor(const[0:1, H:], const[0:1, H:], bp[0:1, 0:H], ALU.add))
                v.sem_inc(proj_ready, 1)
                with v.Fori(0, T // GRP) as i:
                    for j in range(GRP):
                        v.wait_ge(x_turned, i * GRP)
                        v.wait_ge(out, i * (16 * GRP))
                        t = i * GRP + j
                        v.tensor_scalar(tile[:, j, :], xf[:, at(t, D)], g.mean[:, bass.ds(t, 1)], g.rstd[:, bass.ds(t, 1)],
                                        ALU.subtract, ALU.mult).then_inc(normed, 1)
                    for j in range(GRP):
                        v.wait_ge(e_done, i * GRP + j + 1)
                        v.tensor_copy(ends[:, bass.ds(i * GRP + j, 1), :].rearrange("p t h -> p (t h)"), ep[j % 2][:, 0:2 * H]).then_inc(e_out, 1)

            @block.scalar
            def _(act):
                with act.Fori(0, T // GRP) as i:
                    for j in range(GRP):
                        act.wait_ge(x_turned, i * GRP + j + 1)
                        act.wait_ge(e_done, i * GRP)
                        act.activation(x_t[:, j, :, :].rearrange("p k n -> p (k n)"), tp[j % 2][:, 0:KD * P], ACT.Copy).then_inc(x_t_ready, 1)

            @block.tensor
            def _(pe):
                pe.wait_ge(w_in, 16 * 6)
                pe.wait_ge(made, 1)
                for k in range(KD):
                    for m in range(KD):
                        mm = pe.matmul(pp[k][:, 0:H], w1[:, m, k * 128:(k + 1) * 128], w4[:, m, :], start=(m == 0), stop=(m == KD - 1))
                    mm.then_inc(proj_done, 1)
                for m in range(KD):
                    mm = pe.matmul(bp[0:1, 0:H], b1[:, m:m + 1], w4[:, m, :], start=(m == 0), stop=(m == KD - 1))
                mm.then_inc(proj_done, 1)
                pe.wait_ge(proj_ready, 1)
                with pe.Fori(0, T // GRP) as i:
                    for j in range(GRP):
                        pe.wait_ge(normed, i * GRP + j + 1)
                        pe.wait_ge(x_t_ready, i * GRP + max(j - 1, 0))
                        for k in range(KD):
                            mm = pe.transpose(tp[j % 2][:, k * P:(k + 1) * P], tile[:, j, k * 128:(k + 1) * 128], g.ident[0:P, 0:P])
                        mm.then_inc(x_turned, 1)
                    for j in range(GRP):
                        pe.wait_ge(x_t_ready, i * GRP + j + 1)
                        pe.wait_ge(e_out, i * GRP + max(j - 1, 0))
                        for k in range(KD):
                            pe.matmul(ep[j % 2][:, 0:2 * H], x_t[:, j, k, :], proj[:, k, :], start=(k == 0), stop=False)
                        pe.matmul(ep[j % 2][:, 0:2 * H], one_row[:], const[:], start=False, stop=True).then_inc(e_done, 1)


def edge_out(nc, g, A, acc):
    SLOPE = 11.0 / 48.0
    with Stage(nc, g, "edge_out") as st:
        w23 = st.sb("w23", [128, KD, 2 * D])
        w1 = st.sb("w1", [128, KD, D])
        b = st.sb("b", [P, 3, D])
        tile = st.sb("tile", [P, GRP, 2, D])
        x_t = st.sb("x_t", [128, GRP, 2, KD, P])
        z = st.sb("z", [P, GRP, 2 * D])
        iso = st.sb("iso", [P, T])
        linked = st.sb("linked", [P, T])
        tp = [st.ps(f"tp{j}", [128, 512]) for j in range(2)]
        sp_ = [st.ps(f"sp{j}", [P, 512]) for j in range(2)]
        ap_ = [st.ps(f"ap{j}", [P, 512]) for j in range(2)]
        w_in, normed, turned, x_t_ready, done, z_out, dv = (
            st.sem(n) for n in ("w_in", "normed", "turned", "x_t_ready", "done", "z_out", "dv"))
        xf = g.x[:].rearrange("p t d -> p (t d)")
        with st.block() as block:
            @block.sync
            def _(sp):
                sp.dma_start(w23[:, :, 0:D], A["L1_gnn_W2_t"].rearrange("(k p) n -> p k n", p=128)).then_inc(w_in, 16)
                sp.dma_start(w23[:, :, D:], A["L1_gnn_W3_t"].rearrange("(k p) n -> p k n", p=128)).then_inc(w_in, 16)
                sp.dma_start(w1[:], A["L1_gnn_W1_t"].rearrange("(k p) n -> p k n", p=128)).then_inc(w_in, 16)
                for n, v in enumerate((A["L1_gnn_b2"], A["L1_gnn_b3"], A["L1_gnn_b1"])):
                    sp.dma_start(b[:, n, :], spread(v)).then_inc(w_in, 16)

            @block.vector
            def _(v):
                q = Steps(v, dv)
                sums = acc[:, :, D]
                q.mark(v.tensor_scalar(iso[:], sums, 0.0, None, ALU.is_equal))
                q.then(v.tensor_scalar(linked[:], sums, 0.0, None, ALU.not_equal))
                v.wait_ge(w_in, 16 * 6)
                with q.loop(T // GRP, GRP * 7) as i:
                    for j in range(GRP):
                        v.wait_ge(turned, i * (2 * GRP))
                        t = i * GRP + j
                        v.tensor_scalar(tile[:, j, 0, :], xf[:, at(t, D)], g.mean[:, bass.ds(t, 1)], g.rstd[:, bass.ds(t, 1)],
                                        ALU.subtract, ALU.mult).then_inc(normed, 1)
                        v.tensor_copy(tile[:, j, 1, :], acc[:, bass.ds(t, 1), 0:D].rearrange("p t d -> p (t d)")).then_inc(normed, 1)
                    for j in range(GRP):
                        t = i * GRP + j
                        v.wait_ge(done, i * GRP + j + 1)
                        zj = z[:, j, 0:D]
                        q.then(v.tensor_tensor(z[:, j, :], sp_[j % 2][:], b[:, 0:2, :].rearrange("p a d -> p (a d)"), ALU.add))
                        q.then(v.tensor_scalar(zj, zj, linked[:, bass.ds(t, 1)], None, ALU.mult))
                        q.then(v.scalar_tensor_tensor(zj, z[:, j, D:], iso[:, bass.ds(t, 1)], zj, ALU.mult, ALU.add))
                        q.then(v.scalar_tensor_tensor(zj, b[:, 2, :], acc[:, bass.ds(t, 1), D:D + 1].rearrange("p t d -> p (t d)"), zj, ALU.mult, ALU.add))
                        q.then(v.tensor_tensor(zj, zj, ap_[j % 2][:, 0:D], ALU.add))
                        v.sem_inc(z_out, 1)
                        q.then(v.scalar_tensor_tensor(zj, zj, SLOPE, zj, ALU.mult, ALU.max))
                        q.then(v.tensor_tensor(xf[:, at(t, D)], xf[:, at(t, D)], zj, ALU.add))

            @block.scalar
            def _(act):
                with act.Fori(0, T // GRP) as i:
                    for j in range(GRP):
                        for n in range(2):
                            act.wait_ge(turned, i * (2 * GRP) + 2 * j + n + 1)
                            act.wait_ge(done, i * GRP)
                            act.activation(x_t[:, j, n, :, :].rearrange("p k n -> p (k n)"), tp[n][:, 0:KD * P], ACT.Copy).then_inc(x_t_ready, 1)

            @block.tensor
            def _(pe):
                pe.wait_ge(w_in, 16 * 6)
                with pe.Fori(0, T // GRP) as i:
                    for j in range(GRP):
                        for n in range(2):
                            pe.wait_ge(normed, i * (2 * GRP) + 2 * j + n + 1)
                            pe.wait_ge(x_t_ready, i * (2 * GRP) + max(2 * j + n - 1, 0))
                            for k in range(KD):
                                mm = pe.transpose(tp[n][:, k * P:(k + 1) * P], tile[:, j, n, k * 128:(k + 1) * 128], g.ident[0:P, 0:P])
                            mm.then_inc(turned, 1)
                    for j in range(GRP):
                        pe.wait_ge(x_t_ready, i * (2 * GRP) + 2 * j + 2)
                        pe.wait_ge(z_out, i * GRP + max(j - 1, 0))
                        for k in range(KD):
                            pe.matmul(sp_[j % 2][:], x_t[:, j, 0, k, :], w23[:, k, :], start=(k == 0), stop=(k == KD - 1))
                        for k in range(KD):
                            mm = pe.matmul(ap_[j % 2][:, 0:D], x_t[:, j, 1, k, :], w1[:, k, :], start=(k == 0), stop=(k == KD - 1))
                        mm.then_inc(done, 1)



def nodes_turned(nc, g, name, x_t, heads, head_out, width, bias=None):
    with Stage(nc, g, name) as st:
        w = st.sb("w", [128, KD, width])
        b = st.sb("b", [P, width])
        bias_two = st.sb("bias_two", [P, width])
        tile = st.sb("tile", [P, GRP, D])
        part = st.sb("part", [128, GRP, KD, P])
        tp = [st.ps(f"tp{j}", [128, 512]) for j in range(2)]
        hp = [st.ps(f"hp{j}", [P, 512]) for j in range(2)]
        w_in, normed, turned, part_ready, kept, done, out = (
            st.sem(n) for n in ("w_in", "normed", "turned", "part_ready", "kept", "done", "out"))
        LOADS = (heads is not None) + len(bias or ())
        with st.block() as block:
            @block.sync
            def _(sp):
                if heads is not None:
                    sp.dma_start(w[:], heads).then_inc(w_in, 16)
                for n, v in enumerate(bias or ()):
                    sp.dma_start(b[:] if n == 0 else bias_two[:], spread(v)).then_inc(w_in, 16)

            @block.vector
            def _(v):
                xf = g.x[:].rearrange("p t d -> p (t d)")
                if bias:
                    v.wait_ge(w_in, 16 * LOADS)
                    if len(bias) == 2:
                        v.tensor_tensor(b[:], b[:], bias_two[:], ALU.add).then_inc(out, 1)
                    else:
                        v.sem_inc(out, 1)
                else:
                    v.sem_inc(out, 1)
                v.wait_ge(out, 1)
                with v.Fori(0, T // GRP) as i:
                    for j in range(GRP):
                        t = i * GRP + j
                        v.wait_ge(turned, i * GRP)
                        v.tensor_scalar(tile[:, j, :], xf[:, at(t, D)], g.mean[:, bass.ds(t, 1)], g.rstd[:, bass.ds(t, 1)],
                                        ALU.subtract, ALU.mult).then_inc(normed, 1)
                    if heads is not None:
                        for j in range(GRP):
                            v.wait_ge(done, i * GRP + j + 1)
                            to = head_out[:, bass.ds(i * GRP + j, 1), :].rearrange("p t h -> p (t h)")
                            if bias:
                                v.tensor_tensor(to, hp[j % 2][:, 0:width], b[:], ALU.add).then_inc(out, 1)
                            else:
                                v.tensor_copy(to, hp[j % 2][:, 0:width]).then_inc(out, 1)

            @block.scalar
            def _(act):
                with act.Fori(0, T // GRP) as i:
                    for j in range(GRP):
                        cols = tp[j % 2][:, 0:KD * P].rearrange("p (k n) -> p k n", k=KD)
                        act.wait_ge(turned, i * GRP + j + 1)
                        if heads is not None:
                            act.wait_ge(done, i * GRP)
                            act.activation(part[:, j, :, :], cols, ACT.Copy).then_inc(part_ready, 1)
                        act.activation(x_t[:, :, bass.ds(i * (GRP * P) + j * P, P)], cols, ACT.Copy).then_inc(kept, 1)

            @block.tensor
            def _(pe):
                if heads is not None:
                    pe.wait_ge(w_in, 16 * LOADS)
                with pe.Fori(0, T // GRP) as i:
                    for j in range(GRP):
                        pe.wait_ge(normed, i * GRP + j + 1)
                        pe.wait_ge(kept, i * GRP + max(j - 1, 0))
                        for k in range(KD):
                            mm = pe.transpose(tp[j % 2][:, k * P:(k + 1) * P], tile[:, j, k * 128:(k + 1) * 128], g.ident[0:P, 0:P])
                        mm.then_inc(turned, 1)
                    if heads is not None:
                        for j in range(GRP):
                            pe.wait_ge(part_ready, i * GRP + j + 1)
                            pe.wait_ge(out, i * GRP + max(j - 1, 0) + 1)
                            for k in range(KD):
                                mm = pe.matmul(hp[j % 2][:, 0:width], part[:, j, k, :], w[:, k, :], start=(k == 0), stop=(k == KD - 1))
                            mm.then_inc(done, 1)


def ffn(nc, g, name, x_t, w1, b1, w2, FB, func, finish, scratch, gate=None):
    with Stage(nc, g, name) as st:
        hid = st.sb("hid", [128, 2, W])
        used = st.sb("used", [128, 2, W]) if gate else hid
        if gate:
            coef_t, sel, b2, experts = gate
            spans = sel.shape[1]
            share = FB // spans
            coef = st.sb("coef", [experts, 2, W])
        hp = [st.ps(f"hp{j}", [128, 512]) for j in range(2)]
        cp = [st.ps(f"cp{j}", [128, 512]) for j in range(2)]
        ap = [st.ps(f"ap{j}", [P, 512]) for j in range(3)]
        coef_ready, spread_out, hid_done, hid_ready, gated, taken, put, dv = (
            st.sem(n) for n in ("coef_ready", "spread_out", "hid_done", "hid_ready", "gated", "taken", "put", "dv"))
        b_in = st.sem("b_in")
        tools = scratch(st, b_in)
        loads = tools.loads
        with st.block() as block:
            if loads:
                @block.sync
                def _(sp):
                    for to, of in loads:
                        sp.dma_start(to, of).then_inc(b_in, 16)

            @block.scalar
            def _(act):
                act.sem_inc(hid_ready, 2)
                with act.Fori(0, T // GRP) as i:
                    for h, (t0, n) in enumerate(PARTS):
                        for f in range(FB):
                            u = h * FB + f
                            act.wait_ge(hid_done, i * (2 * FB) + u + 1)
                            act.wait_ge(gated if gate else taken, i * (2 * FB) + u + 1)
                            act.activation(hid[:, f % 2, 0:n * P], hp[f % 2][:, 0:n * P], func, bias=b1[:, f:f + 1]).then_inc(hid_ready, 1)

            @block.vector
            def _(v):
                q = Steps(v, dv)
                if loads:
                    v.wait_ge(b_in, 16 * len(loads))
                if gate:
                    v.sem_inc(gated, 2)
                with q.loop(T // GRP, GRP * tools.steps) as i:
                    for h, (t0, n) in enumerate(PARTS):
                        if gate:
                            v.tensor_copy(coef[:, h, 0:n * P], coef_t[:, nodes(i, h)]).then_inc(coef_ready, 1)
                            for f in range(FB):
                                u = h * FB + f
                                v.wait_ge(hid_ready, i * (2 * FB) + u + 1 + 2)
                                v.wait_ge(spread_out, i * (2 * spans) + h * spans + f // share + 1)
                                v.wait_ge(taken, i * (2 * FB) + u + 1)
                                v.tensor_tensor(used[:, f % 2, 0:n * P], hid[:, f % 2, 0:n * P], cp[f // share % 2][:, 0:n * P],
                                                ALU.mult).then_inc(gated, 1)
                        v.wait_ge(taken, i * (2 * FB) + (h * FB + FB + 2))
                        for j in range(n):
                            finish(v, q, tools, i * GRP + t0 + j, ap[j][:, 0:D])
                        v.sem_inc(put, 1)

            @block.tensor
            def _(pe):
                pe.sem_inc(taken, 2)
                with pe.Fori(0, T // GRP) as i:
                    for h, (t0, n) in enumerate(PARTS):
                        def up(f):
                            u = h * FB + f
                            if gate and f % share == 0:
                                if f == 0:
                                    pe.wait_ge(coef_ready, i * 2 + h + 1)
                                pe.wait_ge(gated, i * (2 * FB) + (h * FB + max(f - share, 0) + 2))
                                pe.matmul(cp[f // share % 2][:, 0:n * P], sel[:, f // share, :], coef[:, h, 0:n * P], start=True, stop=True,
                                          ).then_inc(spread_out, 1)
                            pe.wait_ge(hid_ready, i * (2 * FB) + u + 1)
                            for k in range(KD):
                                mm = pe.matmul(hp[f % 2][:, 0:n * P], w1[:, k, f * 128:(f + 1) * 128], x_t[:, k, nodes(i, h)],
                                               start=(k == 0), stop=(k == KD - 1))
                            mm.then_inc(hid_done, 1)

                        def down(f):
                            u = h * FB + f
                            pe.wait_ge(gated if gate else hid_ready, i * (2 * FB) + u + 1 + 2)
                            for j in range(n):
                                mm = pe.matmul(ap[j][:, 0:D], used[:, f % 2, j * P:(j + 1) * P], w2[:, f, :],
                                               start=(f == 0 and not gate), stop=(f == FB - 1))
                            mm.then_inc(taken, 1)

                        up(0)
                        pe.wait_ge(put, i * 2 + h)
                        if gate:
                            for j in range(n):
                                pe.matmul(ap[j][:, 0:D], coef[:, h, j * P:(j + 1) * P], b2, start=True, stop=False)
                        for f in range(FB):
                            if f + 1 < FB:
                                up(f + 1)
                            down(f)


def add_result(relu):
    def scratch(st, b_in):
        return Tools(1)

    def finish(v, q, tools, t, result):
        x = tools.x[:, at(t, D)]
        if relu:
            q.then(v.scalar_tensor_tensor(x, result, 0.0, x, ALU.max, ALU.add))
        else:
            q.then(v.tensor_tensor(x, x, result, ALU.add))
    return scratch, finish


def load_all(nc, g, name, loads):
    with Stage(nc, g, name) as st:
        w_in = st.sem("w_in")
        with st.block() as block:
            @block.sync
            def _(sp):
                for to, of in loads:
                    sp.dma_start(to, of).then_inc(w_in, 16)
                sp.wait_ge(w_in, 16 * len(loads))


def choose(nc, g, name, logit, coef_t, experts, top):
    with Stage(nc, g, name) as st:
        l = st.sb("l", [P, GRP, experts])
        best = st.sb("best", [P, GRP, 8])
        where = st.sb("where", [P, GRP, 8], U32)
        place = st.sb("place", [P, GRP, 2])
        share = st.sb("share", [P, GRP, 2])
        den = st.sb("den", [P, GRP])
        mask = st.sb("mask", [P, GRP, 2, experts])
        tp = [st.ps(f"tp{j}", [experts, 512]) for j in range(2)]
        dv, waited, gap_ready, exp_ready, mask_ready, turned, put = (st.sem(n) for n in ("dv", "waited", "gap_ready", "exp_ready", "mask_ready", "turned", "put"))
        with st.block() as block:
            @block.vector
            def _(v):
                q = Steps(v, dv)
                with q.loop(T // GRP, 4 * GRP + (0 if top == 1 else 3 + 2 * GRP)) as i:
                    v.wait_ge(turned, i * GRP)
                    for j in range(GRP):
                        q.mark(v.tensor_copy(l[:, j, :], logit[:, bass.ds(i * GRP + j, 1), :].rearrange("p t e -> p (t e)")))
                    q.wait()
                    v.sem_inc(waited, 1)
                    for j in range(GRP):
                        q.mark(v.max(best[:, j, :], l[:, j, :]))
                    q.wait()
                    v.sem_inc(waited, 1)
                    for j in range(GRP):
                        q.mark(v.max_index(where[:, j, :], best[:, j, :], l[:, j, :]))
                    q.wait()
                    for j in range(GRP):
                        q.mark(v.tensor_copy(place[:, j, :], where[:, j, 0:2]))
                    q.wait()
                    if top == 1:
                        for j in range(GRP):
                            v.tensor_scalar(mask[:, j, 0, :], g.iota[0:P, 0:experts], place[:, j, 0:1], None, ALU.is_equal).then_inc(mask_ready, 1)
                    else:
                        v.tensor_tensor(share[:, :, 1], best[:, :, 1], best[:, :, 0], ALU.subtract).then_inc(gap_ready, 1)
                        v.wait_ge(exp_ready, i + 1)
                        q.then(v.tensor_scalar(den[:], share[:, :, 1], 1.0, None, ALU.add))
                        q.then(v.reciprocal(share[:, :, 0], den[:]))
                        q.then(v.tensor_tensor(share[:, :, 1], share[:, :, 1], share[:, :, 0], ALU.mult))
                        for j in range(GRP):
                            for n in range(2):
                                q.mark(v.tensor_scalar(mask[:, j, n, :], g.iota[0:P, 0:experts], place[:, j, n:n + 1], share[:, j, n:n + 1],
                                                       ALU.is_equal, ALU.mult))
                        q.wait()
                        for j in range(GRP):
                            v.tensor_tensor(mask[:, j, 0, :], mask[:, j, 0, :], mask[:, j, 1, :], ALU.add).then_inc(mask_ready, 1)
                    for j in range(GRP):
                        v.wait_ge(turned, i * GRP + j + 1)
                        v.tensor_copy(coef_t[:, bass.ds(i * (GRP * P) + j * P, P)], tp[j % 2][:, 0:P]).then_inc(put, 1)

            if top == 2:
                @block.scalar
                def _(act):
                    with act.Fori(0, T // GRP) as i:
                        act.wait_ge(gap_ready, i + 1)
                        act.activation(share[:, :, 1], share[:, :, 1], ACT.Exp).then_inc(exp_ready, 1)

            @block.tensor
            def _(pe):
                with pe.Fori(0, T // GRP) as i:
                    for j in range(GRP):
                        pe.wait_ge(mask_ready, i * GRP + j + 1)
                        pe.wait_ge(put, i * GRP + max(j - 1, 0))
                        pe.transpose(tp[j % 2][:, 0:P], mask[:, j, 0, :], g.ident[0:P, 0:P]).then_inc(turned, 1)


def moe(nc, g, name, heads, bias, w1, b1_col, w2, b2, sel_in, experts, hidden, top, relu):
    FB = experts * hidden // 128
    norm_stats(nc, g, f"{name}_norm")
    with Stage(nc, g, name) as st:
        x_t = st.sb("x_t", [128, KD, N])
        coef_t = st.sb("coef_t", [experts, N])
        w1s = st.sb("w1s", [128, KD, FB * 128])
        w2s = st.sb("w2s", [128, FB, D])
        b1s = st.sb("b1s", [128, FB])
        b2s = st.sb("b2s", [experts, D])
        sel = st.sb("sel", list(sel_in.shape))
        with Stage(nc, g, f"{name}_gate") as st1:
            logit = st1.sb("logit", [P, T, experts])
            nodes_turned(nc, g, f"{name}_in", x_t, heads, logit, experts, bias)
            choose(nc, g, f"{name}_choose", logit, coef_t, experts, top)
        load_all(nc, g, f"{name}_load",
                 [(w1s[:, k, :].rearrange("p (e h) -> p e h", h=hidden), w1[:, k * 128:(k + 1) * 128, :].rearrange("e p h -> p e h")) for k in range(KD)]
                 + [(w2s[:], w2.rearrange("e h d -> (e h) d").rearrange("(f p) d -> p f d", p=128)),
                    (b1s[:], b1_col), (b2s[:], b2), (sel[:], sel_in)])
        scratch, finish = add_result(relu)

        def with_x(st, b_in):
            tools = scratch(st, b_in)
            tools.x = g.x[:].rearrange("p t d -> p (t d)")
            return tools

        ffn(nc, g, f"{name}_ffn", x_t, w1s, b1s, w2s, FB, ACT.Relu, finish, with_x, (coef_t, sel, b2s[:], experts))


def moe_one(nc, g, A):
    moe(nc, g, "one", A["L0_ffn_router_w_t"].rearrange("(k p) n -> p k n", p=128), [A["L0_ffn_router_b"]], A["L0_ffn_W1"], A["L0_ffn_b1_col"], A["L0_ffn_W2"], A["L0_ffn_b2"], A["sel_one"], 32, 64, 1, True)


def moe_two(nc, g, A):
    moe(nc, g, "two", A["L2_ffn_Wg"].rearrange("(k p) n -> p k n", p=128), [A["L2_ffn_bg"], A["L2_ffn_bias"]], A["L2_ffn_W1"], A["L2_ffn_b1_col"], A["L2_ffn_W2"], A["L2_ffn_b2"], A["sel_two"], 8, 512, 2, False)



def moe_all(nc, g, A):
    EX, F = A["L1_ffn_W1"].shape[0], A["L1_ffn_W1"].shape[2]
    FE = F // 128
    CAPACITY = float(-(-N * 5 // (4 * EX)))
    norm_stats(nc, g, "all_norm")
    with Stage(nc, g, "all") as st0:
        x_t = st0.sb("x_t", [128, KD, N])
        w1s = st0.sb("w1s", [128, KD, 2 * F])
        w2s = st0.sb("w2s", [128, 2 * FE, D])
        b1s = st0.sb("b1s", [128, 2 * FE])
        b2s = st0.sb("b2s", [P, D])
        y = st0.sb("y", [P, T, D])
        nodes_turned(nc, g, "all_in", x_t, None, None, 1)
        with Stage(nc, g, "all_route") as st:
            wr = st.sb("wr", [128, KD, EX])
            br = st.sb("br", [1, EX])
            b2 = st.sb("b2", [EX, D])
            mean = st.sb("mean", [128, KD])
            p = st.sb("p", [1, EX])
            r = st.sb("r", [1, EX])
            one = st.sb("one", [1, 4])
            best = st.sb("best", [1, 8])
            where = st.sb("where", [1, 8], U32)
            place = st.sb("place", [1, 2])
            share = st.sb("share", [1, 2])
            dense = st.sb("dense", [1, 2, EX])
            dense_col = st.sb("dense_col", [EX, P])
            ones = st.sb("ones", [1, 128])
            share_col = st.sb("share_col", [128, 2])
            lp = st.ps("lp", [1, 512])
            dp = st.ps("dp", [EX, 512])
            sp_ = st.ps("sp", [128, 512])
            bp = st.ps("bp", [P, 512])
            c_in, w_in, dv, mean_ready, logit_ready, exp_in, exp_out, chosen, shared, ready, col_ready = (
                st.sem(n) for n in ("c_in", "w_in", "dv", "mean_ready", "logit_ready", "exp_in", "exp_out", "chosen", "shared", "ready", "col_ready"))
            with st.block() as block:
                @block.sync
                def _(sp):
                    sp.dma_start(wr[:], A["L1_ffn_Wr"].rearrange("(k p) n -> p k n", p=128)).then_inc(c_in, 16)
                    sp.dma_start(br[:], row(A["L1_ffn_br"])).then_inc(c_in, 16)
                    sp.dma_start(b2[:], A["L1_ffn_b2"]).then_inc(c_in, 16)
                    sp.wait_ge(chosen, 1)
                    for n in range(2):
                        e = sp.value_load(where[0:1, n:n + 1], min_val=0, max_val=EX - 1)
                        for k in range(KD):
                            sp.dma_start(w1s[:, k:k + 1, n * F:(n + 1) * F],
                                         A["L1_ffn_W1"][bass.ds(e, 1), k * 128:(k + 1) * 128, :].rearrange("e p h -> p e h")).then_inc(w_in, 16)
                        for f in range(FE):
                            sp.dma_start(w2s[:, n * FE + f:n * FE + f + 1, :],
                                         A["L1_ffn_W2"][bass.ds(e, 1), f * 128:(f + 1) * 128, :].rearrange("e p d -> p e d")).then_inc(w_in, 16)
                        sp.dma_start(b1s[:, n * FE:(n + 1) * FE].rearrange("p (e f) -> p e f", e=1),
                                     A["L1_ffn_b1_col"][bass.ds(e, 1), :, :].rearrange("e p f -> p e f")).then_inc(w_in, 16)

                LOADS = 2 * (KD + FE + 1)

                @block.scalar
                def _(act):
                    for n, x in enumerate((p, r, share)):
                        act.wait_ge(exp_in, n + 1)
                        act.activation(x[:], x[:], ACT.Exp).then_inc(exp_out, 1)

                @block.vector
                def _(v):
                    q = Steps(v, dv)

                    def softmax(x, turn):
                        q.then(v.tensor_reduce(one[:, 0:1], x[:], AX.X, ALU.max))
                        q.then(v.tensor_scalar(x[:], x[:], one[:, 0:1], None, ALU.subtract))
                        v.sem_inc(exp_in, 1)
                        v.wait_ge(exp_out, turn)
                        q.then(v.tensor_reduce(one[:, 0:1], x[:], AX.X, ALU.add))
                        q.then(v.reciprocal(one[:, 1:2], one[:, 0:1]))
                        q.then(v.tensor_scalar(x[:], x[:], one[:, 1:2], None, ALU.mult))

                    q.mark(v.memset(ones[:], 1.0))
                    for k in range(KD):
                        q.mark(v.tensor_reduce(mean[:, k:k + 1], x_t[:, k, :], AX.X, ALU.add))
                    q.wait()
                    q.then(v.tensor_scalar(mean[:], mean[:], 1.0 / N, None, ALU.mult))
                    v.sem_inc(mean_ready, 1)
                    v.wait_ge(logit_ready, 1)
                    v.wait_ge(c_in, 48)
                    q.then(v.tensor_tensor(p[:], lp[:, 0:EX], br[:], ALU.add))
                    softmax(p, 1)
                    q.then(v.tensor_scalar(r[:], p[:], float(N), None, ALU.mult))
                    q.then(v.reciprocal(r[:], r[:]))
                    q.then(v.tensor_scalar(r[:], r[:], CAPACITY, 1.0, ALU.mult, ALU.min))
                    q.then(v.tensor_tensor(r[:], r[:], p[:], ALU.mult))
                    softmax(r, 2)
                    q.then(v.max(best[:], r[:]))
                    q.then(v.max_index(where[:], best[:], r[:]))
                    v.sem_inc(chosen, 1)
                    q.then(v.tensor_copy(place[:], where[:, 0:2]))
                    q.then(v.memset(share[:, 0:1], 0.0))
                    q.then(v.tensor_tensor(share[:, 1:2], best[:, 1:2], best[:, 0:1], ALU.subtract))
                    v.sem_inc(exp_in, 1)
                    v.wait_ge(exp_out, 3)
                    q.then(v.tensor_reduce(one[:, 0:1], share[:], AX.X, ALU.add))
                    q.then(v.reciprocal(one[:, 1:2], one[:, 0:1]))
                    q.then(v.tensor_scalar(share[:], share[:], one[:, 1:2], None, ALU.mult))
                    for n in range(2):
                        q.mark(v.tensor_scalar(dense[:, n, :], g.iota[0:1, 0:EX], place[:, n:n + 1], share[:, n:n + 1], ALU.is_equal, ALU.mult))
                    q.wait()
                    q.then(v.tensor_tensor(dense[:, 0, :], dense[:, 0, :], dense[:, 1, :], ALU.add))
                    v.sem_inc(shared, 1)
                    v.wait_ge(ready, 2)
                    q.mark(v.tensor_copy(share_col[:], sp_[:, 0:2]))
                    v.tensor_copy(dense_col[:], dp[:, 0:1].to_broadcast([EX, P])).then_inc(col_ready, 1)
                    v.wait_ge(ready, 3)
                    q.then(v.tensor_copy(b2s[:], bp[:, 0:D]))
                    v.wait_ge(w_in, 16 * LOADS)
                    for n in range(2):
                        q.mark(v.tensor_scalar(w2s[:, n * FE:(n + 1) * FE, :], w2s[:, n * FE:(n + 1) * FE, :], share_col[:, n:n + 1], None, ALU.mult))
                    q.wait()

                @block.tensor
                def _(pe):
                    pe.wait_ge(c_in, 48)
                    pe.wait_ge(mean_ready, 1)
                    for k in range(KD):
                        mm = pe.matmul(lp[:, 0:EX], mean[:, k:k + 1], wr[:, k, :], start=(k == 0), stop=(k == KD - 1))
                    mm.then_inc(logit_ready, 1)
                    pe.wait_ge(shared, 1)
                    pe.matmul(sp_[:, 0:2], ones[:], share[:], start=True, stop=True).then_inc(ready, 1)
                    pe.matmul(dp[:, 0:1], dense[:, 0, :], ones[:, 0:1], start=True, stop=True).then_inc(ready, 1)
                    pe.wait_ge(col_ready, 1)
                    pe.matmul(bp[:, 0:D], dense_col[:], b2[:], start=True, stop=True).then_inc(ready, 1)

        def scratch(st, b_in):
            tools = Tools(3)
            tools.n = st.sb("n", [P, D])
            return tools

        def finish(v, q, tools, t, result):
            q.then(v.tensor_scalar(tools.n[:], g.x[:, bass.ds(t, 1), :].rearrange("p t d -> p (t d)"), g.mean[:, bass.ds(t, 1)],
                                   g.rstd[:, bass.ds(t, 1)], ALU.subtract, ALU.mult))
            q.then(v.tensor_tensor(tools.n[:], tools.n[:], b2s[:], ALU.add))
            q.then(v.tensor_tensor(y[:, bass.ds(t, 1), :].rearrange("p t d -> p (t d)"), tools.n[:], result, ALU.add))

        ffn(nc, g, "all_ffn", x_t, w1s, b1s, w2s, 2 * FE, ACT.Gelu, finish, scratch)
        norm_stats(nc, g, "all_out_norm", y)
        add_normed(nc, g, "all_out", y, A["L1_ffn_gamma"], A["L1_ffn_beta"])



def ffn_top(nc, g, A):
    HID = A["L3_ffn_w1"].shape[1]
    FB = HID // 128
    KEEP = int(0.5 * N) - 1
    norm_stats(nc, g, "top_norm")
    with Stage(nc, g, "top") as st0:
        x_t = st0.sb("x_t", [128, KD, N])
        w1s = st0.sb("w1s", [128, KD, HID])
        w2s = st0.sb("w2s", [128, FB, D])
        b1s = st0.sb("b1s", [128, FB])
        coef = st0.sb("coef", [P, T])
        with Stage(nc, g, "top_rank") as st1:
            weight = st1.sb("weight", [P, T, 1])
            nodes_turned(nc, g, "top_in", x_t, A["L3_ffn_wr_col"], weight, 1, [A["L3_ffn_br"]])
            with Stage(nc, g, "top_count") as st:
                all_w = st.sb("all_w", [P, N])
                junk = st.sb("junk", [P, N])
                pid = st.sb("pid", [P, 1])
                before = st.sb("before", [P, P])
                count = st.sb("count", [P, 4, T])
                rows = st.sb("rows", [T, P])
                rp = st.ps("rp", [T, 512])
                row_d = st.dram("row", (N,))
                out, w_in, made, dv, turned, rows_ready = (st.sem(n) for n in ("out", "w_in", "made", "dv", "turned", "rows_ready"))
                with st.block() as block:
                    @block.sync
                    def _(sp):
                        sp.dma_start(w1s[:], A["L3_ffn_w1"].rearrange("(k p) n -> p k n", p=128)).then_inc(out, 16)
                        sp.dma_start(w2s[:], A["L3_ffn_w2"].rearrange("(f p) n -> p f n", p=128)).then_inc(out, 16)
                        sp.dma_start(b1s[:], A["L3_ffn_b1_col"]).then_inc(out, 16)
                        sp.wait_ge(rows_ready, 1)
                        sp.dma_start(row_d.rearrange("(t p) -> t p", p=P), rows[:]).then_inc(out, 16)
                        sp.wait_ge(out, 64)
                        sp.dma_start(all_w[:], spread(row_d)).then_inc(w_in, 16)

                    @block.gpsimd
                    def _(pool):
                        pool.iota(pid[:], pattern=[[0, 1]], base=0, channel_multiplier=1, allow_small_or_imprecise_dtypes=True).then_inc(made, 1)

                    @block.tensor
                    def _(pe):
                        pe.transpose(rp[:, 0:P], weight[:, :, 0], g.ident[0:P, 0:P]).then_inc(turned, 1)

                    @block.vector
                    def _(v):
                        q = Steps(v, dv)
                        v.wait_ge(turned, 1)
                        v.tensor_copy(rows[:], rp[:, 0:P]).then_inc(rows_ready, 1)
                        v.wait_ge(made, 1)
                        q.then(v.tensor_scalar(before[:], g.iota[0:P, 0:P], pid[:, 0:1], None, ALU.is_lt))
                        q.then(v.memset(count[:], 0.0))
                        v.wait_ge(w_in, 16)
                        for t in range(T):
                            w = weight[:, t, :]
                            if t:
                                q.then(v.tensor_scalar(junk[:, 0:t * P], all_w[:, 0:t * P], w, None, ALU.is_ge, ALU.add, accum_out=count[:, 0, t:t + 1]))
                            q.then(v.tensor_scalar(junk[:, t * P:], all_w[:, t * P:], w, None, ALU.is_gt, ALU.add, accum_out=count[:, 1, t:t + 1]))
                            q.then(v.scalar_tensor_tensor(junk[:, 0:P], all_w[:, t * P:(t + 1) * P], w, before[:], ALU.is_equal, ALU.mult,
                                                          accum_out=count[:, 2, t:t + 1]))
                        q.then(v.tensor_tensor(count[:, 0, :], count[:, 0, :], count[:, 1, :], ALU.add))
                        q.then(v.tensor_tensor(count[:, 0, :], count[:, 0, :], count[:, 2, :], ALU.add))
                        q.then(v.scalar_tensor_tensor(coef[:], count[:, 0, :], float(KEEP), weight[:, :, 0], ALU.is_lt, ALU.mult))

        def scratch(st, b_in):
            b2, y, n = (st.sb(name, [P, D]) for name in ("b2", "y", "n"))
            tools = Tools(4, ((b2[:], spread(A["L3_ffn_b2"])),))
            tools.b2, tools.y, tools.n = b2, y, n
            return tools

        def finish(v, q, tools, t, result):
            x = g.x[:, bass.ds(t, 1), :].rearrange("p t d -> p (t d)")
            q.mark(v.tensor_tensor(tools.y[:], result, tools.b2[:], ALU.add))
            q.then(v.tensor_scalar(tools.n[:], x, g.mean[:, bass.ds(t, 1)], g.rstd[:, bass.ds(t, 1)], ALU.subtract, ALU.mult))
            q.then(v.scalar_tensor_tensor(tools.y[:], tools.y[:], coef[:, bass.ds(t, 1)], tools.n[:], ALU.mult, ALU.add))
            q.then(v.tensor_tensor(x, x, tools.y[:], ALU.add))

        ffn(nc, g, "top_ffn", x_t, w1s, b1s, w2s, FB, ACT.Gelu_apprx_tanh, finish, scratch)



def build(nc, A, out, layers):
    with ExitStack() as ctx:
        g = Core()
        g.first_sem = min(nc.free_semaphores)
        g.gather_sems = [ctx.enter_context(nc.semaphore(f"gathered{i}", max(nc.free_semaphores))) for i in range(32)]
        g.gathered = [0] * 32

        def sb(name, shape, dt=F32):
            return ctx.enter_context(nc.sbuf_tensor(name, shape, dt))

        g.x = sb("x", [P, T, D])
        g.ident = sb("ident", [128, 128])
        g.iota = sb("iota", [128, 128])
        g.ones = sb("ones", [128, 1])
        g.src_e = sb("src_e", [P, C], U32)
        g.dst_e = sb("dst_e", [P, C], U32)
        g.src_s = sb("src_s", [P, S], U32)
        g.place_s = sb("place_s", [P, S])
        g.chunk_of = sb("chunk_of", [1, S], I32)
        g.tile_of = sb("tile_of", [1, S], I32)
        g.border = sb("border", [128, RUN + 1])
        g.has_border = sb("has_border", [128, 1])
        g.has_border_back = sb("has_border_back", [128, 1])
        g.first_row = sb("first_row", [P, T], U32)
        g.first_rows = nc.dram_tensor("first_rows", (E + N, H), F32, kind="Internal").ap()
        g.mean = sb("mean", [P, T])
        g.rstd = sb("rstd", [P, T])

        prepare(nc, g, A)
        for layer in layers:
            layer(nc, g, A)
        with Stage(nc, g, "store") as st:
            stored = st.sem("stored")
            with st.block() as block:
                @block.sync
                def _(sp):
                    for t in range(T):
                        sp.dma_start(out[t * P:(t + 1) * P, :], g.x[:, t, :]).then_inc(stored, 16)
                    sp.wait_ge(stored, 16 * T)


LAYERS = (gat, moe_one, edge_gat, moe_all, gin, moe_two, gat_loops, ffn_top)


def laid_out(inputs):
    a = {n: np.ascontiguousarray(v) for n, v in inputs.items() if n != "L3_ffn_attention_mask"}

    def cols(v):
        return np.swapaxes(v.reshape(v.shape[0], -1, 128), 1, 2)

    def take(names):
        return [cols(a.pop(n)) for n in names]

    a["src_by_place"] = np.ascontiguousarray(a["src"].reshape(C, P).T)
    a["dst_by_place"] = np.ascontiguousarray(a["dst"].reshape(C, P).T)
    rows = [np.concatenate(take([f"L2_gnn_{m}1{n}", f"L2_gnn_{m}2{n}"]), 2) for m, n in (("b", ""), ("bn", "_gamma"), ("bn", "_beta"))]
    a["L2_gnn_cols"] = np.ascontiguousarray(np.stack(rows, 2))
    for n in ("W1", "W2", "W3", "W4", "W5"):
        a[f"L1_gnn_{n}_t"] = np.ascontiguousarray(a[f"L1_gnn_{n}"].T)
    a["L1_gnn_b1_col"] = np.ascontiguousarray(a["L1_gnn_b1"].reshape(KD, 128).T)
    a["L0_ffn_router_w_t"] = np.ascontiguousarray(a["L0_ffn_router_w"].T)
    for n in ("L0_ffn_b1", "L2_ffn_b1", "L3_ffn_b1"):
        a[n + "_col"] = np.ascontiguousarray(a[n].reshape(-1, 128).T)
    a["L3_ffn_wr_col"] = np.ascontiguousarray(a["L3_ffn_wr"].reshape(KD, 128, 1).swapaxes(0, 1))
    a["L1_ffn_b1_col"] = np.ascontiguousarray(cols(a["L1_ffn_b1"]))
    a["sel_one"] = np.ascontiguousarray(np.repeat(np.eye(32, dtype=np.float32), 64, 1).reshape(32, 16, 128))
    a["sel_two"] = np.ascontiguousarray(np.repeat(np.eye(8, dtype=np.float32), 128, 1).reshape(8, 8, 128))
    a["ident"] = np.eye(128, dtype=np.float32)
    return a


def kernel(**inputs):
    import concourse.bacc as bacc
    from concourse.bass_utils import run_bass_kernel_spmd

    nc = bacc.Bacc("TRN2", target_bir_lowering=False, num_devices=1)
    arrays = laid_out({n: np.asarray(v) for n, v in inputs.items()})
    A = {n: nc.dram_tensor(n + "_in", v.shape, mybir.dt.from_np(v.dtype), kind="ExternalInput").ap()
         for n, v in arrays.items()}
    out = nc.dram_tensor("out", (N, D), F32, kind="ExternalOutput").ap()
    build(nc, A, out, LAYERS)
    r = run_bass_kernel_spmd(nc, [{n + "_in": v for n, v in arrays.items()}], core_ids=[0])
    return r.results[0]["out"]
```
